# Optimizing a Trainium2 kernel written in Bass

```python
import numpy as np
import jax
import jax.numpy as jnp

def _softmax(x, axis=-1):
    return jax.nn.softmax(x, axis=axis)

def _gelu(x):
    return jax.nn.gelu(x, approximate=True)

def _silu(x):
    return jax.nn.silu(x)

def _sigmoid(x):
    return jax.nn.sigmoid(x)

def _layernorm(x, axis=-1, eps=1e-05):
    m = jnp.mean(x, axis=axis, keepdims=True)
    v = jnp.var(x, axis=axis, keepdims=True)
    return (x - m) / jnp.sqrt(v + eps)

def _scatter_add(tgt, idx, src, axis=0):
    return tgt.at[idx].add(src)

def _segment_sum(src, seg, n):
    return jax.ops.segment_sum(src, seg, n)
kernel_name = 'mk_pixart_seq_d4_seqx_r8_2be6e0'

def setup_inputs(seed: int=0):
    np.random.seed(seed)
    _w = jnp.asarray

    def _rec_inputs():
        import jax
        import jax.numpy as jnp
        _rk = jax.random.key(seed)
        x = -0.0003929 + 0.9999 * jax.random.normal(jax.random.fold_in(_rk, 1), (8, 56, 128), jnp.float32)
        _lenS = 56 - jax.random.randint(jax.random.fold_in(_rk, 7), (8,), 0, max(1, 56 // 4) + 1, jnp.int32)
        _lenS2 = 1500 - jax.random.randint(jax.random.fold_in(_rk, 8), (8,), 0, max(1, 1500 // 4) + 1, jnp.int32)
        _ctx_1024P = jax.random.normal(jax.random.fold_in(_rk, 11), (8, 16, 128), jnp.float32)
        _ctx_1024c = jax.random.dirichlet(jax.random.fold_in(_rk, 511), 0.3 * jnp.ones((16,), jnp.float32), (8, 1500))
        _ctx_1024t = jnp.einsum('bsk,bkd->bsd', _ctx_1024c, _ctx_1024P)
        _ctx_1024t = _ctx_1024t * jax.lax.rsqrt(jnp.mean(jnp.square(_ctx_1024t)) + 1e-12) * 0.953939
        ctx_1024 = -1.39393e-06 + 0.999914 * (_ctx_1024t + 0.3 * jax.random.normal(jax.random.fold_in(_rk, 611), (8, 1500, 128), jnp.float32))
        cond_1024 = -0.00920427 + 1.00102 * jax.random.normal(jax.random.fold_in(_rk, 12), (8, 128), jnp.float32)
        return (x, ctx_1024, cond_1024)
    x, ctx_1024, cond_1024 = _rec_inputs()

    def _L0_xcond_setup():
        import jax, jax.numpy as jnp
        import numpy as np
        EPS = 1e-05

        def _ada_ln(x, c, W_ss, b_ss):
            mu = jnp.mean(x, axis=-1, keepdims=True)
            var = jnp.mean((x - mu) ** 2, axis=-1, keepdims=True)
            h = (x - mu) / jnp.sqrt(var + EPS)
            ss = jax.nn.silu(c) @ W_ss + b_ss
            scale, bias = jnp.split(ss, 2, axis=-1)
            return (1.0 + scale)[:, None, :] * h + bias[:, None, :]
        key = jax.random.key(seed)
        ks = jax.random.split(key, 12)
        B, Lq, Lkv, H = (8, 256, 64, 128)
        s = 0.02
        return {'x_q': jax.random.normal(ks[0], (B, Lq, H), jnp.float32), 'x_kv': jax.random.normal(ks[1], (B, Lkv, H), jnp.float32), 't_vec': jax.random.normal(ks[2], (B, H), jnp.float32), 'Wq': jax.random.normal(ks[3], (H, H), jnp.float32) * s, 'bq': jnp.zeros((H,), jnp.float32), 'Wkv': jax.random.normal(ks[4], (H, 2 * H), jnp.float32) * s, 'bkv': jnp.zeros((2 * H,), jnp.float32), 'Wp': jax.random.normal(ks[5], (H, H), jnp.float32) * s, 'bp': jnp.zeros((H,), jnp.float32), 'Wss_q': jax.random.normal(ks[6], (H, 2 * H), jnp.float32) * s, 'bss_q': jnp.zeros((2 * H,), jnp.float32), 'Wss_kv': jax.random.normal(ks[7], (H, 2 * H), jnp.float32) * s, 'bss_kv': jnp.zeros((2 * H,), jnp.float32)}
    _L0_xcond_all = _L0_xcond_setup()
    _L0_xcond_in = {k: v for k, v in _L0_xcond_all.items() if k in ('Wq', 'bq', 'Wkv', 'bkv', 'Wp', 'bp', 'Wss_q', 'bss_q', 'Wss_kv', 'bss_kv')}
    del _L0_xcond_all

    def _L1_xcond_setup():
        import jax, jax.numpy as jnp
        import numpy as np
        H = 128
        RH = 2 * H
        E = 3
        B, T, P = (8, 256, 64)
        LN_EPS = 1e-05

        def _layer_norm(x, gamma, beta):
            mu = jnp.mean(x, axis=-1, keepdims=True)
            var = jnp.mean(jnp.square(x - mu), axis=-1, keepdims=True)
            return (x - mu) * jax.lax.rsqrt(var + LN_EPS) * gamma + beta
        key = jax.random.key(seed)
        ks = jax.random.split(key, 24)
        s = lambda fan_in: 1.0 / np.sqrt(fan_in)
        inp = {'mix_hidden_states': jax.random.normal(ks[0], (B, T, H), jnp.float32), 'global_anchor': jax.random.normal(ks[1], (B, H), jnp.float32), 'prototype_bank': jax.random.normal(ks[2], (B, P, H), jnp.float32), 'ln_gamma': jnp.ones((H,), jnp.float32), 'ln_beta': jnp.zeros((H,), jnp.float32), 'Wq': jax.random.normal(ks[3], (H, H), jnp.float32) * s(H), 'Wk': jax.random.normal(ks[4], (H, H), jnp.float32) * s(H), 'Wv': jax.random.normal(ks[5], (H, H), jnp.float32) * s(H), 'router_W': jax.random.normal(ks[6], (3 * H, E), jnp.float32) * s(3 * H), 'router_b': jnp.zeros((E,), jnp.float32), 'e_w1': jax.random.normal(ks[7], (E, 3 * H, RH), jnp.float32) * s(3 * H), 'e_b1': jnp.zeros((E, RH), jnp.float32), 'e_w2': jax.random.normal(ks[8], (E, RH, H), jnp.float32) * s(RH), 'e_b2': jnp.zeros((E, H), jnp.float32), 'gate_w1': jax.random.normal(ks[9], (3 * H, H), jnp.float32) * s(3 * H), 'gate_b1': jnp.zeros((H,), jnp.float32), 'gate_w2': jax.random.normal(ks[10], (H, H), jnp.float32) * s(H), 'gate_b2': jnp.zeros((H,), jnp.float32), 'out_w': jax.random.normal(ks[11], (H, H), jnp.float32) * s(H), 'out_b': jnp.zeros((H,), jnp.float32)}
        return inp
    _L1_xcond_all = _L1_xcond_setup()
    _L1_xcond_in = {k: v for k, v in _L1_xcond_all.items() if k in ('ln_gamma', 'ln_beta', 'Wq', 'Wk', 'Wv', 'router_W', 'router_b', 'e_w1', 'e_b1', 'e_w2', 'e_b2', 'gate_w1', 'gate_b1', 'gate_w2', 'gate_b2', 'out_w', 'out_b')}
    del _L1_xcond_all

    def _L2_xcond_setup():
        import jax, jax.numpy as jnp
        import numpy as np
        LN_EPS = 1e-06

        def _ln(x):
            mu = jnp.mean(x, axis=-1, keepdims=True)
            var = jnp.var(x, axis=-1, keepdims=True)
            return (x - mu) * jax.lax.rsqrt(var + LN_EPS)
        key = jax.random.key(seed)
        H, NH = (128, 16)
        B, N, S = (4, 128, 77)
        MLP = int(H * 4.0)
        ks = jax.random.split(key, 20)
        s = 1.0 / np.sqrt(H)
        return {'x': jax.random.normal(ks[0], (B, N, H), jnp.float32), 'c': jax.random.normal(ks[1], (B, H), jnp.float32), 'context': jax.random.normal(ks[2], (B, S, H), jnp.float32), 'W_mod': jax.random.normal(ks[3], (H, 6 * H), jnp.float32) * s, 'b_mod': jnp.zeros((6 * H,), jnp.float32), 'W_qkv': jax.random.normal(ks[4], (H, 3 * H), jnp.float32) * s, 'b_qkv': jnp.zeros((3 * H,), jnp.float32), 'W_proj': jax.random.normal(ks[5], (H, H), jnp.float32) * s, 'b_proj': jnp.zeros((H,), jnp.float32), 'W_qc': jax.random.normal(ks[6], (H, H), jnp.float32) * s, 'b_qc': jnp.zeros((H,), jnp.float32), 'W_kvc': jax.random.normal(ks[7], (H, 2 * H), jnp.float32) * s, 'b_kvc': jnp.zeros((2 * H,), jnp.float32), 'W_cproj': jax.random.normal(ks[8], (H, H), jnp.float32) * s, 'b_cproj': jnp.zeros((H,), jnp.float32), 'W_mlp1': jax.random.normal(ks[9], (H, MLP), jnp.float32) * s, 'b_mlp1': jnp.zeros((MLP,), jnp.float32), 'W_mlp2': jax.random.normal(ks[10], (MLP, H), jnp.float32) * (1.0 / np.sqrt(MLP)), 'b_mlp2': jnp.zeros((H,), jnp.float32)}
    _L2_xcond_all = _L2_xcond_setup()
    _L2_xcond_in = {k: v for k, v in _L2_xcond_all.items() if k in ('W_mod', 'b_mod', 'W_qkv', 'b_qkv', 'W_proj', 'b_proj', 'W_qc', 'b_qc', 'W_kvc', 'b_kvc', 'W_cproj', 'b_cproj', 'W_mlp1', 'b_mlp1', 'W_mlp2', 'b_mlp2')}
    del _L2_xcond_all

    def _L3_xcond_setup():
        import jax, jax.numpy as jnp
        import numpy as np
        D = 128
        H = 16
        HD = D // H
        MLP = 4 * D
        EPS = 1e-06
        SCALE = HD ** (-0.5)

        def _p(key, shape, s=0.02):
            return jax.random.normal(key, shape, dtype=jnp.float32) * s

        def _ln(x):
            mu = jnp.mean(x, axis=-1, keepdims=True)
            var = jnp.var(x, axis=-1, keepdims=True)
            return (x - mu) * jax.lax.rsqrt(var + EPS)

        def _heads(t):
            B, L, _ = t.shape
            return t.reshape(B, L, H, HD).transpose(0, 2, 1, 3)

        def _attend(q, k, v):
            attn = jnp.einsum('bhnd,bhsd->bhns', q, k) * SCALE
            attn = jax.nn.softmax(attn, axis=-1)
            o = jnp.einsum('bhns,bhsd->bhnd', attn, v)
            B, _, N, _ = q.shape
            return o.transpose(0, 2, 1, 3).reshape(B, N, D)
        key = jax.random.key(seed)
        ks = jax.random.split(key, 24)
        B, N, S = (4, 128, 77)
        return {'x': jax.random.normal(ks[0], (B, N, D), dtype=jnp.float32), 't_emb': jax.random.normal(ks[1], (B, D), dtype=jnp.float32), 'context': jax.random.normal(ks[2], (B, S, D), dtype=jnp.float32), 'adaln_w': _p(ks[3], (D, 6 * D)), 'adaln_b': _p(ks[4], (6 * D,)), 'qkv_w': _p(ks[5], (D, 3 * D)), 'qkv_b': _p(ks[6], (3 * D,)), 'sa_proj_w': _p(ks[7], (D, D)), 'sa_proj_b': _p(ks[8], (D,)), 'q_w': _p(ks[9], (D, D)), 'q_b': _p(ks[10], (D,)), 'kv_w': _p(ks[11], (D, 2 * D)), 'kv_b': _p(ks[12], (2 * D,)), 'ca_proj_w': _p(ks[13], (D, D)), 'ca_proj_b': _p(ks[14], (D,)), 'fc1_w': _p(ks[15], (D, MLP)), 'fc1_b': _p(ks[16], (MLP,)), 'fc2_w': _p(ks[17], (MLP, D)), 'fc2_b': _p(ks[18], (D,))}
    _L3_xcond_all = _L3_xcond_setup()
    _L3_xcond_in = {k: v for k, v in _L3_xcond_all.items() if k in ('adaln_w', 'adaln_b', 'qkv_w', 'qkv_b', 'sa_proj_w', 'sa_proj_b', 'q_w', 'q_b', 'kv_w', 'kv_b', 'ca_proj_w', 'ca_proj_b', 'fc1_w', 'fc1_b', 'fc2_w', 'fc2_b')}
    del _L3_xcond_all
    return {'x': x, 'ctx_1024': ctx_1024, 'cond_1024': cond_1024, 'L0_xcond_Wq': _L0_xcond_in['Wq'], 'L0_xcond_bq': _L0_xcond_in['bq'], 'L0_xcond_Wkv': _L0_xcond_in['Wkv'], 'L0_xcond_bkv': _L0_xcond_in['bkv'], 'L0_xcond_Wp': _L0_xcond_in['Wp'], 'L0_xcond_bp': _L0_xcond_in['bp'], 'L0_xcond_Wss_q': _L0_xcond_in['Wss_q'], 'L0_xcond_bss_q': _L0_xcond_in['bss_q'], 'L0_xcond_Wss_kv': _L0_xcond_in['Wss_kv'], 'L0_xcond_bss_kv': _L0_xcond_in['bss_kv'], 'L1_xcond_ln_gamma': _L1_xcond_in['ln_gamma'], 'L1_xcond_ln_beta': _L1_xcond_in['ln_beta'], 'L1_xcond_Wq': _L1_xcond_in['Wq'], 'L1_xcond_Wk': _L1_xcond_in['Wk'], 'L1_xcond_Wv': _L1_xcond_in['Wv'], 'L1_xcond_router_W': _L1_xcond_in['router_W'], 'L1_xcond_router_b': _L1_xcond_in['router_b'], 'L1_xcond_e_w1': _L1_xcond_in['e_w1'], 'L1_xcond_e_b1': _L1_xcond_in['e_b1'], 'L1_xcond_e_w2': _L1_xcond_in['e_w2'], 'L1_xcond_e_b2': _L1_xcond_in['e_b2'], 'L1_xcond_gate_w1': _L1_xcond_in['gate_w1'], 'L1_xcond_gate_b1': _L1_xcond_in['gate_b1'], 'L1_xcond_gate_w2': _L1_xcond_in['gate_w2'], 'L1_xcond_gate_b2': _L1_xcond_in['gate_b2'], 'L1_xcond_out_w': _L1_xcond_in['out_w'], 'L1_xcond_out_b': _L1_xcond_in['out_b'], 'L2_xcond_W_mod': _L2_xcond_in['W_mod'], 'L2_xcond_b_mod': _L2_xcond_in['b_mod'], 'L2_xcond_W_qkv': _L2_xcond_in['W_qkv'], 'L2_xcond_b_qkv': _L2_xcond_in['b_qkv'], 'L2_xcond_W_proj': _L2_xcond_in['W_proj'], 'L2_xcond_b_proj': _L2_xcond_in['b_proj'], 'L2_xcond_W_qc': _L2_xcond_in['W_qc'], 'L2_xcond_b_qc': _L2_xcond_in['b_qc'], 'L2_xcond_W_kvc': _L2_xcond_in['W_kvc'], 'L2_xcond_b_kvc': _L2_xcond_in['b_kvc'], 'L2_xcond_W_cproj': _L2_xcond_in['W_cproj'], 'L2_xcond_b_cproj': _L2_xcond_in['b_cproj'], 'L2_xcond_W_mlp1': _L2_xcond_in['W_mlp1'], 'L2_xcond_b_mlp1': _L2_xcond_in['b_mlp1'], 'L2_xcond_W_mlp2': _L2_xcond_in['W_mlp2'], 'L2_xcond_b_mlp2': _L2_xcond_in['b_mlp2'], 'L3_xcond_adaln_w': _L3_xcond_in['adaln_w'], 'L3_xcond_adaln_b': _L3_xcond_in['adaln_b'], 'L3_xcond_qkv_w': _L3_xcond_in['qkv_w'], 'L3_xcond_qkv_b': _L3_xcond_in['qkv_b'], 'L3_xcond_sa_proj_w': _L3_xcond_in['sa_proj_w'], 'L3_xcond_sa_proj_b': _L3_xcond_in['sa_proj_b'], 'L3_xcond_q_w': _L3_xcond_in['q_w'], 'L3_xcond_q_b': _L3_xcond_in['q_b'], 'L3_xcond_kv_w': _L3_xcond_in['kv_w'], 'L3_xcond_kv_b': _L3_xcond_in['kv_b'], 'L3_xcond_ca_proj_w': _L3_xcond_in['ca_proj_w'], 'L3_xcond_ca_proj_b': _L3_xcond_in['ca_proj_b'], 'L3_xcond_fc1_w': _L3_xcond_in['fc1_w'], 'L3_xcond_fc1_b': _L3_xcond_in['fc1_b'], 'L3_xcond_fc2_w': _L3_xcond_in['fc2_w'], 'L3_xcond_fc2_b': _L3_xcond_in['fc2_b']}

def reference(x, ctx_1024, cond_1024, L0_xcond_Wq, L0_xcond_bq, L0_xcond_Wkv, L0_xcond_bkv, L0_xcond_Wp, L0_xcond_bp, L0_xcond_Wss_q, L0_xcond_bss_q, L0_xcond_Wss_kv, L0_xcond_bss_kv, L1_xcond_ln_gamma, L1_xcond_ln_beta, L1_xcond_Wq, L1_xcond_Wk, L1_xcond_Wv, L1_xcond_router_W, L1_xcond_router_b, L1_xcond_e_w1, L1_xcond_e_b1, L1_xcond_e_w2, L1_xcond_e_b2, L1_xcond_gate_w1, L1_xcond_gate_b1, L1_xcond_gate_w2, L1_xcond_gate_b2, L1_xcond_out_w, L1_xcond_out_b, L2_xcond_W_mod, L2_xcond_b_mod, L2_xcond_W_qkv, L2_xcond_b_qkv, L2_xcond_W_proj, L2_xcond_b_proj, L2_xcond_W_qc, L2_xcond_b_qc, L2_xcond_W_kvc, L2_xcond_b_kvc, L2_xcond_W_cproj, L2_xcond_b_cproj, L2_xcond_W_mlp1, L2_xcond_b_mlp1, L2_xcond_W_mlp2, L2_xcond_b_mlp2, L3_xcond_adaln_w, L3_xcond_adaln_b, L3_xcond_qkv_w, L3_xcond_qkv_b, L3_xcond_sa_proj_w, L3_xcond_sa_proj_b, L3_xcond_q_w, L3_xcond_q_b, L3_xcond_kv_w, L3_xcond_kv_b, L3_xcond_ca_proj_w, L3_xcond_ca_proj_b, L3_xcond_fc1_w, L3_xcond_fc1_b, L3_xcond_fc2_w, L3_xcond_fc2_b):
    import jax
    import jax.numpy as jnp

    def _L0_xcond_ref(x_q, x_kv, t_vec, Wq, bq, Wkv, bkv, Wp, bp, Wss_q, bss_q, Wss_kv, bss_kv):
        import jax, jax.numpy as jnp
        import numpy as np
        EPS = 1e-05

        def _ada_ln(x, c, W_ss, b_ss):
            mu = jnp.mean(x, axis=-1, keepdims=True)
            var = jnp.mean((x - mu) ** 2, axis=-1, keepdims=True)
            h = (x - mu) / jnp.sqrt(var + EPS)
            ss = jax.nn.silu(c) @ W_ss + b_ss
            scale, bias = jnp.split(ss, 2, axis=-1)
            return (1.0 + scale)[:, None, :] * h + bias[:, None, :]
        B, Lq, H = x_q.shape
        Lkv = x_kv.shape[1]
        nh = 16
        dh = H // nh
        xq = _ada_ln(x_q, t_vec, Wss_q, bss_q)
        xkv = _ada_ln(x_kv, t_vec, Wss_kv, bss_kv)
        q = (xq @ Wq + bq).reshape(B, Lq, nh, dh)
        kv = (xkv @ Wkv + bkv).reshape(B, Lkv, 2, nh, dh)
        k = kv[:, :, 0]
        v = kv[:, :, 1]
        scores = jnp.einsum('bqhd,bkhd->bhqk', q, k) / jnp.sqrt(jnp.float32(dh))
        attn = jax.nn.softmax(scores, axis=-1)
        out = jnp.einsum('bhqk,bkhd->bqhd', attn, v).reshape(B, Lq, H)
        return x_q + (out @ Wp + bp)

    def _L1_xcond_ref(mix_hidden_states, global_anchor, prototype_bank, ln_gamma, ln_beta, Wq, Wk, Wv, router_W, router_b, e_w1, e_b1, e_w2, e_b2, gate_w1, gate_b1, gate_w2, gate_b2, out_w, out_b):
        import jax, jax.numpy as jnp
        import numpy as np
        H = 128
        RH = 2 * H
        E = 3
        B, T, P = (8, 256, 64)
        LN_EPS = 1e-05

        def _layer_norm(x, gamma, beta):
            mu = jnp.mean(x, axis=-1, keepdims=True)
            var = jnp.mean(jnp.square(x - mu), axis=-1, keepdims=True)
            return (x - mu) * jax.lax.rsqrt(var + LN_EPS) * gamma + beta
        x = mix_hidden_states
        nx = _layer_norm(x, ln_gamma, ln_beta)
        q = nx @ Wq
        k = prototype_bank @ Wk
        v = prototype_bank @ Wv
        scores = jnp.einsum('bth,bph->btp', q, k) * H ** (-0.5)
        weights = jax.nn.softmax(scores, axis=-1)
        evidence = jnp.einsum('btp,bph->bth', weights, v)
        anchor = jnp.broadcast_to(global_anchor[:, None, :], nx.shape)
        combined = jnp.concatenate([nx, evidence, anchor], axis=-1)
        router_logits = combined @ router_W + router_b
        router_probs = jax.nn.softmax(router_logits, axis=-1)
        h = jax.nn.silu(jnp.einsum('btc,ecr->bter', combined, e_w1) + e_b1)
        expert_out = jnp.einsum('bter,erh->bteh', h, e_w2) + e_b2
        routed = jnp.sum(expert_out * router_probs[..., None], axis=-2)
        g = jax.nn.sigmoid(jax.nn.silu(combined @ gate_w1 + gate_b1) @ gate_w2 + gate_b2)
        refined_delta = g * (routed @ out_w + out_b)
        return x + refined_delta

    def _L2_xcond_ref(x, c, context, W_mod, b_mod, W_qkv, b_qkv, W_proj, b_proj, W_qc, b_qc, W_kvc, b_kvc, W_cproj, b_cproj, W_mlp1, b_mlp1, W_mlp2, b_mlp2):
        import jax, jax.numpy as jnp
        import numpy as np
        LN_EPS = 1e-06

        def _ln(x):
            mu = jnp.mean(x, axis=-1, keepdims=True)
            var = jnp.var(x, axis=-1, keepdims=True)
            return (x - mu) * jax.lax.rsqrt(var + LN_EPS)
        B, N, H = x.shape
        NH = 16
        hd = H // NH
        scale = hd ** (-0.5)
        c_proj = jax.nn.silu(c) @ W_mod + b_mod
        shift_a, scale_a, gate_a, shift_m, scale_m, gate_m = jnp.split(c_proj, 6, axis=-1)

        def modulate(t, shift, sc):
            return t * (1 + sc[:, None]) + shift[:, None]
        x_norm = modulate(_ln(x), shift_a, scale_a)
        qkv = x_norm @ W_qkv + b_qkv
        q, k, v = jnp.split(qkv, 3, axis=-1)
        q = q.reshape(B, N, NH, hd).transpose(0, 2, 1, 3)
        k = k.reshape(B, N, NH, hd).transpose(0, 2, 1, 3)
        v = v.reshape(B, N, NH, hd).transpose(0, 2, 1, 3)
        attn_w = jax.nn.softmax(jnp.einsum('bhqd,bhkd->bhqk', q, k) * scale, axis=-1)
        attn_out = jnp.einsum('bhqk,bhkd->bhqd', attn_w, v)
        attn_out = attn_out.transpose(0, 2, 1, 3).reshape(B, N, H)
        attn_out = attn_out @ W_proj + b_proj
        x = x + gate_a[:, None] * attn_out
        S = context.shape[1]
        q_c = _ln(x) @ W_qc + b_qc
        kv_c = _ln(context) @ W_kvc + b_kvc
        k_c, v_c = jnp.split(kv_c, 2, axis=-1)
        q_c = q_c.reshape(B, N, NH, hd).transpose(0, 2, 1, 3)
        k_c = k_c.reshape(B, S, NH, hd).transpose(0, 2, 1, 3)
        v_c = v_c.reshape(B, S, NH, hd).transpose(0, 2, 1, 3)
        c_attn_w = jax.nn.softmax(jnp.einsum('bhqd,bhsd->bhqs', q_c, k_c) * scale, axis=-1)
        c_attn_out = jnp.einsum('bhqs,bhsd->bhqd', c_attn_w, v_c)
        c_attn_out = c_attn_out.transpose(0, 2, 1, 3).reshape(B, N, H)
        c_attn_out = c_attn_out @ W_cproj + b_cproj
        x = x + c_attn_out
        x_norm2 = modulate(_ln(x), shift_m, scale_m)
        h = jax.nn.gelu(x_norm2 @ W_mlp1 + b_mlp1)
        h = h @ W_mlp2 + b_mlp2
        x = x + gate_m[:, None] * h
        return x

    def _L3_xcond_ref(x, t_emb, context, adaln_w, adaln_b, qkv_w, qkv_b, sa_proj_w, sa_proj_b, q_w, q_b, kv_w, kv_b, ca_proj_w, ca_proj_b, fc1_w, fc1_b, fc2_w, fc2_b):
        import jax, jax.numpy as jnp
        import numpy as np
        D = 128
        H = 16
        HD = D // H
        MLP = 4 * D
        EPS = 1e-06
        SCALE = HD ** (-0.5)

        def _p(key, shape, s=0.02):
            return jax.random.normal(key, shape, dtype=jnp.float32) * s

        def _ln(x):
            mu = jnp.mean(x, axis=-1, keepdims=True)
            var = jnp.var(x, axis=-1, keepdims=True)
            return (x - mu) * jax.lax.rsqrt(var + EPS)

        def _heads(t):
            B, L, _ = t.shape
            return t.reshape(B, L, H, HD).transpose(0, 2, 1, 3)

        def _attend(q, k, v):
            attn = jnp.einsum('bhnd,bhsd->bhns', q, k) * SCALE
            attn = jax.nn.softmax(attn, axis=-1)
            o = jnp.einsum('bhns,bhsd->bhnd', attn, v)
            B, _, N, _ = q.shape
            return o.transpose(0, 2, 1, 3).reshape(B, N, D)
        B, N, _ = x.shape
        S = context.shape[1]
        mod = jax.nn.silu(t_emb) @ adaln_w + adaln_b
        sh_sa, sc_sa, g_sa, sh_ff, sc_ff, g_ff = jnp.split(mod[:, None, :], 6, axis=-1)
        xm = _ln(x) * (1.0 + sc_sa) + sh_sa
        qkv = (xm @ qkv_w + qkv_b).reshape(B, N, 3, H, HD)
        q = qkv[:, :, 0].transpose(0, 2, 1, 3)
        k = qkv[:, :, 1].transpose(0, 2, 1, 3)
        v = qkv[:, :, 2].transpose(0, 2, 1, 3)
        x_sa = _attend(q, k, v) @ sa_proj_w + sa_proj_b
        x = x + g_sa * x_sa
        xn = _ln(x)
        q = _heads(xn @ q_w + q_b)
        kv = (context @ kv_w + kv_b).reshape(B, S, 2, H, HD)
        k = kv[:, :, 0].transpose(0, 2, 1, 3)
        v = kv[:, :, 1].transpose(0, 2, 1, 3)
        x_ca = _attend(q, k, v) @ ca_proj_w + ca_proj_b
        x = x + x_ca
        xm = _ln(x) * (1.0 + sc_ff) + sh_ff
        h = jax.nn.gelu(xm @ fc1_w + fc1_b, approximate=True)
        x_ff = h @ fc2_w + fc2_b
        x = x + g_ff * x_ff
        return x
    x = _L0_xcond_ref(x, ctx_1024, cond_1024, L0_xcond_Wq, L0_xcond_bq, L0_xcond_Wkv, L0_xcond_bkv, L0_xcond_Wp, L0_xcond_bp, L0_xcond_Wss_q, L0_xcond_bss_q, L0_xcond_Wss_kv, L0_xcond_bss_kv)
    x = _L1_xcond_ref(x, cond_1024, ctx_1024, L1_xcond_ln_gamma, L1_xcond_ln_beta, L1_xcond_Wq, L1_xcond_Wk, L1_xcond_Wv, L1_xcond_router_W, L1_xcond_router_b, L1_xcond_e_w1, L1_xcond_e_b1, L1_xcond_e_w2, L1_xcond_e_b2, L1_xcond_gate_w1, L1_xcond_gate_b1, L1_xcond_gate_w2, L1_xcond_gate_b2, L1_xcond_out_w, L1_xcond_out_b)
    x = _L2_xcond_ref(x, cond_1024, ctx_1024, L2_xcond_W_mod, L2_xcond_b_mod, L2_xcond_W_qkv, L2_xcond_b_qkv, L2_xcond_W_proj, L2_xcond_b_proj, L2_xcond_W_qc, L2_xcond_b_qc, L2_xcond_W_kvc, L2_xcond_b_kvc, L2_xcond_W_cproj, L2_xcond_b_cproj, L2_xcond_W_mlp1, L2_xcond_b_mlp1, L2_xcond_W_mlp2, L2_xcond_b_mlp2)
    x = _L3_xcond_ref(x, cond_1024, ctx_1024, L3_xcond_adaln_w, L3_xcond_adaln_b, L3_xcond_qkv_w, L3_xcond_qkv_b, L3_xcond_sa_proj_w, L3_xcond_sa_proj_b, L3_xcond_q_w, L3_xcond_q_b, L3_xcond_kv_w, L3_xcond_kv_b, L3_xcond_ca_proj_w, L3_xcond_ca_proj_b, L3_xcond_fc1_w, L3_xcond_fc1_b, L3_xcond_fc2_w, L3_xcond_fc2_b)
    return x

_drawn_inputs = setup_inputs


def setup_inputs(seed=0):
    import zlib

    import numpy as np

    out = dict(_drawn_inputs(seed))
    spreads = {'L0_xcond_bq': (0.0, 2.0),
     'L0_xcond_bkv': (0.0, 0.353),
     'L0_xcond_bp': (0.0, 0.1),
     'L0_xcond_bss_q': (0.0, 2.0),
     'L0_xcond_bss_kv': (0.0, 0.8),
     'L1_xcond_ln_gamma': (1.0, 0.6),
     'L1_xcond_ln_beta': (0.0, 0.61),
     'L1_xcond_router_b': (0.0, 0.541),
     'L1_xcond_e_b1': (0.0, 0.397),
     'L1_xcond_e_b2': (0.0, 0.1),
     'L1_xcond_gate_b1': (0.0, 0.8),
     'L1_xcond_gate_b2': (0.0, 0.8),
     'L1_xcond_out_b': (0.0, 0.1),
     'L2_xcond_b_mod': (0.0, 0.1),
     'L2_xcond_b_qkv': (0.0, 0.1),
     'L2_xcond_b_proj': (0.0, 0.1),
     'L2_xcond_b_qc': (0.0, 0.627),
     'L2_xcond_b_kvc': (0.0, 0.1),
     'L2_xcond_b_cproj': (0.0, 0.1),
     'L2_xcond_b_mlp1': (0.0, 0.1),
     'L2_xcond_b_mlp2': (0.0, 0.1)}
    factors = {'L0_xcond_Wq': 8.0,
     'L0_xcond_Wss_q': 22.511,
     'L0_xcond_Wss_kv': 6.915,
     'L3_xcond_adaln_w': 8.0,
     'L3_xcond_adaln_b': 8.0,
     'L3_xcond_qkv_w': 8.0,
     'L3_xcond_qkv_b': 8.0,
     'L3_xcond_sa_proj_w': 8.0,
     'L3_xcond_sa_proj_b': 8.0,
     'L3_xcond_q_w': 26.501,
     'L3_xcond_q_b': 192.731,
     'L3_xcond_kv_w': 3.023,
     'L3_xcond_kv_b': 34.947,
     'L3_xcond_ca_proj_w': 2.97,
     'L3_xcond_ca_proj_b': 21.139,
     'L3_xcond_fc1_w': 8.0,
     'L3_xcond_fc1_b': 8.0,
     'L3_xcond_fc2_w': 8.0,
     'L3_xcond_fc2_b': 34.293}
    for name, (base, spread) in spreads.items():
        noise = np.random.default_rng([zlib.crc32(name.encode()), seed]).standard_normal(out[name].shape)
        drawn = base * np.exp(spread * noise) if base else spread * noise
        out[name] = jnp.asarray(drawn.astype(out[name].dtype))
    for name, factor in factors.items():
        out[name] = (out[name] * factor).astype(out[name].dtype)
    return out
```

```python
from contextlib import ExitStack

import concourse.bass as bass
import numpy as np
from concourse import mybir

F32 = mybir.dt.float32
F32R = mybir.dt.float32r
BF16 = mybir.dt.bfloat16
ALU = mybir.AluOpType
ACT = mybir.ActivationFunctionType
AX = mybir.AxisListType

B, LQ, D = 8, 56, 128
S = 1500
NH, HD = 16, 8
NT = B * LQ
NC = 12
CK = S // NC
KB = 500
NJ = S // KB
CJ = KB // CK
HQ = NH * LQ
HALF = HQ // 2
NG = HQ // 128
GROUPS = [(3 * g, 3) for g in range(4)] + [(12, 2), (14, 2)]
GW = 32
ONE = 24
MLP = 4 * D
E_N = 3
RING = 3

WEIGHTS = [
    ("L0_Wq", 1, 128), ("L0_Wkv", 1, 256), ("L0_Wp", 1, 128), ("L0_Wss_q", 1, 256), ("L0_Wss_kv", 1, 256),
    ("L2_W_mod", 1, 768), ("L3_adaln_w", 1, 768),
    ("L1_Wq", 1, 128), ("L1_WkT", 1, 128), ("L1_Wv", 1, 128), ("L1_router_W", 3, 3), ("L1_e_w1", 9, 256),
    ("L1_e_w2", 6, 128), ("L1_gate_w1", 3, 128), ("L1_gate_w2", 1, 128), ("L1_out_w", 1, 128),
    ("L2_W_qkv", 1, 384), ("L2_W_proj", 1, 128), ("L2_W_qc", 1, 128), ("L2_W_kvc", 1, 256),
    ("L2_W_cproj", 1, 128), ("L2_W_mlp1", 1, 512), ("L2_W_mlp2", 4, 128),
    ("L3_qkv_w", 1, 384), ("L3_sa_proj_w", 1, 128), ("L3_q_w", 1, 128), ("L3_kv_w", 1, 256),
    ("L3_ca_proj_w", 1, 128), ("L3_fc1_w", 1, 512), ("L3_fc2_w", 4, 128),
]
W_AT, _w = {}, 0
for _name, _blocks, _cols in WEIGHTS:
    W_AT[_name] = (_w, _cols)
    _w += _blocks * _cols
W_COLS = _w
MODS = [("L0.scale_q", "L0_Wss_q", "L0_bss_q", 0), ("L0.scale_kv", "L0_Wss_kv", "L0_bss_kv", 0),
        ("L2.scale_a", "L2_W_mod", "L2_b_mod", 1), ("L2.scale_m", "L2_W_mod", "L2_b_mod", 4),
        ("L3.scale_a", "L3_adaln_w", "L3_adaln_b", 1), ("L3.scale_m", "L3_adaln_w", "L3_adaln_b", 4),
        ("L0.shift_q", "L0_Wss_q", "L0_bss_q", 1), ("L0.shift_kv", "L0_Wss_kv", "L0_bss_kv", 1),
        ("L2.shift_a", "L2_W_mod", "L2_b_mod", 0), ("L2.gate_a", "L2_W_mod", "L2_b_mod", 2),
        ("L2.shift_m", "L2_W_mod", "L2_b_mod", 3), ("L2.gate_m", "L2_W_mod", "L2_b_mod", 5),
        ("L3.shift_a", "L3_adaln_w", "L3_adaln_b", 0), ("L3.gate_a", "L3_adaln_w", "L3_adaln_b", 2),
        ("L3.shift_m", "L3_adaln_w", "L3_adaln_b", 3), ("L3.gate_m", "L3_adaln_w", "L3_adaln_b", 5)]
SCALES = 6
MOD = {m[0]: n for n, m in enumerate(MODS)}
VECTORS = [
    ("L0_bq", 1), ("L0_bkv", 2), ("L0_bp", 1),
    ("L1_ln_gamma", 1), ("L1_ln_beta", 1), ("L1_e_b1", 6), ("L1_e_b2", 3), ("L1_gate_b1", 1),
    ("L1_gate_b2", 1), ("L1_out_b", 1),
    ("L2_b_qkv", 3), ("L2_b_proj", 1), ("L2_b_qc", 1), ("L2_b_kvc", 2), ("L2_b_cproj", 1), ("L2_b_mlp1", 4),
    ("L2_b_mlp2", 1),
    ("L3_qkv_b", 3), ("L3_sa_proj_b", 1), ("L3_q_b", 1), ("L3_kv_b", 2), ("L3_ca_proj_b", 1), ("L3_fc1_b", 4),
    ("L3_fc2_b", 1),
]
V_AT, _v = {}, len(MODS)
for _name, _cols in VECTORS:
    V_AT[_name] = _v
    _v += _cols
V_AT["router_b"] = _v
V_COLS = _v + E_N
C_ID, C_HEAD, C_GROUP = 0, 128, 128 + NH
C_COLS = 128 + NH + NG
GELU_IN = 0.7978845608028654
GELU_CUBE = 0.044715
CONSTS = 9


class Ticks:

    def __init__(self, sem, names):
        assert len(set(names)) == len(names), [n for n in names if names.count(n) > 1]
        self.sem, self.names, self.at = sem, names, 0

    def done(self, ins, name):
        assert self.names[self.at] == name, (self.names[self.at], name)
        self.at += 1
        return ins.then_inc(self.sem, 1)

    def after(self, name):
        return self.names.index(name) + 1


class Periods:

    def __init__(self, sem, steps):
        self.sem, self.names, self.leads = sem, [n for n, _ in steps], [d for _, d in steps]
        assert len(set(self.names)) == len(self.names)
        self.at = 0

    def start(self, eng, cur, nxt):
        self.has = (cur is not None, nxt is not None)
        self.at = 0
        if cur is None and not any(self.leads):
            eng.sem_inc(self.sem, len(self.names))

    def done(self, ins, name):
        i = self.names.index(name)
        assert i >= self.at, name
        step = i + 1 - self.at
        assert self.has == (True, True) and step == 1 or self.has != (True, True), name
        self.at = i + 1
        if all(not self.has[d] for d in self.leads[i + 1:]):
            step += len(self.names) - i - 1
            self.at = len(self.names)
        return ins.then_inc(self.sem, step)

    def end(self):
        assert self.at in (0, len(self.names)), (self.at, self.names)

    def place(self, name, d):
        i = self.names.index(name)
        return (d + 1 - self.leads[i]) * len(self.names) + i + 1

    def after(self, name, n):
        return n * len(self.names) + self.place(name, 0)


def wait_steps(eng, n, *steps):
    last = {}
    for plan, name, d in steps:
        last[plan] = max(last.get(plan, -9999), plan.place(name, d))
    for plan, at in last.items():
        eng.wait_ge(plan.sem, n * len(plan.names) + at)


def periods(eng, body):
    body(None, (0, 0, 0))
    with eng.Fori(0, (B - 2) // 2) as j:
        body((2 * j, 0, j), (2 * j + 1, 1, j))
        body((2 * j + 1, 1, j), (2 * j + 2, 0, j + 1))
    body((B - 2, 0, (B - 2) // 2), (B - 1, 1, (B - 2) // 2))
    body((B - 1, 1, (B - 2) // 2), None)


def pixart_program(nc, ctx_nat, ctx_T, x_T, cond_T, weights, vectors, consts, out):
    ctx = ExitStack()
    with ctx:
        def sb(name, shape, dt=F32):
            return ctx.enter_context(nc.sbuf_tensor(name, shape, dt))

        def pb(name, shape):
            return ctx.enter_context(nc.psum_tensor(name, shape, F32))

        def sem(name):
            return ctx.enter_context(nc.semaphore(name))

        w_sb = sb("w_sb", [D, W_COLS])
        vec_sb = sb("vec_sb", [D, V_COLS])
        vec_half = sb("vec_half", [D, V_COLS])
        const_sb = sb("const_sb", [D, C_COLS])
        cond_sb = sb("cond_sb", [D, B])
        cond_t = sb("cond_t", [D, B])
        cond_silu = sb("cond_silu", [D, B])
        mod_sb = sb("mod_sb", [D, len(MODS), B])
        mean_mat = sb("mean_mat", [D, D])
        ones_bf = sb("ones_bf", [D, D], BF16)
        nat_sb = sb("nat_sb", [CK, B, NC, D])
        ctx_mv = sb("ctx_mv", [CK, B, NC, 2])
        mv_now = sb("mv_now", [CK, NC, 2])
        bn_tmp = sb("bn_tmp", [CK, NC, 6])
        rstd_in = sb("rstd_in", [CK, NC])
        neg_mean = sb("neg_mean", [CK, NC])
        rstd = sb("rstd", [CK, NC])
        minus_half = sb("minus_half", [CK, NC])
        hat_sb = sb("hat_sb", [CK, NC, D])
        ctxT_sb = sb("ctxT_sb", [D, 2, S])
        key_sb = sb("key_sb", [D, 2, S])
        keyr_sb = sb("keyr_sb", [D, 2, S], F32R)
        val_sb = sb("val_sb", [CK, 2, NC, len(GROUPS) * GW])
        qblk = sb("qblk", [D, 2, HQ])
        qblkr = sb("qblkr", [D, 2, HQ], F32R)
        shift_sb = sb("shift_sb", [D, 2, HQ], BF16)
        prob_sb = sb("prob_sb", [CK, 2, HQ])
        max_sb = sb("max_sb", [D, NG, NJ])
        max1 = sb("max1", [D, NG])
        maxb = sb("maxb", [D, NG], BF16)
        maxparts = sb("maxparts", [D, 2 * NG])
        o_sb = sb("o_sb", [D, 5 * LQ])
        osum_r = sb("osum_r", [LQ, NH])
        on_sb = sb("on_sb", [LQ, D])
        xslice = sb("xslice", [D, 2, LQ])
        tok = sb("tok", [D, 15, NT])
        s_max = sb("s_max", [LQ, 2, 1])
        s_sum = sb("s_sum", [LQ, 2, 1])
        s_rec = sb("s_rec", [LQ, 1])

        score_ps = pb("score_ps", [D, 2, 2, 512])
        oacc_ps = pb("oacc_ps", [D, 512])
        ring_ps = pb("ring_ps", [D, RING, 512])

        def w(name, block=0, lo=0, n=None):
            at, cols = W_AT[name]
            at += block * cols + lo
            return w_sb[:, at:at + (n or cols - lo)]

        def vec(name, j=0, half=False):
            at = V_AT[name] + j
            return (vec_half if half else vec_sb)[:, at:at + 1]

        def T(i):
            return tok[:, i, :]

        def scratch(i):
            return key_sb[:, i // 3, (i % 3) * NT:(i % 3 + 1) * NT]

        def by_batch(ap):
            return ap.rearrange("p (b q) -> p b q", q=LQ)

        def mod(name):
            return mod_sb[:, MOD[name], :].unsqueeze(2).broadcast_to([D, B, LQ])

        ident = const_sb[:, C_ID:C_ID + 128]
        x_t, xc_t, xh_t, q_t, k_t, o_t = (T(i) for i in range(6))

        eps_sb = sb("eps_sb", [D, 2])
        nat_loaded = [sem(f"context_loaded{u}") for u in range(2)]
        consts_ready = sem("constants_ready")
        settled = sem("settled")
        ev_t, anchor_t = T(6), T(7)
        rw_sb = ctxT_sb[:, 0, 0:9 * D].rearrange("p (e m) -> p e m", m=D)
        logit = (q_t, k_t, o_t)
        hidden = [T(9), T(10), T(11), T(13), scratch(0), scratch(1)]
        curve = [T(8), T(14), scratch(2), scratch(3), scratch(4), scratch(5)]

        def settle(eng):
            eng.sem_inc(settled, 1)

        class Heads:
            def __init__(self, tag, wkey, wval, bkey, bval, hat, eps=None, modulated=False, own=False):
                self.tag, self.wkey, self.wval, self.bkey, self.bval = tag, wkey, wval, bkey, bval
                self.hat, self.eps, self.modulated, self.own = hat, eps, modulated, own
                self.stats = modulated
                nj, self.nc, self.ck = (1, 1, LQ) if own else (NJ, NC, CK)
                self.nj = nj
                J = range(nj)
                mm = ["M0"] if own else [f"M{j}.{g}" for j in J for g in range(NG)]
                self.mm = mm
                pe, i = [], 0
                if hat:
                    pe += [(f"T{j}", 1) for j in J]
                if not own:
                    pe += [(f"K{j}", 1) for j in J]
                pe += [(f"V{j}", 1) for j in J]
                for c in range(self.nc):
                    pe.append((f"S{c}", 0))
                    take = 1 if own else 2
                    pe += [(m, 1) for m in mm[i:i + take]]
                    i += take
                    if c:
                        pe.append((f"PV{c - 1}", 0))
                assert i >= len(mm)
                pe += [(f"PV{self.nc - 1}", 0), ("MT", 1), ("OT", 0), ("OTT", 0)]
                act = ([(f"T{j}", 1) for j in J] if hat else []) + ([] if own else [(f"K{j}", 1) for j in J])
                act += [(f"E{c}", 0) for c in range(self.nc)]
                dve = []
                if self.stats:
                    dve += [("stats", 1), ("aggr", 1), ("keep", 1)]
                if hat:
                    dve += [("hat", 1)]
                dve += [(f"V{j}", 1) for j in J] + [(m, 1) for m in mm] + ([] if own else [("maxall", 1)])
                dve += [("maxb", 1), ("part0", 1), ("part1", 1), ("shift", 1)]
                dve += [("O", 0), ("sum0", 0), ("sum1", 0), ("norm0", 0), ("norm1", 0), ("OTT", 0)]
                pool = []
                if hat:
                    pool += ([] if self.stats else [("mv", 1)]) + [("var", 1), ("negmean", 1), ("rstd", 1)]
                if own:
                    pool += [("x", 1), ("k", 1)]
                pool += [("q", 1), ("qr", 1)] + [(f"kr{j}", 1) for j in J]
                self.pe = Periods(sem(f"{tag}_pe_done"), pe)
                self.act = Periods(sem(f"{tag}_act_done"), act)
                self.dve = Periods(sem(f"{tag}_dve_done"), dve)
                self.pool = Periods(sem(f"{tag}_pool_done"), pool)
                self.loaded = None if (hat or own) else [sem(f"{tag}_ctx_loaded{u}") for u in range(2)]
                reader = {}
                for j in J:
                    reader[f"T{j}"] = (self.act, f"T{j}")
                    reader[f"K{j}"] = (self.act, f"K{j}")
                    reader[f"V{j}"] = (self.dve, f"V{j}")
                for m in mm:
                    reader[m] = (self.dve, m)
                reader |= {"MT": (self.dve, "shift"), "OT": (self.dve, "norm1"), "OTT": (self.dve, "OTT")}
                self.reader = reader
                self.uses = [(n, d) for n, d in pe if n in reader]
                self.use_at = {n: i for i, (n, _) in enumerate(self.uses)}

            def bank(self, name):
                return self.use_at[name] % RING

            def ring_read(self, name, cur, nxt):
                i = self.use_at[name]
                ref = self.uses[i][1]
                same = [m for m in range(len(self.uses)) if m % RING == i % RING]
                before = [m for m in same if m < i and (cur is not None or self.uses[m][1])]
                if before:
                    other, lead = self.uses[before[-1]]
                    return [(*self.reader[other], lead - ref)]
                if cur is None:
                    return []
                other, lead = self.uses[same[-1]]
                return [(*self.reader[other], lead - ref - 1)]

            def tensor(self, pe, before):
                P, A, V, G = self.pe, self.act, self.dve, self.pool
                ck = self.ck
                before(pe)

                def key_maxima_scores(m, nxt, cur):
                    n, u, half = nxt
                    free = self.ring_read(m, cur, nxt)
                    ps = ring_ps[:, self.bank(m), :]
                    if self.own:
                        wait_steps(pe, n, (G, "kr0", 0), *free)
                        for g in range(NG):
                            last = pe.matmul(ps[:, g * LQ:(g + 1) * LQ], qblkr[:, u, g * 128:(g + 1) * 128],
                                             keyr_sb[:, u, 0:LQ], start=True, stop=True)
                    else:
                        j, g = (int(t) for t in m[1:].split("."))
                        wait_steps(pe, n, *([(G, f"kr{j}", 0)] if g == 0 else []), *free)
                        last = pe.matmul(ps[:, 0:KB], qblkr[:, u, g * 128:(g + 1) * 128],
                                         keyr_sb[:, u, j * KB:(j + 1) * KB], start=True, stop=True)
                    P.done(last, m)

                def prepare(nxt, cur):
                    n, u, half = nxt
                    if self.hat:
                        pe.wait_ge(V.sem, V.after("hat", n))
                        for j in range(NJ):
                            wait_steps(pe, n, *self.ring_read(f"T{j}", cur, nxt))
                            for c in range(CJ):
                                last = pe.transpose(ring_ps[:, self.bank(f"T{j}"), c * CK:(c + 1) * CK],
                                                    hat_sb[:, j * CJ + c, :], ident[0:CK, 0:CK])
                            P.done(last, f"T{j}")
                    if self.loaded:
                        pe.wait_ge(self.loaded[u], 16 * (half + 1))
                    if not self.own:
                        for j in range(NJ):
                            wait_steps(pe, n, *([(A, f"T{j}", 0)] if self.hat else []),
                                       *self.ring_read(f"K{j}", cur, nxt))
                            last = pe.matmul(ring_ps[:, self.bank(f"K{j}"), 0:KB], self.wkey,
                                             ctxT_sb[:, u, j * KB:(j + 1) * KB], start=True, stop=True)
                            P.done(last, f"K{j}")
                    for j in range(self.nj):
                        wait_steps(pe, n, *([(G, "x", 0)] if self.own else []), *self.ring_read(f"V{j}", cur, nxt))
                        if self.own:
                            settle(pe)
                            last = pe.matmul(ring_ps[0:LQ, self.bank("V0"), 0:D], xslice[:, u, :], self.wval,
                                             start=True, stop=True)
                        else:
                            for c in range(CJ):
                                k0 = (j * CJ + c) * CK
                                last = pe.matmul(ring_ps[0:CK, self.bank(f"V{j}"), c * D:(c + 1) * D],
                                                 ctxT_sb[:, u, k0:k0 + CK], self.wval, start=True, stop=True)
                        P.done(last, f"V{j}")

                def scores(c, cur):
                    n, u, half = cur
                    need = []
                    if c == 0:
                        need += [(V, "shift", 0), (G, f"kr{self.nj - 1}", 0)]
                        need += [] if self.own else [(A, f"K{NJ - 1}", 0)]
                    need.append((A, f"E{c - 2}", 0) if c >= 2 else (A, f"E{max(self.nc - 2 + c, 0)}", -1))
                    wait_steps(pe, n, *need)
                    buf = (c if not self.own else u) % 2
                    for h in range(2):
                        cols = slice(h * HALF, (h + 1) * HALF)
                        pe.matmul(score_ps[0:ck, buf, h, 0:HALF], key_sb[:, u, c * CK:c * CK + ck],
                                  qblk[:, u, cols], start=True, stop=False)
                        last = pe.matmul(score_ps[0:ck, buf, h, 0:HALF], ones_bf[:, 0:ck],
                                         shift_sb[:, u, cols], start=False, stop=True)
                    P.done(last, f"S{c}")

                def attend(c, cur):
                    n, u, half = cur
                    wait_steps(pe, n, (A, f"E{c}", 0),
                               *([(V, f"V{self.nj - 1}", 0), (V, "O", -1)] if c == 0 else []))
                    buf = (c if not self.own else u) % 2
                    if self.own:
                        settle(pe)
                    for g, (h0, nh) in enumerate(GROUPS):
                        q = g % 4
                        at = 0 if g < 4 else 3 * LQ
                        last = pe.matmul(oacc_ps[q * GW:(q + 1) * GW, at:at + nh * LQ],
                                         val_sb[0:ck, u, c, g * GW:(g + 1) * GW],
                                         prob_sb[0:ck, buf, h0 * LQ:(h0 + nh) * LQ],
                                         start=(c == 0 and g < 4), stop=(c == self.nc - 1), skip_group_check=True)
                    P.done(last, f"PV{c}")

                def body(cur, nxt):
                    P.start(pe, cur, nxt)
                    if nxt:
                        prepare(nxt, cur)
                    i = 0
                    for c in range(self.nc):
                        if cur:
                            scores(c, cur)
                        take = 1 if self.own else 2
                        if nxt:
                            for m in self.mm[i:i + take]:
                                key_maxima_scores(m, nxt, cur)
                        i += take
                        if c and cur:
                            attend(c - 1, cur)
                    if cur:
                        attend(self.nc - 1, cur)
                    if nxt:
                        wait_steps(pe, nxt[0], (V, "part1", 0), *self.ring_read("MT", cur, nxt))
                        P.done(pe.transpose(ring_ps[0:2 * NG, self.bank("MT"), 0:D], maxparts[:, :], ident), "MT")
                    if cur:
                        n, u, half = cur
                        wait_steps(pe, n, (V, "O", 0), *self.ring_read("OT", cur, nxt))
                        settle(pe)
                        for i in range(5):
                            rows = D if i < 3 else 64
                            at = 128 * i if i < 3 else 384 + 64 * (i - 3)
                            last = pe.transpose(ring_ps[0:LQ, self.bank("OT"), at:at + rows],
                                                o_sb[0:rows, i * LQ:(i + 1) * LQ], ident[0:rows, 0:rows])
                        P.done(last, "OT")
                        wait_steps(pe, n, (V, "norm1", 0), *self.ring_read("OTT", cur, nxt))
                        settle(pe)
                        P.done(pe.transpose(ring_ps[:, self.bank("OTT"), 0:LQ], on_sb[:, :], ident[0:LQ, 0:LQ]),
                               "OTT")
                    P.end()

                periods(pe, body)

            def scalar(self, act):
                P, A, V = self.pe, self.act, self.dve

                def body(cur, nxt):
                    A.start(act, cur, nxt)
                    if nxt:
                        n, u, half = nxt
                        if self.hat:
                            for j in range(NJ):
                                act.wait_ge(P.sem, P.after(f"T{j}", n))
                                settle(act)
                                src, dst = ring_ps[:, self.bank(f"T{j}"), 0:KB], ctxT_sb[:, u, j * KB:(j + 1) * KB]
                                if self.modulated:
                                    ins = act.activation(dst, src, ACT.Identity,
                                                         bias=mod_sb[:, MOD["L0.shift_kv"], bass.ds(n, 1)],
                                                         scale=mod_sb[:, MOD["L0.scale_kv"], bass.ds(n, 1)])
                                else:
                                    ins = act.copy(dst, src)
                                A.done(ins, f"T{j}")
                        if not self.own:
                            for j in range(NJ):
                                act.wait_ge(P.sem, P.after(f"K{j}", n))
                                A.done(act.activation(key_sb[:, u, j * KB:(j + 1) * KB],
                                                      ring_ps[:, self.bank(f"K{j}"), 0:KB], ACT.Identity,
                                                      bias=self.bkey), f"K{j}")
                    if cur:
                        n, u, half = cur
                        ck = self.ck
                        for c in range(self.nc):
                            wait_steps(act, n, (P, f"S{c}", 0),
                                       (P, f"PV{c - 2}", 0) if c >= 2 else (P, f"PV{max(self.nc - 2 + c, 0)}", -1))
                            buf = (c if not self.own else u) % 2
                            dst = prob_sb[0:ck, buf, :].rearrange("p (h q) -> p h q", h=2)
                            A.done(act.activation(dst, score_ps[0:ck, buf, :, 0:HALF], ACT.Exp), f"E{c}")
                    A.end()

                periods(act, body)

            def vector(self, dve):
                P, V, G = self.pe, self.dve, self.pool

                def body(cur, nxt):
                    V.start(dve, cur, nxt)
                    if nxt:
                        n, u, half = nxt
                        if self.stats:
                            nat_b = nat_sb[:, n, :, :]
                            dve.wait_ge(nat_loaded[u], 16 * (half + 1))
                            for c in range(NC):
                                last = dve.bn_stats(bn_tmp[:, c, :], nat_b[:, c, :])
                            V.done(last, "stats")
                            dve.wait_ge(V.sem, V.after("stats", n))
                            settle(dve)
                            for c in range(NC):
                                last = dve.bn_aggr(mv_now[:, c, :], bn_tmp[:, c, :])
                            V.done(last, "aggr")
                            dve.wait_ge(V.sem, V.after("aggr", n))
                            V.done(dve.tensor_copy(ctx_mv[:, n, :, :], mv_now[:, :, :]), "keep")
                        if self.hat:
                            dve.wait_ge(G.sem, G.after("rstd", n))
                            if cur:
                                dve.wait_ge(P.sem, P.after(f"T{NJ - 1}", n - 1))
                            for c in range(NC):
                                last = dve.tensor_scalar(hat_sb[:, c, :], nat_sb[:, n, c, :], neg_mean[:, c:c + 1],
                                                         rstd[:, c:c + 1], ALU.add, ALU.mult)
                            V.done(last, "hat")
                        for j in range(self.nj):
                            dve.wait_ge(P.sem, P.after(f"V{j}", n))
                            if self.own:
                                src = ring_ps[0:LQ, self.bank("V0"), 0:D].rearrange("p (c k) -> p c k", c=1)
                                dst = val_sb[0:LQ, u, 0:1, :]
                            else:
                                src = ring_ps[0:CK, self.bank(f"V{j}"), :].rearrange("p (c k) -> p c k", c=CJ)
                                dst = val_sb[0:CK, u, j * CJ:(j + 1) * CJ, :]
                            dst = dst.rearrange("p c (g k) -> p c g k", k=GW)
                            dve.tensor_copy(dst[:, :, 0:4, 0:24], src[:, :, 0:96].rearrange("p c (g k) -> p c g k", k=24))
                            V.done(dve.tensor_copy(dst[:, :, 4:6, 0:16],
                                                   src[:, :, 96:128].rearrange("p c (g k) -> p c g k", k=16)), f"V{j}")
                        for m in self.mm:
                            dve.wait_ge(P.sem, P.after(m, n))
                            ps = ring_ps[:, self.bank(m), :]
                            if self.own:
                                ins = dve.tensor_reduce(max1[:, :], ps[:, 0:NG * LQ].rearrange("p (g k) -> p g k", k=LQ),
                                                        AX.X, ALU.max)
                            else:
                                j, g = (int(t) for t in m[1:].split("."))
                                ins = dve.tensor_reduce(max_sb[:, g, j:j + 1], ps[:, 0:KB], AX.X, ALU.max)
                            V.done(ins, m)
                        dve.wait_ge(V.sem, V.after(self.mm[-1], n))
                        if not self.own:
                            V.done(dve.tensor_reduce(max1[:, :], max_sb[:, :, :], AX.X, ALU.max), "maxall")
                            dve.wait_ge(V.sem, V.after("maxall", n))
                        V.done(dve.tensor_scalar(maxb[:, :], max1[:, :], -1.0, None, ALU.mult), "maxb")
                        dve.wait_ge(V.sem, V.after("maxb", n))
                        V.done(dve.tensor_copy(maxparts[:, 0:NG], maxb[:, :]), "part0")
                        V.done(dve.scalar_tensor_tensor(maxparts[:, NG:2 * NG], max1[:, :], -1.0, maxb[:, :],
                                                        ALU.mult, ALU.subtract), "part1")
                        dve.wait_ge(P.sem, P.after("MT", n))
                        V.done(dve.tensor_tensor(
                            shift_sb[0:2 * NG, u, :].rearrange("p (g c) -> p g c", g=NG),
                            ring_ps[0:2 * NG, self.bank("MT"), 0:D].unsqueeze(1).broadcast_to([2 * NG, NG, D]),
                            const_sb[0:2 * NG, C_GROUP:C_GROUP + NG].unsqueeze(2).broadcast_to([2 * NG, NG, D]),
                            ALU.mult), "shift")
                    if cur:
                        n, u, half = cur
                        dve.wait_ge(P.sem, P.after(f"PV{self.nc - 1}", n))
                        dve.tensor_copy(o_sb[:, 0:3 * LQ], oacc_ps[:, 0:3 * LQ])
                        V.done(dve.tensor_copy(o_sb[0:64, 3 * LQ:5 * LQ], oacc_ps[0:64, 3 * LQ:5 * LQ]), "O")
                        dve.wait_ge(P.sem, P.after("OT", n))
                        ps = ring_ps[0:LQ, self.bank("OT"), :]

                        def view(base, off, dims):
                            return bass.AP(tensor=base.tensor, offset=base.offset + off, ap=[list(base.ap[0])] + dims)

                        V.done(dve.reciprocal(view(osum_r[:, :], 0, [[1, 3], [3, 4]]),
                                              view(ps, ONE, [[128, 3], [GW, 4]])), "sum0")
                        V.done(dve.reciprocal(view(osum_r[:, :], 12, [[1, 2], [2, 2]]),
                                              view(ps, 384 + ONE, [[64, 2], [GW, 2]])), "sum1")
                        dve.wait_ge(V.sem, V.after("sum1", n))
                        V.done(dve.tensor_tensor(view(on_sb[:, :], 0, [[8, 3], [24, 4], [1, 8]]),
                                                 view(ps, 0, [[136, 3], [GW, 4], [1, 8]]),
                                                 view(osum_r[:, :], 0, [[1, 3], [3, 4], [0, 8]]), ALU.mult), "norm0")
                        V.done(dve.tensor_tensor(view(on_sb[:, :], 96, [[8, 2], [16, 2], [1, 8]]),
                                                 view(ps, 384, [[72, 2], [GW, 2], [1, 8]]),
                                                 view(osum_r[:, :], 12, [[1, 2], [2, 2], [0, 8]]), ALU.mult), "norm1")
                        dve.wait_ge(P.sem, P.after("OTT", n))
                        V.done(dve.tensor_scalar(by_batch(o_t)[:, n, :], ring_ps[:, self.bank("OTT"), 0:LQ],
                                                 self.bval, None, ALU.add), "OTT")
                    V.end()

                periods(dve, body)

            def gpsimd(self, pool, before):
                P, A, V, G = self.pe, self.act, self.dve, self.pool
                self.started = False

                def body(cur, nxt):
                    G.start(pool, cur, nxt)
                    if nxt:
                        n, u, half = nxt
                        if self.hat:
                            if self.stats:
                                pool.wait_ge(V.sem, V.after("keep", n))
                            else:
                                if cur:
                                    pool.wait_ge(V.sem, V.after("hat", cur[0]))
                                settle(pool)
                                G.done(pool.tensor_copy(mv_now[:, :, :], ctx_mv[:, n, :, :]), "mv")
                                pool.wait_ge(G.sem, G.after("mv", n))
                            settle(pool)
                            mv = mv_now[:, :, :]
                            G.done(pool.tensor_scalar(rstd_in[:, :], mv[:, :, 1], self.eps, None, ALU.add), "var")
                            G.done(pool.tensor_scalar(neg_mean[:, :], mv[:, :, 0], -1.0, None, ALU.mult), "negmean")
                            pool.wait_ge(G.sem, G.after("negmean", n))
                            G.done(pool.tensor_tensor(rstd[:, :], rstd_in[:, :], minus_half[:, :], ALU.pow), "rstd")
                        if not self.started:
                            before(pool)
                            self.started = True
                        if cur:
                            pool.wait_ge(P.sem, P.after(f"PV{self.nc - 1}", cur[0] - 1))
                        settle(pool)
                        if self.own:
                            G.done(pool.tensor_copy(xslice[:, u, :], by_batch(xh_t)[:, n, :]), "x")
                            G.done(pool.tensor_copy(key_sb[:, u, 0:LQ], by_batch(k_t)[:, n, :]), "k")
                        q3 = qblk[:, u, :].rearrange("p (h q) -> p h q", h=NH)
                        G.done(pool.tensor_tensor(q3, by_batch(q_t)[:, n, :].unsqueeze(1).broadcast_to([D, NH, LQ]),
                                                  const_sb[:, C_HEAD:C_HEAD + NH].unsqueeze(2).broadcast_to([D, NH, LQ]),
                                                  ALU.mult), "q")
                        pool.wait_ge(G.sem, G.after("q", n))
                        settle(pool)
                        G.done(pool.tensor_copy(qblkr[:, u, :], qblk[:, u, :]), "qr")
                        for j in range(self.nj):
                            cols = slice(0, LQ) if self.own else slice(j * KB, (j + 1) * KB)
                            if not self.own:
                                pool.wait_ge(A.sem, A.after(f"K{j}", n))
                                settle(pool)
                            G.done(pool.tensor_copy(keyr_sb[:, u, cols], key_sb[:, u, cols]), f"kr{j}")
                    G.end()

                periods(pool, body)

        class Evidence:
            def __init__(self):
                self.pe = Periods(sem("ev_pe_done"), [("S", 1), ("PT0", 0), ("PT1", 0), ("U", 0), ("UT", 0)])
                self.act = Periods(sem("ev_act_done"), [("E", 1)])
                self.dve = Periods(sem("ev_dve_done"), [("max", 1), ("PT0", 0), ("PT1", 0), ("rec", 0), ("U", 0),
                                                        ("UT", 0)])
                self.pool = Periods(sem("ev_pool_done"), [("q", 1)])
                self.loaded = [sem(f"ev_ctx_loaded{u}") for u in range(2)]
                self.bank = {"PT0": 0, "PT1": 1, "U": 2, "UT": 0}

            def scores(self):
                return score_ps[0:LQ, :, :, :].rearrange("p a b c -> p (a b) c")[:, 0:NJ, 0:KB]

            def tensor(self, pe, before):
                P, A, V, G = self.pe, self.act, self.dve, self.pool
                before(pe)

                def body(cur, nxt):
                    P.start(pe, cur, nxt)
                    if nxt:
                        n, u, half = nxt
                        pe.wait_ge(self.loaded[u], 16 * (half + 1))
                        pe.wait_ge(G.sem, G.after("q", n))
                        if cur:
                            pe.wait_ge(A.sem, A.after("E", n - 1))
                        for j in range(NJ):
                            last = pe.matmul(self.scores()[:, j, :], xslice[:, u, :],
                                             ctxT_sb[:, u, j * KB:(j + 1) * KB], start=True, stop=True)
                        P.done(last, "S")
                    if cur:
                        n, u, half = cur
                        pe.wait_ge(A.sem, A.after("E", n))
                        for i in range(2):
                            pe.wait_ge(V.sem, V.after(("UT", "PT1")[i], n - 1))
                            settle(pe)
                            for c in range(6):
                                k0 = (6 * i + c) * CK
                                last = pe.transpose(ring_ps[0:CK, self.bank[f"PT{i}"], c * LQ:(c + 1) * LQ],
                                                    key_sb[0:LQ, u, k0:k0 + CK], ident[0:LQ, 0:LQ])
                            P.done(last, f"PT{i}")
                        pe.wait_ge(V.sem, V.after("PT1", n))
                        for c in range(NC):
                            last = pe.matmul(ring_ps[0:LQ, self.bank["U"], 0:D], hat_sb[:, c, 0:LQ],
                                             nat_sb[:, n, c, :], start=(c == 0), stop=(c == NC - 1))
                        P.done(last, "U")
                        pe.wait_ge(V.sem, V.after("U", n))
                        settle(pe)
                        P.done(pe.transpose(ring_ps[:, self.bank["UT"], 0:LQ], on_sb[:, :], ident[0:LQ, 0:LQ]), "UT")
                    P.end()

                periods(pe, body)

            def scalar(self, act):
                P, A, V = self.pe, self.act, self.dve

                def body(cur, nxt):
                    A.start(act, cur, nxt)
                    if nxt:
                        n, u, half = nxt
                        act.wait_ge(V.sem, V.after("max", n))
                        if cur:
                            act.wait_ge(V.sem, V.after("U", cur[0] - 1))
                        A.done(act.activation(key_sb[0:LQ, u, :].rearrange("p (j k) -> p j k", j=NJ), self.scores(),
                                              ACT.Exp, bias=s_max[:, u, :], accum_out=s_sum[:, u, :]), "E")
                    A.end()

                periods(act, body)

            def vector(self, dve):
                P, A, V = self.pe, self.act, self.dve

                def body(cur, nxt):
                    V.start(dve, cur, nxt)
                    if nxt:
                        n, u, half = nxt
                        dve.wait_ge(P.sem, P.after("S", n))
                        V.done(dve.tensor_reduce(s_max[:, u, :], self.scores(), AX.XY, ALU.max, negate=True), "max")
                    if cur:
                        n, u, half = cur
                        for i in range(2):
                            dve.wait_ge(P.sem, P.after(f"PT{i}", n))
                            src = ring_ps[0:CK, self.bank[f"PT{i}"], 0:6 * LQ].rearrange("p (c q) -> p c q", q=LQ)
                            V.done(dve.tensor_copy(hat_sb[:, 6 * i:6 * i + 6, 0:LQ], src), f"PT{i}")
                        dve.wait_ge(A.sem, A.after("E", n))
                        V.done(dve.reciprocal(s_rec[:, :], s_sum[:, u, :]), "rec")
                        dve.wait_ge(V.sem, V.after("rec", n))
                        dve.wait_ge(P.sem, P.after("U", n))
                        V.done(dve.tensor_scalar(on_sb[:, :], ring_ps[0:LQ, self.bank["U"], 0:D], s_rec[:, 0:1], None,
                                                 ALU.mult), "U")
                        dve.wait_ge(P.sem, P.after("UT", n))
                        V.done(dve.tensor_copy(by_batch(o_t)[:, n, :], ring_ps[:, self.bank["UT"], 0:LQ]), "UT")
                    V.end()

                periods(dve, body)

            def gpsimd(self, pool, before):
                P, G = self.pe, self.pool
                before(pool)

                def body(cur, nxt):
                    G.start(pool, cur, nxt)
                    if nxt:
                        n, u, half = nxt
                        if cur:
                            pool.wait_ge(P.sem, P.after("S", cur[0]))
                            settle(pool)
                        G.done(pool.tensor_copy(xslice[:, u, :], by_batch(q_t)[:, n, :]), "q")
                    G.end()

                periods(pool, body)

        def load_context(sp, loaded, used):
            for u in range(2):
                sp.dma_start(ctxT_sb[:, u, :], ctx_T[u]).then_inc(loaded[u], 16)
            with sp.Fori(0, (B - 2) // 2) as j:
                for u in range(2):
                    s, v = used(2 * j + u)
                    sp.wait_ge(s, v)
                    sp.dma_start(ctxT_sb[:, u, :], ctx_T[2 * j + 2 + u]).then_inc(loaded[u], 16)

        class Dense:

            def __init__(self, tag, products, curves, values):
                self.pe = Ticks(sem(f"{tag}_pe_done"), [p[0] for p in products])
                self.act = Ticks(sem(f"{tag}_act_done"), curves)
                self.dve = Ticks(sem(f"{tag}_dve_done"), values)
                self.products = products

            def ps(self, name):
                return ring_ps[:, self.pe.names.index(name) % RING, 0:NT]

            def product(self, pe, name, pairs, out=None):
                i = self.pe.names.index(name)
                if i >= RING:
                    _, reader, step = self.products[i - RING]
                    plan = self.act if reader == "act" else self.dve
                    pe.wait_ge(plan.sem, plan.after(step))
                for k, (lhsT, rhs) in enumerate(pairs):
                    last = pe.matmul(self.ps(name) if out is None else out, lhsT, rhs, start=(k == 0),
                                     stop=(k == len(pairs) - 1))
                self.pe.done(last, name)

            @staticmethod
            def ln_products(t):
                return [(f"{t}.mean", "dve", f"{t}.xc"), (f"{t}.var", "act", f"{t}.sd")]

            @staticmethod
            def ln_values(t):
                return [f"{t}.xc", f"{t}.sq", f"{t}.rs", f"{t}.xh"]

            def ln_pe(self, pe, t, x_ready):
                if x_ready:
                    pe.wait_ge(self.dve.sem, self.dve.after(x_ready))
                self.product(pe, f"{t}.mean", [(mean_mat[:, :], x_t)])
                pe.wait_ge(self.dve.sem, self.dve.after(f"{t}.sq"))
                self.product(pe, f"{t}.var", [(mean_mat[:, :], T(6))])

            def ln_act(self, act, t, eps):
                act.wait_ge(self.pe.sem, self.pe.after(f"{t}.var"))
                self.act.done(act.activation(T(7), self.ps(f"{t}.var"), ACT.Sqrt, bias=eps_sb[:, eps:eps + 1]),
                              f"{t}.sd")

            def step(self, dve, ins, name):
                self.dve.done(ins, name)
                dve.wait_ge(self.dve.sem, self.dve.after(name))

            def ln_dve(self, dve, t):
                dve.wait_ge(self.pe.sem, self.pe.after(f"{t}.mean"))
                self.step(dve, dve.tensor_tensor(xc_t, x_t, self.ps(f"{t}.mean"), ALU.subtract), f"{t}.xc")
                self.step(dve, dve.tensor_tensor(T(6), xc_t, xc_t, ALU.mult), f"{t}.sq")
                dve.wait_ge(self.act.sem, self.act.after(f"{t}.sd"))
                self.step(dve, dve.reciprocal(T(6), T(7)), f"{t}.rs")
                self.step(dve, dve.tensor_tensor(xh_t, xc_t, T(6), ALU.mult), f"{t}.xh")

            def modulate(self, dve, scale, shift, t):
                self.step(dve, dve.tensor_tensor(by_batch(xh_t), by_batch(xh_t), mod(scale), ALU.mult), f"{t}.scaled")
                self.step(dve, dve.tensor_tensor(by_batch(xh_t), by_batch(xh_t), mod(shift), ALU.add), f"{t}.shifted")

            def gated(self, dve, y, gate, t):
                self.step(dve, dve.tensor_tensor(by_batch(y), by_batch(y), mod(gate), ALU.mult), f"{t}.gated")
                self.step(dve, dve.tensor_tensor(x_t, x_t, y, ALU.add), f"{t}.x")

        L = Dense
        d0 = Dense("d0", [("mods", "dve", "mods"), *L.ln_products("ln"), ("q", "dve", "q")],
                   ["tanh", "ln.sd"],
                   ["half", "silu", "mods", "scales", *L.ln_values("ln"), "m.scaled", "m.shifted", "q"])
        att0 = Heads("att0", w("L0_Wkv", 0, 0, 128), w("L0_Wkv", 0, 128, 128), vec("L0_bkv", 0), vec("L0_bkv", 1),
                     hat=True, eps=1e-5, modulated=True)
        d1 = Dense("d1", [("proj", "dve", "x"), *L.ln_products("ln"), ("q", "dve", "q"), ("qk", "dve", "qk")],
                   ["ln.sd"], ["x", *L.ln_values("ln"), "nx", "q", "qk"])
        evi = Evidence()
        H = [(e, r) for e in range(E_N) for r in range(2)]

        def own_products(t):
            return [*L.ln_products(t), (f"{t}.q", "dve", f"{t}.q"), (f"{t}.k", "dve", f"{t}.k")]

        def own_values(t):
            return [*L.ln_values(t), f"{t}.scaled", f"{t}.shifted", f"{t}.q", f"{t}.k"]

        d2 = Dense("d2", [("ev", "dve", "ev"), *[(f"l{e}", "dve", f"l{e}") for e in range(E_N)],
                          ("g1", "dve", "gu"), ("g2", "act", "gt2"),
                          *[(f"u{e}{r}", "dve", f"u{e}{r}") for e, r in H],
                          *[(f"o{e}", "dve", f"o{e}") for e in range(E_N)],
                          ("out", "dve", "outg"), *own_products("own")],
                   ["gt", *[f"p{e}" for e in range(E_N)], "gt2", *[f"t{e}{r}" for e, r in H], "own.sd"],
                   ["rw", "anchor", "ev", *[f"l{e}" for e in range(E_N)], "m01", "m", *[f"d{e}" for e in range(E_N)],
                    "gu", "gh", "s01", "s", "r", *[f"p{e}" for e in range(E_N)], "g",
                    *[f"u{e}{r}" for e, r in H], *[f"h{e}{r}" for e, r in H],
                    "o0", "r0", "o1", "r1", "a1", "o2", "r2", "a2", "outg", "x", *own_values("own")])
        att_own = {"L2": Heads("own2", None, w("L2_W_qkv", 0, 256, 128), None, vec("L2_b_qkv", 2), hat=False, own=True),
                   "L3": Heads("own3", None, w("L3_qkv_w", 0, 256, 128), None, vec("L3_qkv_b", 2), hat=False, own=True)}
        att_ctx = {"L2": Heads("att2", w("L2_W_kvc", 0, 0, 128), w("L2_W_kvc", 0, 128, 128), vec("L2_b_kvc", 0),
                               vec("L2_b_kvc", 1), hat=True, eps=1e-6),
                   "L3": Heads("att3", w("L3_kv_w", 0, 0, 128), w("L3_kv_w", 0, 128, 128), vec("L3_kv_b", 0),
                               vec("L3_kv_b", 1), hat=False)}
        NAMES = {"L2": dict(qkv="L2_W_qkv", qkv_b="L2_b_qkv", proj="L2_W_proj", proj_b="L2_b_proj", q="L2_W_qc",
                            q_b="L2_b_qc", cproj="L2_W_cproj", cproj_b="L2_b_cproj", w1="L2_W_mlp1", b1="L2_b_mlp1",
                            w2="L2_W_mlp2", b2="L2_b_mlp2"),
                 "L3": dict(qkv="L3_qkv_w", qkv_b="L3_qkv_b", proj="L3_sa_proj_w", proj_b="L3_sa_proj_b", q="L3_q_w",
                            q_b="L3_q_b", cproj="L3_ca_proj_w", cproj_b="L3_ca_proj_b", w1="L3_fc1_w", b1="L3_fc1_b",
                            w2="L3_fc2_w", b2="L3_fc2_b")}
        d_mid = {l: Dense(f"dm{l}", [("proj", "dve", "y"), *L.ln_products("ln"), ("q", "dve", "q")], ["ln.sd"],
                          ["y", "y.gated", "y.x", *L.ln_values("ln"), "q"]) for l in ("L2", "L3")}
        J4 = range(4)

        def end_part(l, follow):
            return Dense(f"de{l}", [("proj", "dve", "x"), *L.ln_products("ln"), *[(f"u{j}", "dve", f"u{j}") for j in J4],
                                    ("y", "dve", "y"), *(own_products("own") if follow else [])],
                         ["ln.sd", *[f"t{j}" for j in J4], *(["own.sd"] if follow else [])],
                         ["x", *L.ln_values("ln"), "m.scaled", "m.shifted",
                          *[f"{s}{j}" for j in J4 for s in ("u", "sq", "cu", "in")], *[f"h{j}" for j in J4],
                          "y", "y.gated", "y.x", *(own_values("own") if follow else [])])

        d_end = {"L2": end_part("L2", True), "L3": end_part("L3", False)}

        def own_pe(d, pe, l, x_ready):
            d.ln_pe(pe, "own", x_ready)
            pe.wait_ge(d.dve.sem, d.dve.after("own.shifted"))
            d.product(pe, "own.q", [(w(NAMES[l]["qkv"], 0, 0, 128), xh_t)])
            d.product(pe, "own.k", [(w(NAMES[l]["qkv"], 0, 128, 128), xh_t)])

        def own_dve(d, dve, l):
            d.ln_dve(dve, "own")
            d.modulate(dve, f"{l}.scale_a", f"{l}.shift_a", "own")
            dve.wait_ge(d.pe.sem, d.pe.after("own.q"))
            d.step(dve, dve.tensor_scalar(q_t, d.ps("own.q"), vec(NAMES[l]["qkv_b"], 0), HD ** -0.5, ALU.add, ALU.mult),
                   "own.q")
            dve.wait_ge(d.pe.sem, d.pe.after("own.k"))
            d.step(dve, dve.tensor_scalar(k_t, d.ps("own.k"), vec(NAMES[l]["qkv_b"], 1), None, ALU.add), "own.k")

        def last_output(att):
            return att.dve.sem, att.dve.after("OTT" if isinstance(att, Heads) else "UT", B - 1)

        loaded_early = sem("condition_and_constants_loaded")
        loaded_w0 = sem("first_weights_loaded")
        loaded_w1 = sem("other_weights_loaded")
        loaded_x = sem("tokens_loaded")
        stored = sem("output_stored")

        block = ctx.enter_context(nc.Block())

        @block.sync
        def _(sp):
            w0 = W_AT["L1_Wq"][0]
            sp.dma_start(cond_sb[:, :], cond_T).then_inc(loaded_early, 16)
            sp.dma_start(vec_sb[:, :], vectors).then_inc(loaded_early, 16)
            sp.dma_start(const_sb[:, :], consts).then_inc(loaded_early, 16)
            sp.dma_start(x_t, x_T).then_inc(loaded_x, 16)
            sp.dma_start(w_sb[:, 0:w0], weights[:, 0:w0]).then_inc(loaded_w0, 16)
            for u in range(2):
                sp.dma_start(nat_sb[:, u, :, :], ctx_nat[u]).then_inc(nat_loaded[u], 16)
            sp.dma_start(w_sb[:, w0:W_COLS], weights[:, w0:W_COLS]).then_inc(loaded_w1, 16)
            for n in range(2, B):
                sp.wait_ge(nat_loaded[n % 2], 16 * (n // 2))
                sp.dma_start(nat_sb[:, n, :, :], ctx_nat[n]).then_inc(nat_loaded[n % 2], 16)
            sp.wait_ge(att0.pe.sem, att0.pe.after(f"V{NJ - 1}", B - 1))
            load_context(sp, evi.loaded, lambda n: (evi.pe.sem, evi.pe.after("S", n)))
            a2, a3 = att_ctx["L2"], att_ctx["L3"]
            sp.wait_ge(a2.pe.sem, a2.pe.after(f"V{NJ - 1}", B - 1))
            load_context(sp, a3.loaded, lambda n: (a3.pe.sem, a3.pe.after(f"V{NJ - 1}", n)))
            d = d_end["L3"]
            sp.wait_ge(d.dve.sem, d.dve.after("y.x"))
            sp.dma_start(out, x_t).then_inc(stored, 16)
            sp.wait_ge(stored, 16)

        @block.gpsimd
        def _(pool):
            pool.memset(mean_mat[:, :], 1.0 / D).then_inc(consts_ready, 1)
            pool.memset(minus_half[:, :], -0.5).then_inc(consts_ready, 1)
            pool.memset(eps_sb[:, 0:1], 1e-5).then_inc(consts_ready, 1)
            pool.memset(eps_sb[:, 1:2], 1e-6).then_inc(consts_ready, 1)
            pool.memset(ones_bf[:, :], 1.0).then_inc(consts_ready, 1)
            pool.memset(shift_sb[:, :, :], 0.0).then_inc(consts_ready, 1)
            pool.memset(val_sb[:, :, :, :], 0.0).then_inc(consts_ready, 1)
            pool.wait_ge(consts_ready, 7)
            for u in range(2):
                pool.memset(val_sb[:, u, :, :].rearrange("p c (g k) -> p (c g) k", k=GW)[:, :, ONE:ONE + 1], 1.0)\
                    .then_inc(consts_ready, 1)
            pool.wait_ge(consts_ready, CONSTS)
            pool.wait_ge(loaded_early, 48)

            def queries(d, name):
                return lambda eng: eng.wait_ge(d.dve.sem, d.dve.after(name))

            att0.gpsimd(pool, queries(d0, "q"))
            evi.gpsimd(pool, queries(d1, "qk"))
            att_own["L2"].gpsimd(pool, queries(d2, "own.k"))
            att_ctx["L2"].gpsimd(pool, queries(d_mid["L2"], "q"))
            att_own["L3"].gpsimd(pool, queries(d_end["L2"], "own.k"))
            att_ctx["L3"].gpsimd(pool, queries(d_mid["L3"], "q"))

        @block.tensor
        def _(pe):
            pe.wait_ge(consts_ready, CONSTS)
            pe.wait_ge(loaded_early, 48)
            d = d0
            pe.wait_ge(loaded_w0, 16)
            pe.wait_ge(d.dve.sem, d.dve.after("silu"))
            for i, (_, name, _, j) in enumerate(MODS):
                last = pe.matmul(d.ps("mods")[:, i * B:(i + 1) * B], w(name, 0, j * D, D), cond_silu[:, :],
                                 start=True, stop=True)
            d.pe.done(last, "mods")
            pe.wait_ge(loaded_x, 16)
            d.ln_pe(pe, "ln", None)
            pe.wait_ge(d.dve.sem, d.dve.after("m.shifted"))
            d.product(pe, "q", [(w("L0_Wq"), xh_t)])
            att0.tensor(pe, lambda eng: eng.wait_ge(d0.dve.sem, d0.dve.after("q")))
            d = d1
            pe.wait_ge(*last_output(att0))
            pe.wait_ge(loaded_w1, 16)
            d.product(pe, "proj", [(w("L0_Wp"), o_t)])
            d.ln_pe(pe, "ln", "x")
            pe.wait_ge(d.dve.sem, d.dve.after("nx"))
            d.product(pe, "q", [(w("L1_Wq"), xh_t)])
            pe.wait_ge(d.dve.sem, d.dve.after("q"))
            d.product(pe, "qk", [(w("L1_WkT"), k_t)])
            evi.tensor(pe, lambda eng: eng.wait_ge(d1.dve.sem, d1.dve.after("qk")))
            d = d2
            pe.wait_ge(*last_output(evi))
            d.product(pe, "ev", [(w("L1_Wv"), o_t)])
            pe.wait_ge(d.dve.sem, d.dve.after("ev"))
            combined = (xh_t, ev_t, anchor_t)
            for e in range(E_N):
                d.product(pe, f"l{e}", [(rw_sb[:, 3 * e + c, :], combined[c]) for c in range(3)])
            d.product(pe, "g1", [(w("L1_gate_w1", c), combined[c]) for c in range(3)])
            pe.wait_ge(d.dve.sem, d.dve.after("gh"))
            d.product(pe, "g2", [(w("L1_gate_w2"), T(8))])
            for e, r in H:
                d.product(pe, f"u{e}{r}", [(w("L1_e_w1", 3 * e + c, r * D, D), combined[c]) for c in range(3)])
            for e in range(E_N):
                pe.wait_ge(d.dve.sem, d.dve.after(f"h{e}1"))
                d.product(pe, f"o{e}", [(w("L1_e_w2", 2 * e + r), hidden[2 * e + r]) for r in range(2)])
            pe.wait_ge(d.dve.sem, d.dve.after("a2"))
            d.product(pe, "out", [(w("L1_out_w"), T(14))])
            own_pe(d, pe, "L2", "x")
            att_own["L2"].tensor(pe, lambda eng: eng.wait_ge(d2.dve.sem, d2.dve.after("own.k")))
            for l in ("L2", "L3"):
                d, nm = d_mid[l], NAMES[l]
                pe.wait_ge(*last_output(att_own[l]))
                d.product(pe, "proj", [(w(nm["proj"]), o_t)])
                d.ln_pe(pe, "ln", "y.x")
                pe.wait_ge(d.dve.sem, d.dve.after("ln.xh"))
                d.product(pe, "q", [(w(nm["q"]), xh_t)])
                att_ctx[l].tensor(pe, lambda eng, d=d: eng.wait_ge(d.dve.sem, d.dve.after("q")))
                d = d_end[l]
                pe.wait_ge(*last_output(att_ctx[l]))
                d.product(pe, "proj", [(w(nm["cproj"]), o_t)])
                d.ln_pe(pe, "ln", "x")
                pe.wait_ge(d.dve.sem, d.dve.after("m.shifted"))
                for j in J4:
                    d.product(pe, f"u{j}", [(w(nm["w1"], 0, j * D, D), xh_t)])
                pe.wait_ge(d.dve.sem, d.dve.after("h3"))
                d.product(pe, "y", [(w(nm["w2"], j), T(8 + j)) for j in J4])
                if l == "L2":
                    own_pe(d, pe, "L3", "y.x")
                    att_own["L3"].tensor(pe, lambda eng, d=d: eng.wait_ge(d.dve.sem, d.dve.after("own.k")))

        @block.scalar
        def _(act):
            d = d0
            act.wait_ge(consts_ready, CONSTS)
            act.wait_ge(loaded_early, 48)
            d.act.done(act.activation(cond_t[:, :], cond_sb[:, :], ACT.Tanh, scale=0.5), "tanh")
            d.ln_act(act, "ln", 0)
            act.wait_ge(d.dve.sem, d.dve.after("scales"))
            att0.scalar(act)
            d1.ln_act(act, "ln", 0)
            evi.scalar(act)
            d = d2
            act.wait_ge(d.dve.sem, d.dve.after("gu"))
            d.act.done(act.activation(T(12), T(8), ACT.Tanh, scale=0.5), "gt")
            for e in range(E_N):
                act.wait_ge(d.dve.sem, d.dve.after(f"d{e}"))
                d.act.done(act.activation(logit[e], logit[e], ACT.Exp), f"p{e}")
            act.wait_ge(d.pe.sem, d.pe.after("g2"))
            d.act.done(act.activation(T(12), d.ps("g2"), ACT.Tanh, scale=0.25, bias=vec("L1_gate_b2", 0, half=True)),
                       "gt2")
            for i, (e, r) in enumerate(H):
                act.wait_ge(d.dve.sem, d.dve.after(f"u{e}{r}"))
                d.act.done(act.activation(curve[i], hidden[i], ACT.Tanh, scale=0.5), f"t{e}{r}")
            d.ln_act(act, "own", 1)
            att_own["L2"].scalar(act)
            for l in ("L2", "L3"):
                d_mid[l].ln_act(act, "ln", 1)
                att_ctx[l].scalar(act)
                d = d_end[l]
                d.ln_act(act, "ln", 1)
                for j in J4:
                    act.wait_ge(d.dve.sem, d.dve.after(f"in{j}"))
                    d.act.done(act.activation(scratch(j), scratch(j), ACT.Tanh, scale=GELU_IN), f"t{j}")
                if l == "L2":
                    d.ln_act(act, "own", 1)
                    att_own["L3"].scalar(act)

        @block.vector
        def _(dve):
            d = d0
            dve.wait_ge(consts_ready, CONSTS)
            dve.wait_ge(loaded_early, 48)
            d.step(dve, dve.tensor_scalar(vec_half[:, :], vec_sb[:, :], 0.5, None, ALU.mult), "half")
            dve.wait_ge(d.act.sem, d.act.after("tanh"))
            d.step(dve, dve.scalar_tensor_tensor(cond_silu[:, :], cond_t[:, :], 1.0, cond_sb[:, :], ALU.add, ALU.mult),
                   "silu")
            dve.wait_ge(d.pe.sem, d.pe.after("mods"))
            d.step(dve, dve.scalar_tensor_tensor(
                mod_sb[:, :, :], d.ps("mods")[:, 0:len(MODS) * B].rearrange("p (m b) -> p m b", b=B), 0.5,
                vec_sb[:, 0:len(MODS)].unsqueeze(2).broadcast_to([D, len(MODS), B]), ALU.mult, ALU.add), "mods")
            d.step(dve, dve.tensor_scalar(mod_sb[:, 0:SCALES, :], mod_sb[:, 0:SCALES, :], 1.0, None, ALU.add), "scales")
            dve.wait_ge(loaded_x, 16)
            d.ln_dve(dve, "ln")
            d.modulate(dve, "L0.scale_q", "L0.shift_q", "m")
            dve.wait_ge(d.pe.sem, d.pe.after("q"))
            d.step(dve, dve.tensor_scalar(q_t, d.ps("q"), vec("L0_bq"), HD ** -0.5, ALU.add, ALU.mult), "q")
            att0.vector(dve)
            d = d1
            dve.wait_ge(d.pe.sem, d.pe.after("proj"))
            d.step(dve, dve.scalar_tensor_tensor(x_t, d.ps("proj"), vec("L0_bp"), x_t, ALU.add, ALU.add), "x")
            d.ln_dve(dve, "ln")
            d.step(dve, dve.tensor_scalar(xh_t, xh_t, vec("L1_ln_gamma"), vec("L1_ln_beta"), ALU.mult, ALU.add), "nx")
            dve.wait_ge(d.pe.sem, d.pe.after("q"))
            d.step(dve, dve.tensor_copy(k_t, d.ps("q")), "q")
            dve.wait_ge(d.pe.sem, d.pe.after("qk"))
            d.step(dve, dve.tensor_scalar(q_t, d.ps("qk"), D ** -0.5, None, ALU.mult), "qk")
            evi.vector(dve)
            d = d2
            at, _ = W_AT["L1_router_W"]
            d.step(dve, dve.tensor_copy(
                rw_sb.rearrange("p (e c) m -> p e c m", e=E_N),
                w_sb[:, at:at + 9].rearrange("p (c e) -> p e c", e=E_N).unsqueeze(3).broadcast_to([D, E_N, 3, D])), "rw")
            d.step(dve, dve.tensor_copy(by_batch(anchor_t), cond_sb[:, :].unsqueeze(2).broadcast_to([D, B, LQ])),
                   "anchor")
            dve.wait_ge(d.pe.sem, d.pe.after("ev"))
            d.step(dve, dve.tensor_copy(ev_t, d.ps("ev")), "ev")
            for e in range(E_N):
                dve.wait_ge(d.pe.sem, d.pe.after(f"l{e}"))
                d.step(dve, dve.tensor_scalar(logit[e], d.ps(f"l{e}"), vec("router_b", e), None, ALU.add), f"l{e}")
            d.step(dve, dve.tensor_tensor(xc_t, logit[0], logit[1], ALU.max), "m01")
            d.step(dve, dve.tensor_tensor(xc_t, xc_t, logit[2], ALU.max), "m")
            for e in range(E_N):
                d.step(dve, dve.tensor_tensor(logit[e], logit[e], xc_t, ALU.subtract), f"d{e}")
            dve.wait_ge(d.pe.sem, d.pe.after("g1"))
            d.step(dve, dve.tensor_scalar(T(8), d.ps("g1"), vec("L1_gate_b1"), None, ALU.add), "gu")
            dve.wait_ge(d.act.sem, d.act.after("gt"))
            d.step(dve, dve.scalar_tensor_tensor(T(8), T(12), 1.0, T(8), ALU.add, ALU.mult), "gh")
            dve.wait_ge(d.act.sem, d.act.after("p2"))
            d.step(dve, dve.tensor_tensor(xc_t, logit[0], logit[1], ALU.add), "s01")
            d.step(dve, dve.tensor_tensor(xc_t, xc_t, logit[2], ALU.add), "s")
            d.step(dve, dve.reciprocal(xc_t, xc_t), "r")
            for e in range(E_N):
                d.step(dve, dve.tensor_tensor(logit[e], logit[e], xc_t, ALU.mult), f"p{e}")
            dve.wait_ge(d.act.sem, d.act.after("gt2"))
            d.step(dve, dve.tensor_scalar(T(12), T(12), 1.0, None, ALU.add), "g")
            for i, (e, r) in enumerate(H):
                dve.wait_ge(d.pe.sem, d.pe.after(f"u{e}{r}"))
                d.step(dve, dve.tensor_scalar(hidden[i], d.ps(f"u{e}{r}"), vec("L1_e_b1", i), None, ALU.add), f"u{e}{r}")
            for i, (e, r) in enumerate(H):
                dve.wait_ge(d.act.sem, d.act.after(f"t{e}{r}"))
                d.step(dve, dve.scalar_tensor_tensor(hidden[i], curve[i], 1.0, hidden[i], ALU.add, ALU.mult), f"h{e}{r}")
            for e in range(E_N):
                dve.wait_ge(d.pe.sem, d.pe.after(f"o{e}"))
                d.step(dve, dve.tensor_scalar(T(8), d.ps(f"o{e}"), 0.5, vec("L1_e_b2", e), ALU.mult, ALU.add), f"o{e}")
                d.step(dve, dve.tensor_tensor(T(14) if e == 0 else T(8), T(8), logit[e], ALU.mult), f"r{e}")
                if e:
                    d.step(dve, dve.tensor_tensor(T(14), T(14), T(8), ALU.add), f"a{e}")
            dve.wait_ge(d.pe.sem, d.pe.after("out"))
            d.step(dve, dve.scalar_tensor_tensor(T(13), d.ps("out"), vec("L1_out_b"), T(12), ALU.add, ALU.mult), "outg")
            d.step(dve, dve.scalar_tensor_tensor(x_t, T(13), 0.5, x_t, ALU.mult, ALU.add), "x")
            own_dve(d, dve, "L2")
            att_own["L2"].vector(dve)
            for l in ("L2", "L3"):
                d, nm = d_mid[l], NAMES[l]
                dve.wait_ge(d.pe.sem, d.pe.after("proj"))
                d.step(dve, dve.tensor_scalar(T(8), d.ps("proj"), vec(nm["proj_b"]), None, ALU.add), "y")
                d.gated(dve, T(8), f"{l}.gate_a", "y")
                d.ln_dve(dve, "ln")
                dve.wait_ge(d.pe.sem, d.pe.after("q"))
                d.step(dve, dve.tensor_scalar(q_t, d.ps("q"), vec(nm["q_b"]), HD ** -0.5, ALU.add, ALU.mult), "q")
                att_ctx[l].vector(dve)
                d = d_end[l]
                dve.wait_ge(d.pe.sem, d.pe.after("proj"))
                d.step(dve, dve.scalar_tensor_tensor(x_t, d.ps("proj"), vec(nm["cproj_b"]), x_t, ALU.add, ALU.add), "x")
                d.ln_dve(dve, "ln")
                d.modulate(dve, f"{l}.scale_m", f"{l}.shift_m", "m")
                for j in J4:
                    u, s = T(8 + j), scratch(j)
                    dve.wait_ge(d.pe.sem, d.pe.after(f"u{j}"))
                    d.step(dve, dve.tensor_scalar(u, d.ps(f"u{j}"), vec(nm["b1"], j), None, ALU.add), f"u{j}")
                    d.step(dve, dve.tensor_tensor(s, u, u, ALU.mult), f"sq{j}")
                    d.step(dve, dve.tensor_scalar(s, s, GELU_CUBE, 1.0, ALU.mult, ALU.add), f"cu{j}")
                    d.step(dve, dve.tensor_tensor(s, s, u, ALU.mult), f"in{j}")
                for j in J4:
                    dve.wait_ge(d.act.sem, d.act.after(f"t{j}"))
                    d.step(dve, dve.scalar_tensor_tensor(T(8 + j), scratch(j), 1.0, T(8 + j), ALU.add, ALU.mult), f"h{j}")
                dve.wait_ge(d.pe.sem, d.pe.after("y"))
                d.step(dve, dve.tensor_scalar(T(12), d.ps("y"), 0.5, vec(nm["b2"]), ALU.mult, ALU.add), "y")
                d.gated(dve, T(12), f"{l}.gate_m", "y")
                if l == "L2":
                    own_dve(d, dve, "L3")
                    att_own["L3"].vector(dve)


def kernel(**inputs):
    import concourse.bacc as bacc
    from concourse.bass_utils import run_bass_kernel_spmd

    a = {}
    for name, value in inputs.items():
        a[name.replace("_xcond", "")] = np.asarray(value)
    nat = a["ctx_1024"].reshape(B, CK, NC, D)
    a["L1_WkT"] = a["L1_Wk"].T
    blocks = [a[name].reshape(n, D, cols).transpose(1, 0, 2).reshape(D, n * cols) for name, n, cols in WEIGHTS]
    columns = [a[bias][j * D:(j + 1) * D][:, None] for _, _, bias, j in MODS]
    columns += [a[name].reshape(n, D).T for name, n in VECTORS]
    columns.append(np.broadcast_to(a["L1_router_b"][None, :], (D, E_N)))
    consts = np.zeros((D, C_COLS), np.float32)
    consts[:, C_ID:C_ID + D] = np.eye(D)
    for p in range(D):
        consts[p, C_HEAD + p // HD] = 1.0
    for p in range(2 * NG):
        consts[p, C_GROUP + p % NG] = 1.0
    arrays = {
        "ctx_nat": nat,
        "ctx_T": nat.transpose(0, 3, 2, 1).reshape(B, D, S),
        "x_T": a["x"].reshape(NT, D).T,
        "cond_T": a["cond_1024"].T,
        "weights": np.concatenate(blocks, axis=1),
        "vectors": np.concatenate(columns, axis=1),
        "consts": consts,
    }
    arrays = {name: np.ascontiguousarray(value) for name, value in arrays.items()}
    nc = bacc.Bacc("TRN2", target_bir_lowering=False, num_devices=1)
    args = [nc.dram_tensor(name, value.shape, F32, kind="ExternalInput").ap() for name, value in arrays.items()]
    out = nc.dram_tensor("out_T", (D, NT), F32, kind="ExternalOutput").ap()
    pixart_program(nc, *args, out)
    r = run_bass_kernel_spmd(nc, [arrays], core_ids=[0])
    return np.ascontiguousarray(r.results[0]["out_T"].T).reshape(B, LQ, D)
```

```python
from contextlib import ExitStack

import concourse.bass as bass
import numpy as np
from concourse import mybir

F32 = mybir.dt.float32
F32R = mybir.dt.float32r
BF16 = mybir.dt.bfloat16
ALU = mybir.AluOpType
ACT = mybir.ActivationFunctionType
AX = mybir.AxisListType

B, LQ, D = 8, 56, 128
S = 1500
NH, HD = 16, 8
NT = B * LQ
NC = 12
CK = S // NC
KB = 500
NJ = S // KB
CJ = KB // CK
HQ = NH * LQ
HALF = HQ // 2
NG = HQ // 128
GROUPS = [(3 * g, 3) for g in range(4)] + [(12, 2), (14, 2)]
PAIRS = NH // 2
SLOTS = [(0, 0), (0, 1), (0, 2), (1, 0), (1, 1), (2, 0)]
SHIFT_ROW = 16 * len(SLOTS)
OW = HD + 1
GW = 32
ONE = 24
MLP = 4 * D
E_N = 3
RING = 3

WEIGHTS = [
    ("L0_Wq", 1, 128), ("L0_Wkv", 1, 256), ("L0_Wp", 1, 128), ("L0_Wss_q", 1, 256), ("L0_Wss_kv", 1, 256),
    ("L2_W_mod", 1, 768), ("L3_adaln_w", 1, 768),
    ("L1_Wq", 1, 128), ("L1_WkT", 1, 128), ("L1_Wv", 1, 128), ("L1_router_W", 3, 3), ("L1_e_w1", 9, 256),
    ("L1_e_w2", 6, 128), ("L1_gate_w1", 3, 128), ("L1_gate_w2", 1, 128), ("L1_out_w", 1, 128),
    ("L2_W_qkv", 1, 384), ("L2_W_proj", 1, 128), ("L2_W_qc", 1, 128), ("L2_W_kvc", 1, 256),
    ("L2_W_cproj", 1, 128), ("L2_W_mlp1", 1, 512), ("L2_W_mlp2", 4, 128),
    ("L3_qkv_w", 1, 384), ("L3_sa_proj_w", 1, 128), ("L3_q_w", 1, 128), ("L3_kv_w", 1, 256),
    ("L3_ca_proj_w", 1, 128), ("L3_fc1_w", 1, 512), ("L3_fc2_w", 4, 128),
]
W_AT, _w = {}, 0
for _name, _blocks, _cols in WEIGHTS:
    if _name == "L3_qkv_w":
        W_L3 = _w
        _w = 0
    W_AT[_name] = (_w + (W_AT["L1_Wq"][0] if _name.startswith("L3") and _name != "L3_adaln_w" else 0), _cols)
    _w += _blocks * _cols
L3_COLS = _w
MODS = [("L0.scale_q", "L0_Wss_q", "L0_bss_q", 0), ("L0.scale_kv", "L0_Wss_kv", "L0_bss_kv", 0),
        ("L2.scale_a", "L2_W_mod", "L2_b_mod", 1), ("L2.scale_m", "L2_W_mod", "L2_b_mod", 4),
        ("L3.scale_a", "L3_adaln_w", "L3_adaln_b", 1), ("L3.scale_m", "L3_adaln_w", "L3_adaln_b", 4),
        ("L0.shift_q", "L0_Wss_q", "L0_bss_q", 1), ("L0.shift_kv", "L0_Wss_kv", "L0_bss_kv", 1),
        ("L2.shift_a", "L2_W_mod", "L2_b_mod", 0), ("L2.gate_a", "L2_W_mod", "L2_b_mod", 2),
        ("L2.shift_m", "L2_W_mod", "L2_b_mod", 3), ("L2.gate_m", "L2_W_mod", "L2_b_mod", 5),
        ("L3.shift_a", "L3_adaln_w", "L3_adaln_b", 0), ("L3.gate_a", "L3_adaln_w", "L3_adaln_b", 2),
        ("L3.shift_m", "L3_adaln_w", "L3_adaln_b", 3), ("L3.gate_m", "L3_adaln_w", "L3_adaln_b", 5)]
SCALES = 6
MOD = {m[0]: n for n, m in enumerate(MODS)}
VECTORS = [
    ("L0_bq", 1), ("L0_bkv", 2), ("L0_bp", 1),
    ("L1_ln_gamma", 1), ("L1_ln_beta", 1), ("L1_e_b1", 6), ("L1_e_b2", 3), ("L1_gate_b1", 1),
    ("L1_gate_b2", 1), ("L1_out_b", 1),
    ("L2_b_qkv", 3), ("L2_b_proj", 1), ("L2_b_qc", 1), ("L2_b_kvc", 2), ("L2_b_cproj", 1), ("L2_b_mlp1", 4),
    ("L2_b_mlp2", 1),
    ("L3_qkv_b", 3), ("L3_sa_proj_b", 1), ("L3_q_b", 1), ("L3_kv_b", 2), ("L3_ca_proj_b", 1), ("L3_fc1_b", 4),
    ("L3_fc2_b", 1),
]
V_AT, _v = {}, len(MODS)
for _name, _cols in VECTORS:
    V_AT[_name] = _v
    _v += _cols
V_AT["router_b"] = _v
V_COLS = _v + E_N
C_ID, C_HEAD = 0, 128
C_COLS = 128 + NH
HEAD_OF = [2 * (p % PAIRS) + p // 64 for p in range(D)]
FEATURE_AT = [HD * HEAD_OF[p] + (p // PAIRS) % HD for p in range(D)]
HEADED = {"L0_Wq": 1, "L0_bq": 1, "L0_Wkv": 1, "L0_bkv": 1, "L2_W_qkv": 2, "L2_b_qkv": 2, "L2_W_qc": 1, "L2_b_qc": 1,
          "L2_W_kvc": 1, "L2_b_kvc": 1, "L3_qkv_w": 2, "L3_qkv_b": 2, "L3_q_w": 1, "L3_q_b": 1, "L3_kv_w": 1,
          "L3_kv_b": 1}
GELU_IN = 0.7978845608028654
GELU_CUBE = 0.044715
K_REPLICA = 16 * len(SLOTS)
Q_REPLICA = 2 * K_REPLICA
CONSTS = 3
BUFFERS = 7


class Ticks:

    def __init__(self, sem, names):
        assert len(set(names)) == len(names), [n for n in names if names.count(n) > 1]
        self.sem, self.names, self.at = sem, names, 0

    def done(self, ins, name):
        assert self.names[self.at] == name, (self.names[self.at], name)
        self.at += 1
        return ins.then_inc(self.sem, 1)

    def after(self, name):
        return self.names.index(name) + 1


class Periods:

    def __init__(self, sem, steps):
        self.sem, self.names, self.leads = sem, [n for n, _ in steps], [d for _, d in steps]
        assert len(set(self.names)) == len(self.names)
        self.at = 0

    def start(self, eng, batches):
        self.has = {d: batches.get(d) is not None for d in (-1, 0, 1)}
        self.at = 0
        if not any(self.has[d] for d in self.leads):
            if self.has[1]:
                eng.sem_inc(self.sem, len(self.names))
            else:
                self.at = len(self.names)

    def done(self, ins, name):
        i = self.names.index(name)
        assert i >= self.at, name
        step = i + 1 - self.at
        assert self.has[self.leads[i]] and not any(self.has[d] for d in self.leads[self.at:i]), name
        self.at = i + 1
        if not any(self.has[d] for d in self.leads[i + 1:]):
            step += len(self.names) - i - 1
            self.at = len(self.names)
        return ins.then_inc(self.sem, step)

    def end(self):
        assert self.at in (0, len(self.names)), (self.at, self.names)

    def place(self, name, d):
        i = self.names.index(name)
        return (d + 1 - self.leads[i]) * len(self.names) + i + 1

    def after(self, name, n):
        return n * len(self.names) + self.place(name, 0)


def wait_steps(eng, n, *steps):
    last = {}
    for plan, name, d in steps:
        last[plan] = max(last.get(plan, -9999), plan.place(name, d))
    for plan, at in last.items():
        eng.wait_ge(plan.sem, n * len(plan.names) + at)


def periods(eng, body):
    body(None, (0, 0, 0))
    with eng.Fori(0, (B - 2) // 2) as j:
        body((2 * j, 0, j), (2 * j + 1, 1, j))
        body((2 * j + 1, 1, j), (2 * j + 2, 0, j + 1))
    body((B - 2, 0, (B - 2) // 2), (B - 1, 1, (B - 2) // 2))
    body((B - 1, 1, (B - 2) // 2), None)


def later_periods(eng, body):
    body(None, (0, 0, 0), (1, 1, 0))
    with eng.Fori(0, (B - 2) // 2) as j:
        body((2 * j, 0, j), (2 * j + 1, 1, j), (2 * j + 2, 0, j + 1))
        body((2 * j + 1, 1, j), (2 * j + 2, 0, j + 1), (2 * j + 3, 1, j + 1))
    body((B - 2, 0, (B - 2) // 2), (B - 1, 1, (B - 2) // 2), None)
    body((B - 1, 1, (B - 2) // 2), None, None)


def pixart_program(nc, ctx_nat, ctx_T, x_T, cond_T, weights, vectors, consts, out):
    ctx = ExitStack()
    with ctx:
        def sb(name, shape, dt=F32):
            return ctx.enter_context(nc.sbuf_tensor(name, shape, dt))

        def pb(name, shape):
            return ctx.enter_context(nc.psum_tensor(name, shape, F32))

        def sem(name):
            return ctx.enter_context(nc.semaphore(name))

        w_sb = sb("w_sb", [D, W_L3])
        vec_sb = sb("vec_sb", [D, V_COLS])
        vec_half = sb("vec_half", [D, V_COLS])
        const_sb = sb("const_sb", [D, C_COLS])
        cond_sb = sb("cond_sb", [D, B])
        cond_t = sb("cond_t", [D, B])
        cond_silu = sb("cond_silu", [D, B])
        mod_sb = sb("mod_sb", [D, len(MODS), B])
        mean_mat = sb("mean_mat", [D, D])
        nat_sb = sb("nat_sb", [CK, 2, NC, D])
        ctx_mv = sb("ctx_mv", [CK, B, NC, 2])
        mv_now = sb("mv_now", [CK, NC, 2])
        bn_tmp = sb("bn_tmp", [CK, NC, 6])
        norm_all = sb("norm_all", [CK, B, 2, NC])
        norm_now = sb("norm_now", [CK, 2, NC])
        hat_sb = sb("hat_sb", [CK, NC, D])
        ctxT_sb = sb("ctxT_sb", [D, S])
        key_sb = sb("key_sb", [D, S])
        keyr_sb = sb("keyr_sb", [D, S], F32R)
        part_sb = sb("part_sb", [D, 3, S], BF16)
        qpart_sb = sb("qpart_sb", [D, 3, NT], BF16)
        kstack = sb("kstack", [D, 2, PAIRS, S], BF16)
        qstack_flat = sb("qstack", [D, 2 * PAIRS * NT + 8], BF16)
        qstack = qstack_flat[:, 0:2 * PAIRS * NT].rearrange("r (e p k) -> r e p k", e=2, p=PAIRS)
        own_val = sb("own_val", [LQ, B, NH, OW])
        own_max = sb("own_max", [D, PAIRS, B])
        own_maxb = sb("own_maxb", [D, PAIRS, B], BF16)
        own_maxparts = sb("own_maxparts", [D, 2, PAIRS, B])
        own_shift = sb("own_shift", [D, 2, 64], BF16)
        own_rec = sb("own_rec", [LQ, 2, NH])
        own_out = sb("own_out", [LQ, 2, D])
        val_sb = sb("val_sb", [CK, 2, NC, len(GROUPS) * GW])
        qblkr = sb("qblkr", [D, 2, HQ], F32R)
        prob_sb = sb("prob_sb", [D, 2, HQ])
        max_sb = sb("max_sb", [D, NG, NJ])
        max1 = sb("max1", [D, NG])
        maxb = sb("maxb", [D, NG], BF16)
        maxparts = sb("maxparts", [D, NG, 2])
        o_sb = sb("o_sb", [D, 5 * LQ])
        osum_r = sb("osum_r", [LQ, NH])
        on_sb = sb("on_sb", [LQ, D])
        xslice = sb("xslice", [D, 2, LQ])
        tok = sb("tok", [D, 11, NT])
        s_max = sb("s_max", [LQ, 2, 1])
        s_sum = sb("s_sum", [LQ, 2, 1])
        s_rec = sb("s_rec", [LQ, 1])

        score_ps = pb("score_ps", [D, 2, 2, 512])
        oacc_ps = pb("oacc_ps", [D, 512])
        ring_ps = pb("ring_ps", [D, RING, 512])

        def w(name, block=0, lo=0, n=None):
            at, cols = W_AT[name]
            at += block * cols + lo
            return w_sb[:, at:at + (n or cols - lo)]

        def vec(name, j=0, half=False):
            at = V_AT[name] + j
            return (vec_half if half else vec_sb)[:, at:at + 1]

        def T(i):
            if i < 11:
                return tok[:, i, :]
            flat = part_sb[:, :, :].rearrange("p a k -> p (a k)").bitcast(F32)
            return flat[:, (i - 11) * NT:(i - 10) * NT]

        def scratch(i):
            return (key_sb[:, :] if i < 3 else prob_flat)[:, (i % 3) * NT:(i % 3 + 1) * NT]

        prob_flat = prob_sb[:, :, :].rearrange("p a k -> p (a k)")
        kpart_sb = prob_flat[:, 0:3 * NT // 2].bitcast(BF16).rearrange("p (a k) -> p a k", a=3)

        def by_batch(ap):
            return ap.rearrange("p (b q) -> p b q", q=LQ)

        def mod(name):
            return mod_sb[:, MOD[name], :].unsqueeze(2).broadcast_to([D, B, LQ])

        ident = const_sb[:, C_ID:C_ID + 128]
        x_t, xc_t, xh_t, q_t, k_t, o_t = (T(i) for i in range(6))

        eps_sb = sb("eps_sb", [D, 2])
        consts_ready = sem("constants_ready")
        settled = sem("settled")
        ev_t, anchor_t = T(6), T(7)
        rw_sb = ctxT_sb[:, 0:9 * D].rearrange("p (e m) -> p e m", m=D)
        logit = (q_t, k_t, o_t)
        hidden = [T(9), T(10), T(11), T(13), scratch(0), scratch(1)]
        curve = [T(8), T(14), scratch(2), scratch(3), scratch(4), scratch(5)]

        def settle(eng):
            eng.sem_inc(settled, 1)

        def stack_queries(sp, ready, stacked):
            for part in range(3):
                ready(sp, part)
                for slot, (_, qpart) in enumerate(SLOTS):
                    if qpart == part:
                        for e in range(2):
                            r0 = 16 * slot + 8 * e
                            sp.dma_start(qstack[r0:r0 + 8, e, :, :], qpart_sb[64 * e:64 * e + 64, part, :])\
                                .then_inc(stacked, 16)

        def stack_keys(sp, src, part, u, cols, stacked):
            for slot, (kpart, _) in enumerate(SLOTS):
                if kpart == part:
                    sp.dma_start(kstack[16 * slot:16 * slot + 16, u, :, cols], src[:, part, cols])\
                        .then_inc(stacked, 16)

        class Heads:
            def __init__(self, tag, wkey, wval, bkey, bval, hat, modulated=False):
                self.tag, self.wkey, self.wval, self.bkey, self.bval = tag, wkey, wval, bkey, bval
                self.hat, self.modulated = hat, modulated
                J = range(NJ)
                mm = [f"M{j}.{g}" for j in J for g in range(NG)]
                self.mm = mm
                T3 = [f"T{j}" for j in J] if hat else []
                beside = {1: ["OT"], 3: ["OTT"] + T3, 4: ["K0"], 5: mm[0:3], 6: ["K1"] + mm[3:6], 7: mm[6:9],
                          8: ["K2"] + mm[9:12], 9: mm[12:15], 10: mm[15:18], 11: mm[18:21]}
                pe = []
                for c in range(NC):
                    pe += [f"S{c}", *beside.get(c, [])]
                    if c:
                        pe.append(f"PV{c - 1}")
                pe += [f"PV{NC - 1}", "V0", "MTa", "MTb", "V1", "V2"]
                act = ["E0", "E1", "E2", "E3", *T3, "E4", "kr0", "k0.0", "K0", "E5", "E6", "kr1", "k0.1", "K1", "E7",
                       "E8", "kr2", "k0.2", "K2", "E9", "E10", "E11", "V0", "shift1", "V1", "V2"]
                dve = ["O", *(["norm", "hatA"] if hat else []), "sum0", "sum1", "norm0", "norm1",
                       *(["hatB"] if hat else []), "OTT", *mm, "maxall", "maxb", "part0", "part1", "shift0"]
                pool = ["qr", *[f"{s}{j}" for j in J for s in ("rest", "k1.", "k2.")]]
                LEAD = {"S": 0, "P": 0, "E": 0, "O": -1, "s": -1, "n": -1}

                def lead(n):
                    return 1 if n in ("norm", "shift0", "shift1") else LEAD.get(n[0], 1)

                self.lead = lead
                self.orders = {"pe": pe, "act": act, "dve": dve, "pool": pool}
                of_context = {"pe": "TKV", "act": "TkKV", "dve": ("norm", "hatA", "hatB"), "pool": "rk"}

                def context(eng, n):
                    mine = of_context[eng]
                    return n in mine if isinstance(mine, tuple) else n[0] in mine

                self.context = context
                self.plans = {}
                for eng, order in self.orders.items():
                    for which in (False, True):
                        steps = [(n, lead(n)) for n in order if context(eng, n) == which]
                        kind = "context" if which else "attention"
                        self.plans[eng, which] = Periods(sem(f"{tag}_{eng}_{kind}_done"), steps) if steps else None
                self.loaded = sem(f"{tag}_contextT_loaded") if not hat else None
                self.nat_loaded = [sem(f"{tag}_context_loaded{u}") for u in range(2)] if hat else None
                self.stacked = [sem(f"{tag}_keys_stacked{u}") for u in range(2)]
                self.qstacked = sem(f"{tag}_queries_stacked")
                self.reader = {}
                for j in J:
                    self.reader |= {f"T{j}": ("act", f"T{j}"), f"K{j}": ("act", f"K{j}"), f"V{j}": ("act", f"V{j}")}
                for m in mm:
                    self.reader[m] = ("dve", m)
                self.reader |= {"MTa": ("dve", "shift0"), "MTb": ("act", "shift1"), "OT": ("dve", "norm1"),
                                "OTT": ("dve", "OTT")}
                uses = [n for n in pe if n in self.reader]
                self.bank = {n: i % RING for i, n in enumerate(uses)}
                self.users = {}

            def at(self, eng, name, d=0):
                return self.plans[eng, self.context(eng, name)], name, d

            def after(self, eng, name, n):
                plan = self.at(eng, name)[0]
                return plan.sem, plan.after(name, n)

            def done(self, eng, ins, name):
                self.at(eng, name)[0].done(ins, name)

            def ring_read(self, name):
                bank, lead = self.bank[name], self.lead(name)
                last = self.users.get(bank)
                self.users[bank] = (name, lead)
                if last is None:
                    return []
                return [self.at(*self.reader[last[0]], last[1] - lead)]

            def run(self, which, eng, engine, emit, prev, cur, nxt):
                batches = {-1: prev, 0: cur, 1: nxt}
                plans = [self.plans[eng, c] for c in (False, True) if which is None or c == (which == "context")]
                plans = [p for p in plans if p]
                for plan in plans:
                    plan.start(engine, batches)
                if eng == "pe":
                    if which == "context":
                        self.users = {}
                    elif which is None:
                        self.users = {b: (n, d - 1) for b, (n, d) in self.users.items()}
                for name in self.orders[eng]:
                    if self.at(eng, name)[0] in plans and batches[self.lead(name)]:
                        emit(name, batches[self.lead(name)], prev, cur, nxt)
                for plan in plans:
                    plan.end()

            def pe_step(self, pe):
                def emit(name, batch, prev, cur, nxt):
                    n, u, half = batch
                    free = self.ring_read(name) if name in self.bank else []
                    ps = ring_ps[:, self.bank[name], :] if name in self.bank else None
                    if name[0] == "T":
                        wait_steps(pe, n, *([self.at("dve", "hatB")] if name == "T0" else []), *free)
                        j = int(name[1:])
                        for c in range(CJ):
                            last = pe.transpose(ps[:, c * CK:(c + 1) * CK], hat_sb[:, j * CJ + c, :],
                                                ident[0:CK, 0:CK])
                    elif name[0] == "K":
                        j = int(name[1:])
                        if self.loaded and j == 0:
                            pe.wait_ge(self.loaded, 16 * (n + 1))
                        wait_steps(pe, n, *([self.at("act", f"T{j}")] if self.hat else []), *free)
                        last = pe.matmul(ps[:, 0:KB], self.wkey, ctxT_sb[:, j * KB:(j + 1) * KB],
                                         start=True, stop=True)
                    elif name[0] == "V":
                        j = int(name[1:])
                        wait_steps(pe, n, *free)
                        for c in range(CJ):
                            k0 = (j * CJ + c) * CK
                            last = pe.matmul(ps[0:CK, c * D:(c + 1) * D], ctxT_sb[:, k0:k0 + CK], self.wval,
                                             start=True, stop=True)
                    elif name[0:2] == "MT":
                        wait_steps(pe, n, self.at("dve", "part1"), *free)
                        for i in range(4):
                            last = pe.transpose(ps[0:2, i * D:(i + 1) * D], maxparts[:, i + (3 if name == "MTb" else 0), :],
                                                ident)
                    elif name[0] == "M":
                        j, g = (int(t) for t in name[1:].split("."))
                        wait_steps(pe, n, *([self.at("act", f"kr{j}"), self.at("pool", "qr")] if g == 0 else []),
                                   *free)
                        last = pe.matmul(ps[:, 0:KB], qblkr[:, u, g * 128:(g + 1) * 128],
                                         keyr_sb[:, j * KB:(j + 1) * KB], start=True, stop=True)
                    elif name[0] == "S":
                        c = int(name[1:])
                        need = [self.at("dve", "shift0"), self.at("act", "shift1")] if c == 0 else []
                        if c >= 2:
                            need.append(self.at("act", f"E{c - 2}"))
                        elif prev:
                            need.append(self.at("act", f"E{NC - 2 + c}", -1))
                        wait_steps(pe, n, *need)
                        if c == 0:
                            pe.wait_ge(self.stacked[u], K_REPLICA * (half + 1))
                            pe.wait_ge(self.qstacked, Q_REPLICA)
                        for p in range(PAIRS):
                            at = (p % 4) * 2 * LQ
                            last = pe.matmul(score_ps[0:CK, c % 2, p // 4, at:at + 2 * LQ],
                                             kstack[:, u, p, c * CK:(c + 1) * CK],
                                             qstack[:, :, p, bass.ds(n * LQ, LQ)], start=True, stop=True)
                    elif name[0] == "P":
                        c = int(name[2:])
                        wait_steps(pe, n, self.at("act", f"E{c}"), *([self.at("act", "V2")] if c == 0 else []),
                                   *([self.at("dve", "O", -1)] if c == 0 and prev else []))
                        for g, (h0, nh) in enumerate(GROUPS):
                            q = g % 4
                            at = 0 if g < 4 else 3 * LQ
                            last = pe.matmul(oacc_ps[q * GW:(q + 1) * GW, at:at + nh * LQ],
                                             val_sb[0:CK, u, c, g * GW:(g + 1) * GW],
                                             prob_sb[0:CK, c % 2, h0 * LQ:(h0 + nh) * LQ],
                                             start=(c == 0 and g < 4), stop=(c == NC - 1), skip_group_check=True)
                    elif name == "OT":
                        wait_steps(pe, n, self.at("dve", "O"), *free)
                        settle(pe)
                        for i in range(5):
                            rows = D if i < 3 else 64
                            at = 128 * i if i < 3 else 384 + 64 * (i - 3)
                            last = pe.transpose(ps[0:LQ, at:at + rows], o_sb[0:rows, i * LQ:(i + 1) * LQ],
                                                ident[0:rows, 0:rows])
                    elif name == "OTT":
                        wait_steps(pe, n, self.at("dve", "norm1"), *free)
                        settle(pe)
                        last = pe.transpose(ps[:, 0:LQ], on_sb[:, :], ident[0:LQ, 0:LQ])
                    self.done("pe", last, name)
                return emit

            def act_step(self, act):
                def emit(name, batch, prev, cur, nxt):
                    n, u, half = batch
                    ps = ring_ps[:, self.bank[name], :] if name in self.bank else None
                    if name[0] == "T":
                        j = int(name[1:])
                        act.wait_ge(*self.after("pe", name, n))
                        settle(act)
                        src, dst = ps[:, 0:KB], ctxT_sb[:, j * KB:(j + 1) * KB]
                        if self.modulated:
                            ins = act.activation(dst, src, ACT.Identity,
                                                 bias=mod_sb[:, MOD["L0.shift_kv"], bass.ds(n, 1)],
                                                 scale=mod_sb[:, MOD["L0.scale_kv"], bass.ds(n, 1)])
                        else:
                            ins = act.copy(dst, src)
                    elif name[0] in "kK":
                        j = int(name[-1])
                        cols, src = slice(j * KB, (j + 1) * KB), ring_ps[:, self.bank[f"K{j}"], 0:KB]
                        if name[0:2] == "kr":
                            act.wait_ge(*self.after("pe", f"K{j}", n))
                            dst = keyr_sb[:, cols]
                        elif name[0:2] == "k0":
                            if j == 0 and cur:
                                act.wait_ge(self.stacked[1 - u], K_REPLICA * (half + 1 if u else half))
                                wait_steps(act, n, self.at("pool", f"k2.{NJ - 1}", -1))
                            dst = part_sb[:, 0, cols]
                        else:
                            dst = key_sb[:, cols]
                        ins = act.activation(dst, src, ACT.Identity, bias=self.bkey)
                    elif name[0] == "V":
                        j = int(name[1:])
                        act.wait_ge(*self.after("pe", name, n))
                        src = ps[0:CK, :].rearrange("p (c k) -> p c k", c=CJ)
                        dst = val_sb[0:CK, u, j * CJ:(j + 1) * CJ, :].rearrange("p c (g k) -> p c g k", k=GW)
                        act.copy(dst[:, :, 0:4, 0:24], src[:, :, 0:96].rearrange("p c (g k) -> p c g k", k=24))
                        ins = act.copy(dst[:, :, 4:6, 0:16], src[:, :, 96:128].rearrange("p c (g k) -> p c g k", k=16))
                    elif name[0] == "E":
                        c = int(name[1:])
                        need = [self.at("pe", f"S{c}")]
                        if c < 2 and prev:
                            need.append(self.at("pe", f"PV{NC - 2 + c}", -1))
                        elif c >= 2:
                            need.append(self.at("pe", f"PV{c - 2}"))
                        wait_steps(act, n, *need)
                        dst = prob_sb[0:CK, c % 2, :].rearrange("p (h q) -> p h q", h=2)
                        ins = act.activation(dst, score_ps[0:CK, c % 2, :, 0:HALF], ACT.Exp)
                    else:
                        act.wait_ge(*self.after("pe", "MTb", n))
                        settle(act)
                        ins = act.copy(*self.shift(1, n))
                    self.done("act", ins, name)
                return emit

            def shift(self, half, n):
                rows = ring_ps[0:2, self.bank[("MTa", "MTb")[half]], :][:, (0, 64)[half]:(0, 64)[half] + HALF]
                return (qstack[SHIFT_ROW:SHIFT_ROW + 2, :, 4 * half:4 * half + 4, bass.ds(n * LQ, LQ)]
                        .rearrange("r e p q -> r p e q"), rows.rearrange("r (p e q) -> r p e q", e=2, q=LQ))

            def dve_step(self, dve):
                def view(base, off, dims):
                    return bass.AP(tensor=base.tensor, offset=base.offset + off, ap=[list(base.ap[0])] + dims)

                def emit(name, batch, prev, cur, nxt):
                    n, u, half = batch
                    ps_ot = ring_ps[0:LQ, self.bank["OT"], :]
                    if name == "norm":
                        ins = dve.tensor_copy(norm_now[:, :, :], norm_all[:, n, :, :])
                    elif name[0:3] == "hat":
                        if name == "hatA":
                            dve.wait_ge(*self.after("dve", "norm", n))
                            dve.wait_ge(self.nat_loaded[u], 16 * (half + 1))
                            if cur:
                                dve.wait_ge(*self.after("pe", f"T{NJ - 1}", n - 1))
                        for c in (range(6) if name == "hatA" else range(6, NC)):
                            ins = dve.tensor_scalar(hat_sb[:, c, :], nat_sb[:, u, c, :], norm_now[:, 0, c:c + 1],
                                                    norm_now[:, 1, c:c + 1], ALU.add, ALU.mult)
                    elif name[0] == "M":
                        j, g = (int(t) for t in name[1:].split("."))
                        dve.wait_ge(*self.after("pe", name, n))
                        ins = dve.tensor_reduce(max_sb[:, g, j:j + 1], ring_ps[:, self.bank[name], 0:KB], AX.X, ALU.max)
                    elif name == "maxall":
                        dve.wait_ge(*self.after("dve", self.mm[-1], n))
                        ins = dve.tensor_reduce(max1[:, :], max_sb[:, :, :], AX.X, ALU.max)
                    elif name == "maxb":
                        dve.wait_ge(*self.after("dve", "maxall", n))
                        ins = dve.tensor_scalar(maxb[:, :], max1[:, :], -1.0, None, ALU.mult)
                    elif name == "part0":
                        dve.wait_ge(*self.after("dve", "maxb", n))
                        ins = dve.tensor_copy(maxparts[:, :, 0], maxb[:, :])
                    elif name == "part1":
                        ins = dve.scalar_tensor_tensor(maxparts[:, :, 1], max1[:, :], -1.0, maxb[:, :],
                                                       ALU.mult, ALU.subtract)
                    elif name == "shift0":
                        dve.wait_ge(*self.after("pe", "MTa", n))
                        ins = dve.tensor_copy(*self.shift(0, n))
                    elif name == "O":
                        dve.wait_ge(*self.after("pe", f"PV{NC - 1}", n))
                        dve.tensor_copy(o_sb[:, 0:3 * LQ], oacc_ps[:, 0:3 * LQ])
                        ins = dve.tensor_copy(o_sb[0:64, 3 * LQ:5 * LQ], oacc_ps[0:64, 3 * LQ:5 * LQ])
                    elif name == "sum0":
                        dve.wait_ge(*self.after("pe", "OT", n))
                        ins = dve.reciprocal(view(osum_r[:, :], 0, [[1, 3], [3, 4]]),
                                             view(ps_ot, ONE, [[128, 3], [GW, 4]]))
                    elif name == "sum1":
                        ins = dve.reciprocal(view(osum_r[:, :], 12, [[1, 2], [2, 2]]),
                                             view(ps_ot, 384 + ONE, [[64, 2], [GW, 2]]))
                    elif name == "norm0":
                        dve.wait_ge(*self.after("dve", "sum1", n))
                        ins = dve.tensor_tensor(view(on_sb[:, :], 0, [[8, 3], [24, 4], [1, 8]]),
                                                view(ps_ot, 0, [[136, 3], [GW, 4], [1, 8]]),
                                                view(osum_r[:, :], 0, [[1, 3], [3, 4], [0, 8]]), ALU.mult)
                    elif name == "norm1":
                        ins = dve.tensor_tensor(view(on_sb[:, :], 96, [[8, 2], [16, 2], [1, 8]]),
                                                view(ps_ot, 384, [[72, 2], [GW, 2], [1, 8]]),
                                                view(osum_r[:, :], 12, [[1, 2], [2, 2], [0, 8]]), ALU.mult)
                    elif name == "OTT":
                        dve.wait_ge(*self.after("pe", "OTT", n))
                        ins = dve.tensor_scalar(by_batch(o_t)[:, n, :], ring_ps[:, self.bank["OTT"], 0:LQ], self.bval,
                                                None, ALU.add)
                    self.done("dve", ins, name)
                return emit

            def pool_step(self, pool):
                def emit(name, batch, prev, cur, nxt):
                    n, u, half = batch
                    if name == "qr":
                        if cur:
                            pool.wait_ge(*self.after("pe", self.mm[-1], cur[0]))
                        q3 = qblkr[:, u, :].rearrange("p (h q) -> p h q", h=NH)
                        ins = pool.tensor_tensor(q3, by_batch(q_t)[:, n, :].unsqueeze(1).broadcast_to([D, NH, LQ]),
                                                 const_sb[:, C_HEAD:C_HEAD + NH].unsqueeze(2)
                                                 .broadcast_to([D, NH, LQ]), ALU.mult)
                    else:
                        j = int(name[-1])
                        cols = slice(j * KB, (j + 1) * KB)
                        rest = key_sb[:, cols]
                        if name[0] == "r":
                            pool.wait_ge(*self.after("act", f"K{j}", n))
                            ins = pool.tensor_tensor(rest, rest, part_sb[:, 0, cols], ALU.subtract)
                        elif name[1] == "1":
                            pool.wait_ge(*self.after("pool", f"rest{j}", n))
                            settle(pool)
                            ins = pool.tensor_copy(part_sb[:, 1, cols], rest)
                        else:
                            pool.wait_ge(*self.after("pool", f"k1.{j}", n))
                            ins = pool.tensor_tensor(part_sb[:, 2, cols], rest, part_sb[:, 1, cols], ALU.subtract)
                    self.done("pool", ins, name)
                return emit

            def emitter(self, eng):
                return {"pe": self.pe_step, "act": self.act_step, "dve": self.dve_step, "pool": self.pool_step}[eng]

            def first_context(self, eng, engine):
                self.run("context", eng, engine, self.emitter(eng)(engine), None, None, (0, 0, 0))

            def first_queries(self, eng, engine):
                self.run("queries", eng, engine, self.emitter(eng)(engine), None, None, (0, 0, 0))

            def later(self, eng, engine):
                emit = self.emitter(eng)(engine)
                later_periods(engine, lambda prev, cur, nxt: self.run(None, eng, engine, emit, prev, cur, nxt))

            def load_nat(self, sp, n, u):
                sp.dma_start(nat_sb[:, u, :, :], ctx_nat[n]).then_inc(self.nat_loaded[u], 16)

            def sync_batch(self, sp, cur, nxt):
                n, u, half = nxt
                last = isinstance(n, int) and n == B - 1
                if self.hat and cur and not last:
                    sp.wait_ge(*self.after("dve", "hatB", cur[0]))
                    self.load_nat(sp, n + 1, 1 - u)
                if cur:
                    sp.wait_ge(*self.after("pe", f"S{NC - 1}", cur[0] - 1))
                sp.wait_ge(*self.after("act", f"k0.{NJ - 1}", n))
                stack_keys(sp, part_sb, 0, u, slice(0, S), self.stacked[u])
                sp.wait_ge(*self.after("pool", f"k1.{NJ - 1}", n))
                stack_keys(sp, part_sb, 1, u, slice(0, S), self.stacked[u])
                sp.wait_ge(*self.after("pool", f"k2.{NJ - 1}", n))
                stack_keys(sp, part_sb, 2, u, slice(0, S), self.stacked[u])
                if not self.hat and not last:
                    sp.wait_ge(*self.after("pe", f"V{NJ - 1}", n))
                    sp.dma_start(ctxT_sb[:, :], ctx_T[n + 1]).then_inc(self.loaded, 16)

            def sync_load(self, sp):
                if self.hat:
                    self.load_nat(sp, 0, 0)
                    self.load_nat(sp, 1, 1)
                else:
                    sp.dma_start(ctxT_sb[:, :], ctx_T[0]).then_inc(self.loaded, 16)

            def sync_later(self, sp):
                self.sync_batch(sp, (0, 0, 0), (1, 1, 0))
                with sp.Fori(0, (B - 4) // 2) as j:
                    self.sync_batch(sp, (2 * j + 1, 1, j), (2 * j + 2, 0, j + 1))
                    self.sync_batch(sp, (2 * j + 2, 0, j + 1), (2 * j + 3, 1, j + 1))
                self.sync_batch(sp, (B - 3, 1, B // 2 - 2), (B - 2, 0, B // 2 - 1))
                self.sync_batch(sp, (B - 2, 0, B // 2 - 1), (B - 1, 1, B // 2 - 1))

        class Own:
            def __init__(self, tag, wval, bval):
                self.wval, self.bval = wval, bval
                names = ("values_made", "values_in", "max_scores", "maxima", "max_parts", "shifts_turned", "shifts_in",
                         "scores", "probs", "attended", "sums", "normed", "turned", "finished", "rows_clear",
                         "shifts_placed", "queries_stacked", "keys_stacked")
                self.s = {n: sem(f"{tag}_{n}") for n in names}

            def tensor(self, pe, x_ready):
                s = self.s
                x_ready(pe)
                for b in range(B):
                    last = pe.matmul(score_ps[0:LQ, 0, b // 4, (b % 4) * D:(b % 4 + 1) * D], by_batch(xh_t)[:, b, :],
                                     self.wval, start=True, stop=True)
                last.then_inc(s["values_made"], 1)
                pe.wait_ge(s["values_in"], 2)
                pe.wait_ge(s["rows_clear"], 1)
                pe.wait_ge(s["queries_stacked"], Q_REPLICA)
                pe.wait_ge(s["keys_stacked"], K_REPLICA)
                for k in range(B // 2):
                    pe.wait_ge(s["maxima"], k + 1)
                    for i in range(2):
                        n = 2 * k + i
                        for p in range(PAIRS):
                            for e in range(2):
                                q0 = (e * PAIRS + p) * NT + n * LQ
                                last = pe.matmul(score_ps[64 * e:64 * e + 64, k % 2, i, p * LQ:(p + 1) * LQ],
                                                 qstack_flat[:, q0:q0 + 64], kstack[:, 1, p, n * LQ:(n + 1) * LQ],
                                                 start=True, stop=True)
                    last.then_inc(s["max_scores"], 1)
                pe.wait_ge(s["max_parts"], 1)
                pe.transpose(ring_ps[:, 0, 0:D], own_maxparts[:, :, :, :].rearrange("r t p b -> r (t p b)"), ident)\
                    .then_inc(s["shifts_turned"], 1)

                def scores(n, r):
                    for p in range(PAIRS):
                        at = (p % 4) * 2 * LQ
                        last = pe.matmul(score_ps[:, r, p // 4, at:at + 2 * LQ], kstack[:, 1, p, n * LQ:n * LQ + D],
                                         qstack[:, :, p, n * LQ:(n + 1) * LQ], start=True, stop=True)
                    last.then_inc(s["scores"], 1)

                def pair(i, more):
                    pe.wait_ge(s["normed"], i + 1)
                    for r in range(2):
                        pe.wait_ge(s["probs"], 2 * i + r + 1)
                        for h in range(NH):
                            last = pe.matmul(oacc_ps[0:LQ, (r * NH + h) * OW:(r * NH + h + 1) * OW],
                                             prob_sb[0:LQ, r, h * LQ:(h + 1) * LQ], own_val[:, 2 * i + r, h, :],
                                             start=True, stop=True)
                        last.then_inc(s["attended"], 1)
                    if more:
                        for r in range(2):
                            scores(2 * i + 2 + r, r)
                    pe.wait_ge(s["normed"], i + 2)
                    pe.wait_ge(s["finished"], i + 1)
                    for r in range(2):
                        last = pe.transpose(ring_ps[:, 1, r * LQ:(r + 1) * LQ], own_out[:, r, :], ident[0:LQ, 0:LQ])
                    last.then_inc(s["turned"], 1)

                pe.wait_ge(s["shifts_placed"], 32)
                for r in range(2):
                    scores(r, r)
                for i in range(B // 2):
                    pair(i, i < B // 2 - 1)

            def scalar(self, act):
                s = self.s
                act.wait_ge(s["values_made"], 1)
                for i in range(2):
                    act.copy(own_val[:, 4 * i:4 * i + 4, :, 0:HD],
                             score_ps[0:LQ, 0, i, :].rearrange("p (b h k) -> p b h k", b=4, k=HD))\
                        .then_inc(s["values_in"], 1)
                act.wait_ge(s["shifts_turned"], 1)
                act.copy(own_shift[:, :, :], ring_ps[:, 0, 0:D].rearrange("p (e q) -> p e q", e=2))\
                    .then_inc(s["shifts_in"], 1)
                with act.Fori(0, B // 2) as i:
                    for r in range(2):
                        act.wait_ge(s["scores"], 2 * i + r + 1)
                        act.wait_ge(s["attended"], 2 * i + r + 1)
                        act.activation(prob_sb[0:LQ, r, :].rearrange("p (h q) -> p h q", h=2),
                                       score_ps[0:LQ, r, :, 0:HALF], ACT.Exp).then_inc(s["probs"], 1)

            def vector(self, dve):
                s = self.s
                for k in range(B // 2):
                    dve.wait_ge(s["max_scores"], k + 1)
                    dve.tensor_reduce(own_max[:, :, 2 * k:2 * k + 2].rearrange("r p b -> r b p"),
                                      score_ps[:, k % 2, :, 0:HALF].rearrange("r b (p k) -> r b p k", k=LQ),
                                      AX.X, ALU.max).then_inc(s["maxima"], 1)
                dve.wait_ge(s["maxima"], B // 2 + 2)
                dve.tensor_scalar(own_maxb[:, :, :], own_max[:, :, :], -1.0, None, ALU.mult).then_inc(s["maxima"], 1)
                dve.wait_ge(s["maxima"], B // 2 + 3)
                dve.tensor_copy(own_maxparts[:, 0, :, :], own_maxb[:, :, :])
                dve.scalar_tensor_tensor(own_maxparts[:, 1, :, :], own_max[:, :, :], -1.0, own_maxb[:, :, :], ALU.mult,
                                         ALU.subtract).then_inc(s["max_parts"], 1)
                with dve.Fori(0, B // 2) as i:
                    dve.wait_ge(s["attended"], 2 * i + 4)
                    ps = oacc_ps[0:LQ, 0:2 * NH * OW].rearrange("q (r h k) -> q r h k", r=2, k=OW)
                    dve.reciprocal(own_rec[:, :, :], ps[:, :, :, HD]).then_inc(s["sums"], 1)
                    dve.wait_ge(s["sums"], i + 1)
                    dve.tensor_tensor(own_out[:, :, :].rearrange("q r (h k) -> q r h k", k=HD), ps[:, :, :, 0:HD],
                                      own_rec[:, :, :].unsqueeze(3).broadcast_to([LQ, 2, NH, HD]),
                                      ALU.mult).then_inc(s["normed"], 1)
                    dve.wait_ge(s["turned"], i + 1)
                    dve.tensor_scalar(o_t[:, bass.ds(i * 2 * LQ, 2 * LQ)], ring_ps[:, 1, 0:2 * LQ], self.bval, None,
                                      ALU.add).then_inc(s["finished"], 1)

            def gpsimd(self, pool, rows_free, earlier):
                s = self.s
                for name, n in (("maxima", 2), ("attended", 2), ("normed", 1), ("finished", 1)):
                    pool.sem_inc(s[name], n)
                rows_free(pool)
                earlier(pool)
                pool.memset(qstack_flat[SHIFT_ROW:SHIFT_ROW + 2, :].bitcast(F32), 0.0).then_inc(s["rows_clear"], 1)
                pool.wait_ge(s["rows_clear"], 1)

            def sync(self, sp, queries_ready, keys_ready, buffers_free):
                s = self.s
                buffers_free(sp)
                stack_queries(sp, queries_ready, s["queries_stacked"])
                for part in range(3):
                    keys_ready(sp, part)
                    stack_keys(sp, kpart_sb, part, 1, slice(0, NT), s["keys_stacked"])

            def sync_shifts(self, sp):
                s = self.s
                sp.wait_ge(s["shifts_in"], 1)
                for e in range(2):
                    sp.dma_start(qstack[SHIFT_ROW:SHIFT_ROW + 2, e, :, :], own_shift[:, e, 0:LQ])\
                        .then_inc(s["shifts_placed"], 16)

        class Evidence:
            def __init__(self):
                self.pe = Periods(sem("ev_pe_done"), [("S", 1), ("PT0", 0), ("PT1", 0), ("U", 0), ("UT", 0)])
                self.act = Periods(sem("ev_act_done"), [("E", 1)])
                self.dve = Periods(sem("ev_dve_done"), [("max", 1), ("PT0", 0), ("PT1", 0), ("rec", 0), ("U", 0),
                                                        ("UT", 0)])
                self.pool = Periods(sem("ev_pool_done"), [("q", 1)])
                self.loaded = sem("ev_contextT_loaded")
                self.nat_loaded = [sem(f"ev_context_loaded{u}") for u in range(2)]
                self.bank = {"PT0": 0, "PT1": 1, "U": 2, "UT": 0}

            def probs(self, u):
                return (prob_flat if u else key_sb[:, :])[0:LQ, 0:S]

            def scores(self):
                return score_ps[0:LQ, :, :, :].rearrange("p a b c -> p (a b) c")[:, 0:NJ, 0:KB]

            def tensor(self, pe, before):
                P, A, V, G = self.pe, self.act, self.dve, self.pool
                before(pe)

                def body(cur, nxt):
                    P.start(pe, {0: cur, 1: nxt})
                    if nxt:
                        n, u, half = nxt
                        pe.wait_ge(self.loaded, 16 * (n + 1))
                        pe.wait_ge(G.sem, G.after("q", n))
                        if cur:
                            pe.wait_ge(A.sem, A.after("E", n - 1))
                        for j in range(NJ):
                            last = pe.matmul(self.scores()[:, j, :], xslice[:, u, :],
                                             ctxT_sb[:, j * KB:(j + 1) * KB], start=True, stop=True)
                        P.done(last, "S")
                    if cur:
                        n, u, half = cur
                        pe.wait_ge(A.sem, A.after("E", n))
                        for i in range(2):
                            pe.wait_ge(V.sem, V.after(("UT", "PT1")[i], n - 1))
                            settle(pe)
                            for c in range(6):
                                k0 = (6 * i + c) * CK
                                last = pe.transpose(ring_ps[0:CK, self.bank[f"PT{i}"], c * LQ:(c + 1) * LQ],
                                                    self.probs(u)[:, k0:k0 + CK], ident[0:LQ, 0:LQ])
                            P.done(last, f"PT{i}")
                        pe.wait_ge(V.sem, V.after("PT1", n))
                        pe.wait_ge(self.nat_loaded[u], 16 * (half + 1))
                        for c in range(NC):
                            last = pe.matmul(ring_ps[0:LQ, self.bank["U"], 0:D], hat_sb[:, c, 0:LQ],
                                             nat_sb[:, u, c, :], start=(c == 0), stop=(c == NC - 1))
                        P.done(last, "U")
                        pe.wait_ge(V.sem, V.after("U", n))
                        settle(pe)
                        P.done(pe.transpose(ring_ps[:, self.bank["UT"], 0:LQ], on_sb[:, :], ident[0:LQ, 0:LQ]), "UT")
                    P.end()

                periods(pe, body)

            def scalar(self, act):
                P, A, V = self.pe, self.act, self.dve

                def body(cur, nxt):
                    A.start(act, {0: cur, 1: nxt})
                    if nxt:
                        n, u, half = nxt
                        act.wait_ge(V.sem, V.after("max", n))
                        if cur:
                            act.wait_ge(V.sem, V.after("U", cur[0] - 1))
                        A.done(act.activation(self.probs(u).rearrange("p (j k) -> p j k", j=NJ), self.scores(),
                                              ACT.Exp, bias=s_max[:, u, :], accum_out=s_sum[:, u, :]), "E")
                    A.end()

                periods(act, body)

            def vector(self, dve):
                P, A, V = self.pe, self.act, self.dve

                def body(cur, nxt):
                    V.start(dve, {0: cur, 1: nxt})
                    if nxt:
                        n, u, half = nxt
                        dve.wait_ge(P.sem, P.after("S", n))
                        V.done(dve.tensor_reduce(s_max[:, u, :], self.scores(), AX.XY, ALU.max, negate=True), "max")
                    if cur:
                        n, u, half = cur
                        for i in range(2):
                            dve.wait_ge(P.sem, P.after(f"PT{i}", n))
                            src = ring_ps[0:CK, self.bank[f"PT{i}"], 0:6 * LQ].rearrange("p (c q) -> p c q", q=LQ)
                            V.done(dve.tensor_copy(hat_sb[:, 6 * i:6 * i + 6, 0:LQ], src), f"PT{i}")
                        dve.wait_ge(A.sem, A.after("E", n))
                        V.done(dve.reciprocal(s_rec[:, :], s_sum[:, u, :]), "rec")
                        dve.wait_ge(V.sem, V.after("rec", n))
                        dve.wait_ge(P.sem, P.after("U", n))
                        V.done(dve.tensor_scalar(on_sb[:, :], ring_ps[0:LQ, self.bank["U"], 0:D], s_rec[:, 0:1], None,
                                                 ALU.mult), "U")
                        dve.wait_ge(P.sem, P.after("UT", n))
                        V.done(dve.tensor_copy(by_batch(o_t)[:, n, :], ring_ps[:, self.bank["UT"], 0:LQ]), "UT")
                    V.end()

                periods(dve, body)

            def gpsimd(self, pool, before):
                P, G = self.pe, self.pool
                before(pool)

                def body(cur, nxt):
                    G.start(pool, {0: cur, 1: nxt})
                    if nxt:
                        n, u, half = nxt
                        if cur:
                            pool.wait_ge(P.sem, P.after("S", cur[0]))
                            settle(pool)
                        G.done(pool.tensor_copy(xslice[:, u, :], by_batch(q_t)[:, n, :]), "q")
                    G.end()

                periods(pool, body)

            def sync(self, sp):
                P = self.pe
                sp.dma_start(ctxT_sb[:, :], ctx_T[0]).then_inc(self.loaded, 16)
                for u in range(2):
                    sp.dma_start(nat_sb[:, u, :, :], ctx_nat[u]).then_inc(self.nat_loaded[u], 16)

                def body(cur, nxt):
                    if not nxt or isinstance(nxt[0], int) and nxt[0] == B - 1:
                        return
                    n, u, half = nxt
                    sp.wait_ge(P.sem, P.after("S", n))
                    sp.dma_start(ctxT_sb[:, :], ctx_T[n + 1]).then_inc(self.loaded, 16)
                    if cur:
                        sp.wait_ge(P.sem, P.after("U", cur[0]))
                        sp.dma_start(nat_sb[:, 1 - u, :, :], ctx_nat[n + 1]).then_inc(self.nat_loaded[1 - u], 16)

                periods(sp, body)

        class Dense:

            def __init__(self, tag, products, curves, values):
                self.pe = Ticks(sem(f"{tag}_pe_done"), [p[0] for p in products])
                self.act = Ticks(sem(f"{tag}_act_done"), curves)
                self.dve = Ticks(sem(f"{tag}_dve_done"), values)
                self.products = products

            def ps(self, name):
                return ring_ps[:, self.pe.names.index(name) % RING, 0:NT]

            def product(self, pe, name, pairs, out=None):
                i = self.pe.names.index(name)
                if i >= RING:
                    _, reader, step = self.products[i - RING]
                    plan = self.act if reader == "act" else self.dve
                    pe.wait_ge(plan.sem, plan.after(step))
                for k, (lhsT, rhs) in enumerate(pairs):
                    last = pe.matmul(self.ps(name) if out is None else out, lhsT, rhs, start=(k == 0),
                                     stop=(k == len(pairs) - 1))
                self.pe.done(last, name)

            @staticmethod
            def ln_products(t):
                return [(f"{t}.mean", "dve", f"{t}.xc"), (f"{t}.var", "act", f"{t}.sd")]

            @staticmethod
            def ln_values(t):
                return [f"{t}.xc", f"{t}.sq", f"{t}.rs", f"{t}.xh"]

            def ln_pe(self, pe, t, x_ready):
                if x_ready:
                    pe.wait_ge(self.dve.sem, self.dve.after(x_ready))
                self.product(pe, f"{t}.mean", [(mean_mat[:, :], x_t)])
                pe.wait_ge(self.dve.sem, self.dve.after(f"{t}.sq"))
                self.product(pe, f"{t}.var", [(mean_mat[:, :], T(6))])

            def ln_act(self, act, t, eps):
                act.wait_ge(self.pe.sem, self.pe.after(f"{t}.var"))
                self.act.done(act.activation(T(7), self.ps(f"{t}.var"), ACT.Sqrt, bias=eps_sb[:, eps:eps + 1]),
                              f"{t}.sd")

            def step(self, dve, ins, name):
                self.dve.done(ins, name)
                dve.wait_ge(self.dve.sem, self.dve.after(name))

            def ln_dve(self, dve, t, meanwhile=None):
                dve.wait_ge(self.pe.sem, self.pe.after(f"{t}.mean"))
                self.step(dve, dve.tensor_tensor(xc_t, x_t, self.ps(f"{t}.mean"), ALU.subtract), f"{t}.xc")
                self.step(dve, dve.tensor_tensor(T(6), xc_t, xc_t, ALU.mult), f"{t}.sq")
                if meanwhile:
                    meanwhile()
                dve.wait_ge(self.act.sem, self.act.after(f"{t}.sd"))
                self.step(dve, dve.reciprocal(T(6), T(7)), f"{t}.rs")
                self.step(dve, dve.tensor_tensor(xh_t, xc_t, T(6), ALU.mult), f"{t}.xh")

            def split(self, dve, x, parts, t):
                self.step(dve, dve.tensor_copy(parts[0], x), f"{t}.0")
                self.step(dve, dve.tensor_tensor(T(6), x, parts[0], ALU.subtract), f"{t}.r")
                self.step(dve, dve.tensor_copy(parts[1], T(6)), f"{t}.1")
                self.step(dve, dve.tensor_tensor(parts[2], T(6), parts[1], ALU.subtract), f"{t}.2")

            def modulate(self, dve, scale, shift, t):
                self.step(dve, dve.tensor_tensor(by_batch(xh_t), by_batch(xh_t), mod(scale), ALU.mult), f"{t}.scaled")
                self.step(dve, dve.tensor_tensor(by_batch(xh_t), by_batch(xh_t), mod(shift), ALU.add), f"{t}.shifted")

            def gated(self, dve, y, gate, t):
                self.step(dve, dve.tensor_tensor(by_batch(y), by_batch(y), mod(gate), ALU.mult), f"{t}.gated")
                self.step(dve, dve.tensor_tensor(x_t, x_t, y, ALU.add), f"{t}.x")

        L = Dense
        d0 = Dense("d0", [("mods", "dve", "mods"), *L.ln_products("ln"), ("q", "dve", "q")],
                   ["tanh", "ln.sd", "c.sd"],
                   ["half", "silu", "mods", "scales", *L.ln_values("ln"), "m.scaled", "m.shifted", "q",
                    *[f"q.{s}" for s in "0r12"], "c.negmean", "c.rs"])
        att0 = Heads("att0", w("L0_Wkv", 0, 0, 128), w("L0_Wkv", 0, 128, 128), vec("L0_bkv", 0), vec("L0_bkv", 1),
                     hat=True, modulated=True)
        d1 = Dense("d1", [("proj", "dve", "x"), *L.ln_products("ln"), ("q", "dve", "q"), ("qk", "dve", "qk")],
                   ["ln.sd"], ["x", *L.ln_values("ln"), "nx", "q", "qk"])
        evi = Evidence()
        H = [(e, r) for e in range(E_N) for r in range(2)]

        def own_products(t):
            return [*L.ln_products(t), (f"{t}.q", "dve", f"{t}.q"), (f"{t}.k", "dve", f"{t}.k")]

        def own_values(t):
            return [*L.ln_values(t), f"{t}.scaled", f"{t}.shifted", f"{t}.q", *[f"q.{s}" for s in "0r12"], f"{t}.k", *[f"k.{s}" for s in "0r12"]]

        d2 = Dense("d2", [("ev", "dve", "ev"), *[(f"l{e}", "dve", f"l{e}") for e in range(E_N)],
                          ("g1", "dve", "gu"), ("g2", "act", "gt2"),
                          *[(f"u{e}{r}", "dve", f"u{e}{r}") for e, r in H],
                          *[(f"o{e}", "dve", f"o{e}") for e in range(E_N)],
                          ("out", "dve", "outg"), *own_products("own")],
                   ["gt", *[f"p{e}" for e in range(E_N)], "gt2", *[f"t{e}{r}" for e, r in H], "own.sd", "c.sd"],
                   ["rw", "anchor", "ev", *[f"l{e}" for e in range(E_N)], "m01", "m", *[f"d{e}" for e in range(E_N)],
                    "gu", "gh", "s01", "s", "r", *[f"p{e}" for e in range(E_N)], "g",
                    *[f"u{e}{r}" for e, r in H], *[f"h{e}{r}" for e, r in H],
                    "o0", "r0", "o1", "r1", "a1", "o2", "r2", "a2", "outg", "x", *own_values("own"), "c.rs"])
        att_own = {"L2": Own("own2", w("L2_W_qkv", 0, 256, 128), vec("L2_b_qkv", 2)),
                   "L3": Own("own3", w("L3_qkv_w", 0, 256, 128), vec("L3_qkv_b", 2))}
        att_ctx = {"L2": Heads("att2", w("L2_W_kvc", 0, 0, 128), w("L2_W_kvc", 0, 128, 128), vec("L2_b_kvc", 0),
                               vec("L2_b_kvc", 1), hat=True),
                   "L3": Heads("att3", w("L3_kv_w", 0, 0, 128), w("L3_kv_w", 0, 128, 128), vec("L3_kv_b", 0),
                               vec("L3_kv_b", 1), hat=False)}
        NAMES = {"L2": dict(qkv="L2_W_qkv", qkv_b="L2_b_qkv", proj="L2_W_proj", proj_b="L2_b_proj", q="L2_W_qc",
                            q_b="L2_b_qc", cproj="L2_W_cproj", cproj_b="L2_b_cproj", w1="L2_W_mlp1", b1="L2_b_mlp1",
                            w2="L2_W_mlp2", b2="L2_b_mlp2"),
                 "L3": dict(qkv="L3_qkv_w", qkv_b="L3_qkv_b", proj="L3_sa_proj_w", proj_b="L3_sa_proj_b", q="L3_q_w",
                            q_b="L3_q_b", cproj="L3_ca_proj_w", cproj_b="L3_ca_proj_b", w1="L3_fc1_w", b1="L3_fc1_b",
                            w2="L3_fc2_w", b2="L3_fc2_b")}
        d_mid = {l: Dense(f"dm{l}", [("proj", "dve", "y"), *L.ln_products("ln"), ("q", "dve", "q")], ["ln.sd"],
                          ["y", "y.gated", "y.x", *L.ln_values("ln"), "q", *[f"q.{s}" for s in "0r12"]]) for l in ("L2", "L3")}
        J4 = range(4)

        def end_part(l, follow):
            return Dense(f"de{l}", [("proj", "dve", "x"), *L.ln_products("ln"), *[(f"u{j}", "dve", f"u{j}") for j in J4],
                                    ("y", "dve", "y"), *(own_products("own") if follow else [])],
                         ["ln.sd", *[f"t{j}" for j in J4], *(["own.sd"] if follow else [])],
                         ["x", *L.ln_values("ln"), "m.scaled", "m.shifted",
                          *[f"{s}{j}" for j in J4 for s in ("u", "sq", "cu", "in")], *[f"h{j}" for j in J4],
                          "y", "y.gated", "y.x", *(own_values("own") if follow else [])])

        d_end = {"L2": end_part("L2", True), "L3": end_part("L3", False)}

        def own_pe(d, pe, l, x_ready):
            d.ln_pe(pe, "own", x_ready)
            pe.wait_ge(d.dve.sem, d.dve.after("own.shifted"))
            d.product(pe, "own.q", [(w(NAMES[l]["qkv"], 0, 0, 128), xh_t)])
            d.product(pe, "own.k", [(w(NAMES[l]["qkv"], 0, 128, 128), xh_t)])

        def own_dve(d, dve, l):
            d.ln_dve(dve, "own")
            d.modulate(dve, f"{l}.scale_a", f"{l}.shift_a", "own")
            dve.wait_ge(d.pe.sem, d.pe.after("own.q"))
            d.step(dve, dve.tensor_scalar(q_t, d.ps("own.q"), vec(NAMES[l]["qkv_b"], 0), HD ** -0.5, ALU.add, ALU.mult),
                   "own.q")
            d.split(dve, q_t, [qpart_sb[:, i, :] for i in range(3)], "q")
            dve.wait_ge(d.pe.sem, d.pe.after("own.k"))
            d.step(dve, dve.tensor_scalar(k_t, d.ps("own.k"), vec(NAMES[l]["qkv_b"], 1), None, ALU.add), "own.k")
            d.split(dve, k_t, [kpart_sb[:, i, :] for i in range(3)], "k")

        def last_output(att):
            if isinstance(att, Own):
                return att.s["finished"], B // 2 + 1
            if isinstance(att, Heads):
                return att.after("dve", "OTT", B - 1)
            return att.dve.sem, att.dve.after("UT", B - 1)

        def ready(d, name):
            return lambda eng, part="": eng.wait_ge(d.dve.sem, d.dve.after(f"{name}{part}"))

        a0, a2, a3 = att0, att_ctx["L2"], att_ctx["L3"]
        own2, own3 = att_own["L2"], att_own["L3"]
        buffers_ready = sem("buffers_ready")
        ones_placed = sem("ones_placed")
        stats_loaded = [sem(f"statistics_context_loaded{u}") for u in range(2)]
        stats_done = sem("statistics_done")
        stats_joined = sem("statistics_joined")
        stats_kept = sem("statistics_kept")

        loaded_early = sem("condition_and_constants_loaded")
        loaded_w0 = sem("first_weights_loaded")
        loaded_w1 = sem("other_weights_loaded")
        loaded_w3 = sem("last_weights_loaded")
        loaded_x = sem("tokens_loaded")
        stored = sem("output_stored")

        block = ctx.enter_context(nc.Block())

        @block.sync
        def _(sp):
            w0 = W_AT["L1_Wq"][0]
            sp.dma_start(cond_sb[:, :], cond_T).then_inc(loaded_early, 16)
            sp.dma_start(vec_sb[:, :], vectors).then_inc(loaded_early, 16)
            sp.dma_start(const_sb[:, :], consts).then_inc(loaded_early, 16)
            with sp.Fori(0, (B - 2) // 2) as j:
                for u in range(2):
                    sp.wait_ge(stats_done, 2 * j + u + 1)
                    sp.dma_start(nat_sb[:, u, :, :], ctx_nat[2 * j + 2 + u]).then_inc(stats_loaded[u], 16)
            sp.dma_start(w_sb[:, 0:w0], weights[:, 0:w0]).then_inc(loaded_w0, 16)
            sp.dma_start(x_t, x_T).then_inc(loaded_x, 16)
            for u in range(2):
                sp.wait_ge(stats_done, B - 2 + u + 1)
                a0.load_nat(sp, u, u)
            sp.wait_ge(buffers_ready, BUFFERS)
            for u in range(2):
                sp.dma_start(kstack[SHIFT_ROW:SHIFT_ROW + 2, u, :, :],
                             part_sb[0:2, 0, :].unsqueeze(1).broadcast_to([2, PAIRS, S])).then_inc(ones_placed, 16)
            w1 = w0
            sp.dma_start(w_sb[:, w1:W_L3], weights[:, w1:W_L3]).then_inc(loaded_w1, 16)
            stack_queries(sp, ready(d0, "q."), a0.qstacked)
            a0.sync_batch(sp, None, (0, 0, 0))
            a0.sync_later(sp)
            sp.wait_ge(*a0.after("pe", f"V{NJ - 1}", B - 1))
            evi.sync(sp)
            sp.wait_ge(*last_output(evi))
            a2.sync_load(sp)
            own2.sync(sp, ready(d2, "q."), ready(d2, "k."), ready(d2, "own.xc"))
            sp.dma_start(w_sb[:, w1:w1 + L3_COLS], weights[:, W_L3:W_L3 + L3_COLS]).then_inc(loaded_w3, 16)
            own2.sync_shifts(sp)
            a2.sync_batch(sp, None, (0, 0, 0))
            stack_queries(sp, ready(d_mid["L2"], "q."), a2.qstacked)
            a2.sync_later(sp)
            sp.wait_ge(*a2.after("pe", f"S{NC - 1}", B - 1))
            a3.sync_load(sp)
            own3.sync(sp, ready(d_end["L2"], "q."), ready(d_end["L2"], "k."), lambda eng: None)
            own3.sync_shifts(sp)
            a3.sync_batch(sp, None, (0, 0, 0))
            stack_queries(sp, ready(d_mid["L3"], "q."), a3.qstacked)
            a3.sync_later(sp)
            d = d_end["L3"]
            sp.wait_ge(d.dve.sem, d.dve.after("y.x"))
            sp.dma_start(out, x_t).then_inc(stored, 16)
            sp.wait_ge(stored, 16)

        @block.gpsimd
        def _(pool):
            pool.memset(mean_mat[:, :], 1.0 / D).then_inc(consts_ready, 1)
            pool.memset(eps_sb[:, 0:1], 1e-5).then_inc(consts_ready, 1)
            pool.memset(eps_sb[:, 1:2], 1e-6).then_inc(consts_ready, 1)
            pool.memset(qstack_flat[:, :].bitcast(F32), 0.0).then_inc(buffers_ready, 1)
            pool.wait_ge(buffers_ready, 1)
            pool.memset(kstack[96:128, :, :, :].bitcast(F32), 0.0).then_inc(buffers_ready, 1)
            pool.wait_ge(buffers_ready, 2)
            pool.memset(part_sb[0:2, 0, :], 1.0).then_inc(buffers_ready, 1)
            pool.wait_ge(buffers_ready, 3)
            pool.memset(own_val[:, :, :, :], 1.0).then_inc(buffers_ready, 1)
            pool.wait_ge(buffers_ready, 4)
            pool.memset(val_sb[:, :, :, :], 0.0).then_inc(buffers_ready, 1)
            pool.wait_ge(buffers_ready, 5)
            for u in range(2):
                pool.memset(val_sb[:, u, :, :].rearrange("p c (g k) -> p (c g) k", k=GW)[:, :, ONE:ONE + 1], 1.0)\
                    .then_inc(buffers_ready, 1)
            pool.wait_ge(buffers_ready, BUFFERS)
            pool.wait_ge(loaded_early, 48)
            ready(d0, "q")(pool)
            a0.first_queries("pool", pool)
            a0.first_context("pool", pool)
            a0.later("pool", pool)
            evi.gpsimd(pool, ready(d1, "qk"))
            own2.gpsimd(pool, lambda eng: eng.wait_ge(*last_output(evi)),
                        lambda eng: eng.wait_ge(evi.pool.sem, evi.pool.after("q", B - 1)))
            a2.first_context("pool", pool)
            ready(d_mid["L2"], "q")(pool)
            a2.first_queries("pool", pool)
            a2.later("pool", pool)
            own3.gpsimd(pool, lambda eng: eng.wait_ge(*a2.after("pe", f"S{NC - 1}", B - 1)),
                        lambda eng: eng.wait_ge(*a2.after("pool", f"k2.{NJ - 1}", B - 1)))
            a3.first_context("pool", pool)
            ready(d_mid["L3"], "q")(pool)
            a3.first_queries("pool", pool)
            a3.later("pool", pool)

        @block.tensor
        def _(pe):
            pe.wait_ge(consts_ready, CONSTS)
            pe.wait_ge(loaded_early, 48)
            d = d0
            pe.wait_ge(loaded_w0, 16)
            pe.wait_ge(d.dve.sem, d.dve.after("silu"))
            for i, (_, name, _, j) in enumerate(MODS):
                last = pe.matmul(d.ps("mods")[:, i * B:(i + 1) * B], w(name, 0, j * D, D), cond_silu[:, :],
                                 start=True, stop=True)
            d.pe.done(last, "mods")
            pe.wait_ge(loaded_x, 16)
            d.ln_pe(pe, "ln", None)
            pe.wait_ge(d.dve.sem, d.dve.after("m.shifted"))
            d.product(pe, "q", [(w("L0_Wq"), xh_t)])
            a0.first_context("pe", pe)
            a0.first_queries("pe", pe)
            pe.wait_ge(ones_placed, 32)
            a0.later("pe", pe)
            d = d1
            pe.wait_ge(*last_output(att0))
            pe.wait_ge(loaded_w1, 16)
            d.product(pe, "proj", [(w("L0_Wp"), o_t)])
            d.ln_pe(pe, "ln", "x")
            pe.wait_ge(d.dve.sem, d.dve.after("nx"))
            d.product(pe, "q", [(w("L1_Wq"), xh_t)])
            pe.wait_ge(d.dve.sem, d.dve.after("q"))
            d.product(pe, "qk", [(w("L1_WkT"), k_t)])
            evi.tensor(pe, lambda eng: eng.wait_ge(d1.dve.sem, d1.dve.after("qk")))
            d = d2
            pe.wait_ge(*last_output(evi))
            d.product(pe, "ev", [(w("L1_Wv"), o_t)])
            pe.wait_ge(d.dve.sem, d.dve.after("ev"))
            combined = (xh_t, ev_t, anchor_t)
            for e in range(E_N):
                d.product(pe, f"l{e}", [(rw_sb[:, 3 * e + c, :], combined[c]) for c in range(3)])
            d.product(pe, "g1", [(w("L1_gate_w1", c), combined[c]) for c in range(3)])
            pe.wait_ge(d.dve.sem, d.dve.after("gh"))
            d.product(pe, "g2", [(w("L1_gate_w2"), T(8))])
            for e, r in H:
                d.product(pe, f"u{e}{r}", [(w("L1_e_w1", 3 * e + c, r * D, D), combined[c]) for c in range(3)])
            for e in range(E_N):
                pe.wait_ge(d.dve.sem, d.dve.after(f"h{e}1"))
                d.product(pe, f"o{e}", [(w("L1_e_w2", 2 * e + r), hidden[2 * e + r]) for r in range(2)])
            pe.wait_ge(d.dve.sem, d.dve.after("a2"))
            d.product(pe, "out", [(w("L1_out_w"), T(14))])
            own_pe(d, pe, "L2", "x")
            pe.wait_ge(d.dve.sem, d.dve.after("own.k"))
            a2.first_context("pe", pe)
            own2.tensor(pe, ready(d2, "own.k"))
            for l in ("L2", "L3"):
                d, nm = d_mid[l], NAMES[l]
                pe.wait_ge(*last_output(att_own[l]))
                d.product(pe, "proj", [(w(nm["proj"]), o_t)])
                d.ln_pe(pe, "ln", "y.x")
                pe.wait_ge(d.dve.sem, d.dve.after("ln.xh"))
                d.product(pe, "q", [(w(nm["q"]), xh_t)])
                pe.wait_ge(d.dve.sem, d.dve.after("q"))
                att_ctx[l].first_queries("pe", pe)
                att_ctx[l].later("pe", pe)
                d = d_end[l]
                pe.wait_ge(*last_output(att_ctx[l]))
                d.product(pe, "proj", [(w(nm["cproj"]), o_t)])
                d.ln_pe(pe, "ln", "x")
                pe.wait_ge(d.dve.sem, d.dve.after("m.shifted"))
                for j in J4:
                    d.product(pe, f"u{j}", [(w(nm["w1"], 0, j * D, D), xh_t)])
                pe.wait_ge(d.dve.sem, d.dve.after("h3"))
                d.product(pe, "y", [(w(nm["w2"], j), T(8 + j)) for j in J4])
                if l == "L2":
                    pe.wait_ge(loaded_w3, 16)
                    own_pe(d, pe, "L3", "y.x")
                    pe.wait_ge(d.dve.sem, d.dve.after("own.k"))
                    a3.first_context("pe", pe)
                    own3.tensor(pe, ready(d, "own.k"))

        @block.scalar
        def _(act):
            d = d0
            act.wait_ge(consts_ready, CONSTS)
            act.wait_ge(loaded_early, 48)
            d.act.done(act.activation(cond_t[:, :], cond_sb[:, :], ACT.Tanh, scale=0.5), "tanh")
            d.ln_act(act, "ln", 0)
            act.wait_ge(stats_kept, B + 1)
            d.act.done(act.activation(norm_all[:, :, 1, :], ctx_mv[:, :, :, 1], ACT.Sqrt, bias=eps_sb[0:CK, 0:1]),
                       "c.sd")
            act.wait_ge(d.dve.sem, d.dve.after("scales"))
            act.wait_ge(buffers_ready, BUFFERS)
            act.wait_ge(ones_placed, 32)
            a0.first_context("act", act)
            a0.first_queries("act", act)
            a0.later("act", act)
            d1.ln_act(act, "ln", 0)
            evi.scalar(act)
            d = d2
            act.wait_ge(d.dve.sem, d.dve.after("gu"))
            d.act.done(act.activation(T(12), T(8), ACT.Tanh, scale=0.5), "gt")
            for e in range(E_N):
                act.wait_ge(d.dve.sem, d.dve.after(f"d{e}"))
                d.act.done(act.activation(logit[e], logit[e], ACT.Exp), f"p{e}")
            act.wait_ge(d.pe.sem, d.pe.after("g2"))
            d.act.done(act.activation(T(12), d.ps("g2"), ACT.Tanh, scale=0.25, bias=vec("L1_gate_b2", 0, half=True)),
                       "gt2")
            for i, (e, r) in enumerate(H):
                act.wait_ge(d.dve.sem, d.dve.after(f"u{e}{r}"))
                d.act.done(act.activation(curve[i], hidden[i], ACT.Tanh, scale=0.5), f"t{e}{r}")
            d.ln_act(act, "own", 1)
            d.act.done(act.activation(norm_all[:, :, 1, :], ctx_mv[:, :, :, 1], ACT.Sqrt, bias=eps_sb[0:CK, 1:2]),
                       "c.sd")
            a2.first_context("act", act)
            own2.scalar(act)
            for l in ("L2", "L3"):
                d_mid[l].ln_act(act, "ln", 1)
                att_ctx[l].first_queries("act", act)
                att_ctx[l].later("act", act)
                d = d_end[l]
                d.ln_act(act, "ln", 1)
                for j in J4:
                    act.wait_ge(d.dve.sem, d.dve.after(f"in{j}"))
                    d.act.done(act.activation(scratch(j), scratch(j), ACT.Tanh, scale=GELU_IN), f"t{j}")
                if l == "L2":
                    d.ln_act(act, "own", 1)
                    a3.first_context("act", act)
                    own3.scalar(act)

        @block.vector
        def _(dve):
            d = d0
            dve.wait_ge(consts_ready, CONSTS)
            dve.wait_ge(loaded_early, 48)
            d.step(dve, dve.tensor_scalar(vec_half[:, :], vec_sb[:, :], 0.5, None, ALU.mult), "half")
            dve.wait_ge(d.act.sem, d.act.after("tanh"))
            d.step(dve, dve.scalar_tensor_tensor(cond_silu[:, :], cond_t[:, :], 1.0, cond_sb[:, :], ALU.add, ALU.mult),
                   "silu")

            def statistics(u, n, k):
                dve.wait_ge(stats_kept, k + 1)
                for c in range(NC):
                    last = dve.bn_stats(bn_tmp[:, c, :], nat_sb[:, u, c, :])
                last.then_inc(stats_done, 1)
                dve.wait_ge(stats_done, k + 3)
                settle(dve)
                for c in range(NC):
                    last = dve.bn_aggr(mv_now[:, c, :], bn_tmp[:, c, :])
                last.then_inc(stats_joined, 1)
                dve.wait_ge(stats_joined, k + 1)
                dve.tensor_copy(ctx_mv[:, n, :, :], mv_now[:, :, :]).then_inc(stats_kept, 1)

            dve.sem_inc(stats_done, 2)
            dve.sem_inc(stats_kept, 1)
            with dve.Fori(0, (B - 2) // 2) as j:
                for u in range(2):
                    dve.wait_ge(stats_loaded[u], 16 * (j + 1))
                    settle(dve)
                    statistics(u, 2 * j + 2 + u, 2 * j + u)

            def last_statistics(u):
                dve.wait_ge(a0.nat_loaded[u], 16)
                statistics(u, u, B - 2 + u)

            dve.wait_ge(d.pe.sem, d.pe.after("mods"))
            d.step(dve, dve.scalar_tensor_tensor(
                mod_sb[:, :, :], d.ps("mods")[:, 0:len(MODS) * B].rearrange("p (m b) -> p m b", b=B), 0.5,
                vec_sb[:, 0:len(MODS)].unsqueeze(2).broadcast_to([D, len(MODS), B]), ALU.mult, ALU.add), "mods")
            d.step(dve, dve.tensor_scalar(mod_sb[:, 0:SCALES, :], mod_sb[:, 0:SCALES, :], 1.0, None, ALU.add), "scales")
            dve.wait_ge(loaded_x, 16)
            d.ln_dve(dve, "ln", lambda: last_statistics(0))
            d.modulate(dve, "L0.scale_q", "L0.shift_q", "m")
            last_statistics(1)
            dve.wait_ge(d.pe.sem, d.pe.after("q"))
            d.step(dve, dve.tensor_scalar(q_t, d.ps("q"), vec("L0_bq"), HD ** -0.5, ALU.add, ALU.mult), "q")
            d.split(dve, q_t, [qpart_sb[:, i, :] for i in range(3)], "q")
            dve.wait_ge(stats_kept, B + 1)
            d.step(dve, dve.tensor_scalar(norm_all[:, :, 0, :], ctx_mv[:, :, :, 0], -1.0, None, ALU.mult), "c.negmean")
            dve.wait_ge(d.act.sem, d.act.after("c.sd"))
            d.step(dve, dve.reciprocal(norm_all[:, :, 1, :], norm_all[:, :, 1, :]), "c.rs")
            a0.first_context("dve", dve)
            dve.wait_ge(buffers_ready, BUFFERS)
            a0.first_queries("dve", dve)
            a0.later("dve", dve)
            d = d1
            dve.wait_ge(d.pe.sem, d.pe.after("proj"))
            d.step(dve, dve.scalar_tensor_tensor(x_t, d.ps("proj"), vec("L0_bp"), x_t, ALU.add, ALU.add), "x")
            d.ln_dve(dve, "ln")
            d.step(dve, dve.tensor_scalar(xh_t, xh_t, vec("L1_ln_gamma"), vec("L1_ln_beta"), ALU.mult, ALU.add), "nx")
            dve.wait_ge(d.pe.sem, d.pe.after("q"))
            d.step(dve, dve.tensor_copy(k_t, d.ps("q")), "q")
            dve.wait_ge(d.pe.sem, d.pe.after("qk"))
            d.step(dve, dve.tensor_scalar(q_t, d.ps("qk"), D ** -0.5, None, ALU.mult), "qk")
            evi.vector(dve)
            d = d2
            at, _ = W_AT["L1_router_W"]
            d.step(dve, dve.tensor_copy(
                rw_sb.rearrange("p (e c) m -> p e c m", e=E_N),
                w_sb[:, at:at + 9].rearrange("p (c e) -> p e c", e=E_N).unsqueeze(3).broadcast_to([D, E_N, 3, D])), "rw")
            d.step(dve, dve.tensor_copy(by_batch(anchor_t), cond_sb[:, :].unsqueeze(2).broadcast_to([D, B, LQ])),
                   "anchor")
            dve.wait_ge(d.pe.sem, d.pe.after("ev"))
            d.step(dve, dve.tensor_copy(ev_t, d.ps("ev")), "ev")
            for e in range(E_N):
                dve.wait_ge(d.pe.sem, d.pe.after(f"l{e}"))
                d.step(dve, dve.tensor_scalar(logit[e], d.ps(f"l{e}"), vec("router_b", e), None, ALU.add), f"l{e}")
            d.step(dve, dve.tensor_tensor(xc_t, logit[0], logit[1], ALU.max), "m01")
            d.step(dve, dve.tensor_tensor(xc_t, xc_t, logit[2], ALU.max), "m")
            for e in range(E_N):
                d.step(dve, dve.tensor_tensor(logit[e], logit[e], xc_t, ALU.subtract), f"d{e}")
            dve.wait_ge(d.pe.sem, d.pe.after("g1"))
            d.step(dve, dve.tensor_scalar(T(8), d.ps("g1"), vec("L1_gate_b1"), None, ALU.add), "gu")
            dve.wait_ge(d.act.sem, d.act.after("gt"))
            d.step(dve, dve.scalar_tensor_tensor(T(8), T(12), 1.0, T(8), ALU.add, ALU.mult), "gh")
            dve.wait_ge(d.act.sem, d.act.after("p2"))
            d.step(dve, dve.tensor_tensor(xc_t, logit[0], logit[1], ALU.add), "s01")
            d.step(dve, dve.tensor_tensor(xc_t, xc_t, logit[2], ALU.add), "s")
            d.step(dve, dve.reciprocal(xc_t, xc_t), "r")
            for e in range(E_N):
                d.step(dve, dve.tensor_tensor(logit[e], logit[e], xc_t, ALU.mult), f"p{e}")
            dve.wait_ge(d.act.sem, d.act.after("gt2"))
            d.step(dve, dve.tensor_scalar(T(12), T(12), 1.0, None, ALU.add), "g")
            for i, (e, r) in enumerate(H):
                dve.wait_ge(d.pe.sem, d.pe.after(f"u{e}{r}"))
                d.step(dve, dve.tensor_scalar(hidden[i], d.ps(f"u{e}{r}"), vec("L1_e_b1", i), None, ALU.add), f"u{e}{r}")
            for i, (e, r) in enumerate(H):
                dve.wait_ge(d.act.sem, d.act.after(f"t{e}{r}"))
                d.step(dve, dve.scalar_tensor_tensor(hidden[i], curve[i], 1.0, hidden[i], ALU.add, ALU.mult), f"h{e}{r}")
            for e in range(E_N):
                dve.wait_ge(d.pe.sem, d.pe.after(f"o{e}"))
                d.step(dve, dve.tensor_scalar(T(8), d.ps(f"o{e}"), 0.5, vec("L1_e_b2", e), ALU.mult, ALU.add), f"o{e}")
                d.step(dve, dve.tensor_tensor(T(14) if e == 0 else T(8), T(8), logit[e], ALU.mult), f"r{e}")
                if e:
                    d.step(dve, dve.tensor_tensor(T(14), T(14), T(8), ALU.add), f"a{e}")
            dve.wait_ge(d.pe.sem, d.pe.after("out"))
            d.step(dve, dve.scalar_tensor_tensor(T(13), d.ps("out"), vec("L1_out_b"), T(12), ALU.add, ALU.mult), "outg")
            d.step(dve, dve.scalar_tensor_tensor(x_t, T(13), 0.5, x_t, ALU.mult, ALU.add), "x")
            own_dve(d, dve, "L2")
            dve.wait_ge(d.act.sem, d.act.after("c.sd"))
            d.step(dve, dve.reciprocal(norm_all[:, :, 1, :], norm_all[:, :, 1, :]), "c.rs")
            a2.first_context("dve", dve)
            own2.vector(dve)
            for l in ("L2", "L3"):
                d, nm = d_mid[l], NAMES[l]
                dve.wait_ge(d.pe.sem, d.pe.after("proj"))
                d.step(dve, dve.tensor_scalar(T(8), d.ps("proj"), vec(nm["proj_b"]), None, ALU.add), "y")
                d.gated(dve, T(8), f"{l}.gate_a", "y")
                d.ln_dve(dve, "ln")
                dve.wait_ge(d.pe.sem, d.pe.after("q"))
                d.step(dve, dve.tensor_scalar(q_t, d.ps("q"), vec(nm["q_b"]), HD ** -0.5, ALU.add, ALU.mult), "q")
                d.split(dve, q_t, [qpart_sb[:, i, :] for i in range(3)], "q")
                att_ctx[l].first_queries("dve", dve)
                att_ctx[l].later("dve", dve)
                d = d_end[l]
                dve.wait_ge(d.pe.sem, d.pe.after("proj"))
                d.step(dve, dve.scalar_tensor_tensor(x_t, d.ps("proj"), vec(nm["cproj_b"]), x_t, ALU.add, ALU.add), "x")
                d.ln_dve(dve, "ln")
                d.modulate(dve, f"{l}.scale_m", f"{l}.shift_m", "m")
                for j in J4:
                    u, s = T(8 + j), scratch(j)
                    dve.wait_ge(d.pe.sem, d.pe.after(f"u{j}"))
                    d.step(dve, dve.tensor_scalar(u, d.ps(f"u{j}"), vec(nm["b1"], j), None, ALU.add), f"u{j}")
                    d.step(dve, dve.tensor_tensor(s, u, u, ALU.mult), f"sq{j}")
                    d.step(dve, dve.tensor_scalar(s, s, GELU_CUBE, 1.0, ALU.mult, ALU.add), f"cu{j}")
                    d.step(dve, dve.tensor_tensor(s, s, u, ALU.mult), f"in{j}")
                for j in J4:
                    dve.wait_ge(d.act.sem, d.act.after(f"t{j}"))
                    d.step(dve, dve.scalar_tensor_tensor(T(8 + j), scratch(j), 1.0, T(8 + j), ALU.add, ALU.mult), f"h{j}")
                dve.wait_ge(d.pe.sem, d.pe.after("y"))
                d.step(dve, dve.tensor_scalar(T(12), d.ps("y"), 0.5, vec(nm["b2"]), ALU.mult, ALU.add), "y")
                d.gated(dve, T(12), f"{l}.gate_m", "y")
                if l == "L2":
                    own_dve(d, dve, "L3")
                    own3.vector(dve)


def kernel(**inputs):
    import concourse.bacc as bacc
    from concourse.bass_utils import run_bass_kernel_spmd

    a = {}
    for name, value in inputs.items():
        a[name.replace("_xcond", "")] = np.asarray(value)
    nat = a["ctx_1024"].reshape(B, CK, NC, D)
    a["L1_WkT"] = a["L1_Wk"].T
    for name, n in HEADED.items():
        cols = [j * D + f for j in range(n) for f in FEATURE_AT] + list(range(n * D, a[name].shape[-1]))
        a[name] = a[name][..., cols]
    blocks = [a[name].reshape(n, D, cols).transpose(1, 0, 2).reshape(D, n * cols) for name, n, cols in WEIGHTS]
    columns = [a[bias][j * D:(j + 1) * D][:, None] for _, _, bias, j in MODS]
    columns += [a[name].reshape(n, D).T for name, n in VECTORS]
    columns.append(np.broadcast_to(a["L1_router_b"][None, :], (D, E_N)))
    consts = np.zeros((D, C_COLS), np.float32)
    consts[:, C_ID:C_ID + D] = np.eye(D)
    for p in range(D):
        consts[p, C_HEAD + HEAD_OF[p]] = 1.0
    arrays = {
        "ctx_nat": nat,
        "ctx_T": nat.transpose(0, 3, 2, 1).reshape(B, D, S),
        "x_T": a["x"].reshape(NT, D).T,
        "cond_T": a["cond_1024"].T,
        "weights": np.concatenate(blocks, axis=1),
        "vectors": np.concatenate(columns, axis=1),
        "consts": consts,
    }
    arrays = {name: np.ascontiguousarray(value) for name, value in arrays.items()}
    nc = bacc.Bacc("TRN2", target_bir_lowering=False, num_devices=1)
    args = [nc.dram_tensor(name, value.shape, F32, kind="ExternalInput").ap() for name, value in arrays.items()]
    out = nc.dram_tensor("out_T", (D, NT), F32, kind="ExternalOutput").ap()
    pixart_program(nc, *args, out)
    r = run_bass_kernel_spmd(nc, [arrays], core_ids=[0])
    return np.ascontiguousarray(r.results[0]["out_T"].T).reshape(B, LQ, D)
```

```python
from contextlib import ExitStack

import concourse.bass as bass
import numpy as np
from concourse import mybir

F32 = mybir.dt.float32
BF16 = mybir.dt.bfloat16
ALU = mybir.AluOpType
ACT = mybir.ActivationFunctionType
AX = mybir.AxisListType

B, LQ, D = 8, 56, 128
S = 1500
NH, HD = 16, 8
NT = B * LQ
NC = 12
CK = S // NC
KB = 500
NJ = S // KB
CJ = KB // CK
HQ = NH * LQ
HALF = HQ // 2
GROUPS = [(3 * g, 3) for g in range(4)] + [(12, 2), (14, 2)]
PAIRS = NH // 2
SLOTS = [(0, 0), (0, 1), (0, 2), (1, 0), (1, 1), (2, 0)]
SHIFT_ROW = 16 * len(SLOTS)
OW = HD + 1
GW = 32
ONE = 24
MLP = 4 * D
E_N = 3
RING = 3

WEIGHTS = [
    ("L0_Wq", 1, 128), ("L0_Wkv", 1, 256), ("L0_Wp", 1, 128), ("L0_Wss_q", 1, 256), ("L0_Wss_kv", 1, 256),
    ("L2_W_mod", 1, 768), ("L3_adaln_w", 1, 768),
    ("L1_Wq", 1, 128), ("L1_WkT", 1, 128), ("L1_Wv", 1, 128), ("L1_router_W", 3, 3), ("L1_e_w1", 9, 256),
    ("L1_e_w2", 6, 128), ("L1_gate_w1", 3, 128), ("L1_gate_w2", 1, 128), ("L1_out_w", 1, 128),
    ("L2_W_qkv", 1, 384), ("L2_W_proj", 1, 128), ("L2_W_qc", 1, 128), ("L2_W_kvc", 1, 256),
    ("L2_W_cproj", 1, 128), ("L2_W_mlp1", 1, 512), ("L2_W_mlp2", 4, 128),
    ("L3_qkv_w", 1, 384), ("L3_sa_proj_w", 1, 128), ("L3_q_w", 1, 128), ("L3_kv_w", 1, 256),
    ("L3_ca_proj_w", 1, 128), ("L3_fc1_w", 1, 512), ("L3_fc2_w", 4, 128),
]
W_AT, _w = {}, 0
for _name, _blocks, _cols in WEIGHTS:
    if _name == "L3_qkv_w":
        W_L3 = _w
        _w = 0
    W_AT[_name] = (_w + (W_AT["L1_Wq"][0] if _name.startswith("L3") and _name != "L3_adaln_w" else 0), _cols)
    _w += _blocks * _cols
L3_COLS = _w
MODS = [("L0.scale_q", "L0_Wss_q", "L0_bss_q", 0), ("L0.scale_kv", "L0_Wss_kv", "L0_bss_kv", 0),
        ("L2.scale_a", "L2_W_mod", "L2_b_mod", 1), ("L2.scale_m", "L2_W_mod", "L2_b_mod", 4),
        ("L3.scale_a", "L3_adaln_w", "L3_adaln_b", 1), ("L3.scale_m", "L3_adaln_w", "L3_adaln_b", 4),
        ("L0.shift_q", "L0_Wss_q", "L0_bss_q", 1), ("L0.shift_kv", "L0_Wss_kv", "L0_bss_kv", 1),
        ("L2.shift_a", "L2_W_mod", "L2_b_mod", 0), ("L2.gate_a", "L2_W_mod", "L2_b_mod", 2),
        ("L2.shift_m", "L2_W_mod", "L2_b_mod", 3), ("L2.gate_m", "L2_W_mod", "L2_b_mod", 5),
        ("L3.shift_a", "L3_adaln_w", "L3_adaln_b", 0), ("L3.gate_a", "L3_adaln_w", "L3_adaln_b", 2),
        ("L3.shift_m", "L3_adaln_w", "L3_adaln_b", 3), ("L3.gate_m", "L3_adaln_w", "L3_adaln_b", 5)]
SCALES = 6
MOD = {m[0]: n for n, m in enumerate(MODS)}
VECTORS = [
    ("L0_bq", 1), ("L0_bkv", 2), ("L0_bp", 1),
    ("L1_ln_gamma", 1), ("L1_ln_beta", 1), ("L1_e_b1", 6), ("L1_e_b2", 3), ("L1_gate_b1", 1),
    ("L1_gate_b2", 1), ("L1_out_b", 1),
    ("L2_b_qkv", 3), ("L2_b_proj", 1), ("L2_b_qc", 1), ("L2_b_kvc", 2), ("L2_b_cproj", 1), ("L2_b_mlp1", 4),
    ("L2_b_mlp2", 1),
    ("L3_qkv_b", 3), ("L3_sa_proj_b", 1), ("L3_q_b", 1), ("L3_kv_b", 2), ("L3_ca_proj_b", 1), ("L3_fc1_b", 4),
    ("L3_fc2_b", 1),
]
V_AT, _v = {}, len(MODS)
for _name, _cols in VECTORS:
    V_AT[_name] = _v
    _v += _cols
V_AT["router_b"] = _v
V_COLS = _v + E_N
ANCHORED = [*[("L1_router_W", e, "router_b", e) for e in range(E_N)], ("L1_gate_w1", 0, "L1_gate_b1", 0),
            *[("L1_e_w1", (e, r), "L1_e_b1", 2 * e + r) for e in range(E_N) for r in range(2)]]
HEAD_OF = [2 * (p % PAIRS) + p // 64 for p in range(D)]
FEATURE_AT = [HD * HEAD_OF[p] + (p // PAIRS) % HD for p in range(D)]
HEADED = {"L0_Wq": 1, "L0_bq": 1, "L0_Wkv": 1, "L0_bkv": 1, "L2_W_qkv": 2, "L2_b_qkv": 2, "L2_W_qc": 1, "L2_b_qc": 1,
          "L2_W_kvc": 1, "L2_b_kvc": 1, "L3_qkv_w": 2, "L3_qkv_b": 2, "L3_q_w": 1, "L3_q_b": 1, "L3_kv_w": 1,
          "L3_kv_b": 1}
GELU_IN = 0.7978845608028654
GELU_CUBE = 0.044715
REPLICA = 16 * len(SLOTS)
QB = 2 * LQ
TOK = NT // 4
KEPT = 4
CONSTS = 4
BUFFERS = 8


class Ticks:

    def __init__(self, sem, names):
        assert len(set(names)) == len(names), [n for n in names if names.count(n) > 1]
        self.sem, self.names, self.at = sem, names, 0

    def done(self, ins, name):
        assert self.names[self.at] == name, (self.names[self.at], name)
        self.at += 1
        return ins.then_inc(self.sem, 1)

    def after(self, name):
        return self.names.index(name) + 1


class Periods:

    def __init__(self, sem, steps):
        self.sem, self.names, self.leads = sem, [n for n, _ in steps], [d for _, d in steps]
        assert len(set(self.names)) == len(self.names)
        self.at = 0

    def start(self, eng, batches):
        self.has = {d: batches.get(d) is not None for d in (-1, 0, 1, 2)}
        self.at = 0
        if not any(self.has[d] for d in self.leads):
            self.at = len(self.names)

    def done(self, ins, name):
        i = self.names.index(name)
        assert i >= self.at, name
        step = i + 1 - self.at
        assert self.has[self.leads[i]] and not any(self.has[d] for d in self.leads[self.at:i]), name
        self.at = i + 1
        if not any(self.has[d] for d in self.leads[i + 1:]):
            step += len(self.names) - i - 1
            self.at = len(self.names)
        return ins.then_inc(self.sem, step)

    def end(self):
        assert self.at in (0, len(self.names)), (self.at, self.names)

    def place(self, name, d):
        i = self.names.index(name)
        return (d + max(self.leads) - self.leads[i]) * len(self.names) + i + 1

    def after(self, name, n):
        return n * len(self.names) + self.place(name, 0)


def wait_steps(eng, n, *steps):
    last = {}
    for plan, name, d in steps:
        last[plan] = max(last.get(plan, -9999), plan.place(name, d))
    for plan, at in last.items():
        eng.wait_ge(plan.sem, n * len(plan.names) + at)


def periods(eng, body):
    body(None, (0, 0, 0))
    with eng.Fori(0, (B - 2) // 2) as j:
        body((2 * j, 0, j), (2 * j + 1, 1, j))
        body((2 * j + 1, 1, j), (2 * j + 2, 0, j + 1))
    body((B - 2, 0, (B - 2) // 2), (B - 1, 1, (B - 2) // 2))
    body((B - 1, 1, (B - 2) // 2), None)


def later_periods(body, eng):
    body(None, None, (0, 0, 0), (1, 1, 0))
    body(None, (0, 0, 0), (1, 1, 0), (2, 0, 1))
    with eng.Fori(0, (B - 4) // 2) as j:
        body((2 * j, 0, j), (2 * j + 1, 1, j), (2 * j + 2, 0, j + 1), (2 * j + 3, 1, j + 1))
        body((2 * j + 1, 1, j), (2 * j + 2, 0, j + 1), (2 * j + 3, 1, j + 1), (2 * j + 4, 0, j + 2))
    h = B // 2
    body((B - 4, 0, h - 2), (B - 3, 1, h - 2), (B - 2, 0, h - 1), (B - 1, 1, h - 1))
    body((B - 3, 1, h - 2), (B - 2, 0, h - 1), (B - 1, 1, h - 1), None)
    body((B - 2, 0, h - 1), (B - 1, 1, h - 1), None, None)
    body((B - 1, 1, h - 1), None, None, None)


def pixart_program(nc, ctx_nat, ctx_T, x_T, cond_T, weights, vectors, identity, out):
    ctx = ExitStack()
    with ctx:
        def sb(name, shape, dt=F32):
            return ctx.enter_context(nc.sbuf_tensor(name, shape, dt))

        def pb(name, shape):
            return ctx.enter_context(nc.psum_tensor(name, shape, F32))

        def sem(name):
            return ctx.enter_context(nc.semaphore(name))

        w_sb = sb("w_sb", [D, W_L3])
        vec_sb = sb("vec_sb", [D, V_COLS])
        vec_half = sb("vec_half", [D, V_COLS])
        ident = sb("ident", [D, D])
        cond_sb = sb("cond_sb", [D, B])
        cond_t = sb("cond_t", [D, B])
        cond_silu = sb("cond_silu", [D, B])
        mod_sb = sb("mod_sb", [D, len(MODS), B])
        mean_mat = sb("mean_mat", [D, D])
        nat_sb = sb("nat_sb", [D, 2, NC, D])
        ctx_mv = sb("ctx_mv", [CK, B, NC, 2])
        mv_now = sb("mv_now", [CK, NC, 2])
        bn_tmp = sb("bn_tmp", [CK, NC, 6])
        norm_all = sb("norm_all", [CK, B, 3, NC])
        norm_now = sb("norm_now", [CK, 2, NC])
        hat_sb = sb("hat_sb", [CK, NC, D])
        ctxT_sb = sb("ctxT_sb", [D, S])
        key_sb = sb("key_sb", [D, S])
        part_sb = sb("part_sb", [D, 3, S], BF16)
        qpart_sb = sb("qpart_sb", [D, 3, B, 2, LQ], BF16)
        kstack = sb("kstack", [D, 2, PAIRS, S], BF16)
        qstack = sb("qstack", [D, PAIRS * B * QB + 16], BF16)
        own_val = sb("own_val", [LQ, B, NH, OW])
        own_max = sb("own_max", [D, PAIRS, B])
        own_maxb = sb("own_maxb", [D, PAIRS, B], BF16)
        own_maxparts = sb("own_maxparts", [D, 2, PAIRS, B])
        own_shift = sb("own_shift", [D, QB], BF16)
        own_rec = sb("own_rec", [LQ, 2, NH])
        own_out = sb("own_out", [LQ, 2, D])
        val_sb = sb("val_sb", [CK, 2, NC, len(GROUPS) * GW])
        prob_sb = sb("prob_sb", [D, 2, HQ])
        max_sb = sb("max_sb", [D, PAIRS, NJ])
        max1 = sb("max1", [D, PAIRS])
        maxb = sb("maxb", [D, PAIRS], BF16)
        maxparts = sb("maxparts", [D, PAIRS, 2])
        o_sb = sb("o_sb", [D, 5 * LQ])
        osum_r = sb("osum_r", [LQ, NH])
        on_sb = sb("on_sb", [LQ, D])
        xslice = sb("xslice", [D, 2, LQ])
        tok = sb("tok", [D, 11, NT])
        s_max = sb("s_max", [LQ, 2, 1])
        s_sum = sb("s_sum", [LQ, 2, 1])
        s_rec = sb("s_rec", [LQ, 1])
        sum_rep = sb("sum_rep", [D, LQ])
        anchors = sb("anchors", [D, len(ANCHORED), B])

        score_ps = pb("score_ps", [D, 2, 2, 512])
        oacc_ps = pb("oacc_ps", [D, 512])
        ring_ps = pb("ring_ps", [D, RING, 512])

        def w(name, block=0, lo=0, n=None):
            at, cols = W_AT[name]
            at += block * cols + lo
            return w_sb[:, at:at + (n or cols - lo)]

        def vec(name, j=0, half=False):
            at = V_AT[name] + j
            return (vec_half if half else vec_sb)[:, at:at + 1]

        part_flat = part_sb[:, :, :].rearrange("p a k -> p (a k)").bitcast(F32)

        def T(i):
            if i < 11:
                return tok[:, i, :]
            return part_flat[:, (i - 11) * NT:(i - 10) * NT]

        def scratch(i):
            return (key_sb[:, :] if i < 3 else prob_flat)[:, (i % 3) * NT:(i % 3 + 1) * NT]

        prob_flat = prob_sb[:, :, :].rearrange("p a k -> p (a k)")
        kpart_sb = prob_flat[:, 0:3 * NT // 2].bitcast(BF16).rearrange("p (a k) -> p a k", a=3)

        qsplit_sb = prob_flat[:, 3 * NT // 2:3 * NT].bitcast(BF16).rearrange("p (a k) -> p a k", a=3)

        def queries(p, n, cols=QB):
            return qstack[:, bass.ds((p * B + n) * QB, cols)]

        def by_batch(ap):
            return ap.rearrange("p (b q) -> p b q", q=LQ)

        def mod(name):
            return mod_sb[:, MOD[name], :].unsqueeze(2).broadcast_to([D, B, LQ])

        x_t, xc_t, xh_t, q_t, k_t, o_t = (T(i) for i in range(6))

        eps_sb = sb("eps_sb", [D, 2])
        tok_var = sb("tok_var", [TOK, 4])
        tok_rstd = sb("tok_rstd", [TOK, 4])
        minus_half = sb("minus_half", [TOK, 4])
        consts_ready = sem("constants_ready")
        settled = sem("settled")
        ev_t = T(6)
        logit = (q_t, k_t, o_t)
        hidden = [T(9), T(10), T(11), T(13), scratch(0), scratch(1)]
        curve = [T(8), T(14), scratch(2), scratch(3), scratch(4), scratch(5)]

        def settle(eng):
            eng.sem_inc(settled, 1)

        def stack_queries(sp, ready, stacked):
            for part in range(3):
                ready(sp, part)
                for slot, (_, qpart) in enumerate(SLOTS):
                    if qpart == part:
                        sp.dma_start(qstack[16 * slot:16 * slot + 16, 0:PAIRS * B * QB]
                                     .rearrange("r (p k) -> r p k", p=PAIRS),
                                     qpart_sb[:, part, :, :, :].rearrange("r b e q -> r (b e q)"))\
                            .then_inc(stacked, 16)

        def stack_keys(sp, src, part, u, cols, stacked):
            for slot, (kpart, _) in enumerate(SLOTS):
                if kpart == part:
                    sp.dma_start(kstack[16 * slot:16 * slot + 16, u, :, cols], src[:, part, cols])\
                        .then_inc(stacked, 16)

        class Heads:
            def __init__(self, tag, wkey, wval, bkey, bval, hat, modulated=False):
                self.tag, self.wkey, self.wval, self.bkey, self.bval = tag, wkey, wval, bkey, bval
                self.hat, self.modulated = hat, modulated
                J = range(NJ)
                mm = [f"M{j}.{p}" for p in range(PAIRS) for j in J]
                self.mm = mm
                T3 = [f"T{j}" for j in J] if hat else []
                if hat:
                    beside = {1: ["OT", *T3], 2: ["OTT", "K0"], 3: mm[0:3], 4: ["K1", *mm[3:5]], 5: mm[5:8],
                              6: mm[8:11], 7: ["K2", *mm[11:13]], 8: mm[13:16], 9: mm[16:19], 10: mm[19:22],
                              11: mm[22:24]}
                else:
                    beside = {1: ["K0", "OT"], 2: ["OTT"], 3: ["K1", *mm[0:2]], 4: mm[2:5], 5: ["K2", *mm[5:8]],
                              6: mm[8:11], 7: mm[11:14], 8: mm[14:16], 9: mm[16:19], 10: mm[19:21], 11: mm[21:24]}
                pe = []
                for c in range(NC):
                    more = beside.get(c, [])
                    pe += [f"S{c}", *more[:-1]] + ([f"PV{c - 1}"] if c else []) + more[-1:]
                pe += [f"PV{NC - 1}", "V0", "V1", "MTa", "MTb", "V2"]
                act = []
                for c in range(NC):
                    act += [f"E{c}", *(T3 if c == 1 else [])]
                    for j in J:
                        if f"K{j}" in beside.get(c, []):
                            act += [f"k0.{j}", f"K{j}"]
                act += ["V0", "V1", "shift1", "V2"]
                dve = ["O", "sum0", "sum1", "norm0", "norm1", "OTT", *mm, "maxall", "maxb", "part0", "part1", "shift0"]
                pool = (["norm", "hat0", "hat1", "hat2"] if hat else []) + [f"{s}{j}" for j in J for s in ("rest", "k1.", "k2.")]
                LEAD = {"S": 0, "P": 0, "E": 0, "O": -1, "s": -1, "n": -1, "T": 2, "K": 2, "V": 2, "k": 2, "h": 2, "r": 2}

                def lead(n):
                    return 2 if n == "norm" else 1 if n in ("shift0", "shift1") else LEAD.get(n[0], 1)

                self.lead = lead
                self.orders = {"pe": pe, "act": act, "dve": dve, "pool": pool}
                of_context = {"pe": "TKV", "act": "TkKV", "dve": (), "pool": "nhrk"}

                def context(eng, n):
                    mine = of_context[eng]
                    return n in mine if isinstance(mine, tuple) else n[0] in mine

                self.context = context
                self.plans = {}
                for eng, order in self.orders.items():
                    for which in (False, True):
                        steps = [(n, lead(n)) for n in order if context(eng, n) == which]
                        kind = "context" if which else "attention"
                        self.plans[eng, which] = Periods(sem(f"{tag}_{eng}_{kind}_done"), steps) if steps else None
                self.loaded = [sem(f"{tag}_contextT_loaded{u}") for u in range(2)] if not hat else None
                self.nat_loaded = [sem(f"{tag}_context_loaded{u}") for u in range(2)] if hat else None
                self.stacked = [sem(f"{tag}_keys_stacked{u}") for u in range(2)]
                self.qstacked = sem(f"{tag}_queries_stacked")
                self.rows_clear = sem(f"{tag}_rows_clear")
                self.reader = {}
                for j in J:
                    self.reader |= {f"T{j}": ("act", f"T{j}"), f"K{j}": ("act", f"K{j}"), f"V{j}": ("act", f"V{j}")}
                for m in mm:
                    self.reader[m] = ("dve", m)
                self.reader |= {"MTa": ("dve", "shift0"), "MTb": ("act", "shift1"), "OT": ("dve", "norm1"),
                                "OTT": ("dve", "OTT")}
                self.bank, at, kept = {}, 0, []
                for n in [n for n in pe if n in self.reader]:
                    while at % RING in kept[:1]:
                        at += 1
                    self.bank[n] = at % RING
                    kept = [self.bank[n]] * KEPT if n[0] == "K" and n != "K0" else kept[1:]
                    at += 1
                self.users = {}

            def context_T(self, u):
                return ctxT_sb[:, :] if self.hat else nat_sb[:, u, :, :].rearrange("p c k -> p (c k)")[:, 0:S]

            def at(self, eng, name, d=0):
                return self.plans[eng, self.context(eng, name)], name, d

            def after(self, eng, name, n):
                plan = self.at(eng, name)[0]
                return plan.sem, plan.after(name, n)

            def done(self, eng, ins, name):
                self.at(eng, name)[0].done(ins, name)

            def ring_read(self, name):
                bank, lead = self.bank[name], self.lead(name)
                last = self.users.get(bank)
                self.users[bank] = (name, lead)
                if last is None:
                    return []
                return [self.at(*self.reader[last[0]], last[1] - lead)]

            def run(self, eng, engine, emit, prev, cur, nxt, far, third=None):
                batches = {-1: prev, 0: cur, 1: nxt, 2: far}
                first = not nxt and far
                plans = [self.plans[eng, c] for c in ((True,) if first else (False, True))]
                plans = [p for p in plans if p]
                if not third:
                    for plan in plans:
                        plan.start(engine, batches)
                if eng == "pe":
                    if first and not third:
                        self.users = {}
                    elif not first:
                        self.users = {b: (n, d - 1) for b, (n, d) in self.users.items()}
                for name in self.orders[eng]:
                    if self.at(eng, name)[0] in plans and batches[self.lead(name)] and \
                            (third is None or name[0] in ("T", "kK", "V")[third]):
                        emit(name, batches[self.lead(name)], prev, cur, nxt)
                if third in (None, 2):
                    for plan in plans:
                        plan.end()

            def pe_step(self, pe):
                def emit(name, batch, prev, cur, nxt):
                    n, u, half = batch
                    free = self.ring_read(name) if name in self.bank else []
                    ps = ring_ps[:, self.bank[name], :] if name in self.bank else None
                    if name[0] == "T":
                        wait_steps(pe, n, self.at("pool", f"hat{name[1:]}"), *free)
                        j = int(name[1:])
                        for c in range(CJ):
                            last = pe.transpose(ps[:, c * CK:(c + 1) * CK], hat_sb[:, j * CJ + c, :],
                                                ident[0:CK, 0:CK])
                    elif name[0] == "K":
                        j = int(name[1:])
                        if self.loaded and j == 0:
                            pe.wait_ge(self.loaded[u], 16 * (half + 1))
                        wait_steps(pe, n, *([self.at("act", f"T{j}")] if self.hat else []), *free)
                        last = pe.matmul(ps[:, 0:KB], self.wkey, self.context_T(u)[:, j * KB:(j + 1) * KB],
                                         start=True, stop=True)
                    elif name[0] == "V":
                        j = int(name[1:])
                        wait_steps(pe, n, *free)
                        for c in range(CJ):
                            k0 = (j * CJ + c) * CK
                            last = pe.matmul(ps[0:CK, c * D:(c + 1) * D], self.context_T(u)[:, k0:k0 + CK], self.wval,
                                             start=True, stop=True)
                    elif name[0:2] == "MT":
                        wait_steps(pe, n, self.at("dve", "part1"), *free)
                        for i in range(4):
                            last = pe.transpose(ps[0:2, i * D:(i + 1) * D],
                                                maxparts[:, i + (4 if name == "MTb" else 0), :], ident[:, :])
                    elif name[0] == "M":
                        j, p = (int(t) for t in name[1:].split("."))
                        if name == self.mm[0]:
                            pe.wait_ge(self.stacked[u], REPLICA * (half + 1))
                            pe.wait_ge(self.qstacked, REPLICA)
                            pe.wait_ge(self.rows_clear, 1)
                        wait_steps(pe, n, *free)
                        last = pe.matmul(ps[:, 0:KB], queries(p, n, D), kstack[:, u, p, j * KB:(j + 1) * KB],
                                         start=True, stop=True)
                    elif name[0] == "S":
                        c = int(name[1:])
                        need = [self.at("dve", "shift0"), self.at("act", "shift1")] if c == 0 else []
                        if c >= 2:
                            need.append(self.at("act", f"E{c - 2}"))
                        elif prev:
                            need.append(self.at("act", f"E{NC - 2 + c}", -1))
                        wait_steps(pe, n, *need)
                        for p in range(PAIRS):
                            at = (p % 4) * 2 * LQ
                            last = pe.matmul(score_ps[0:CK, c % 2, p // 4, at:at + 2 * LQ],
                                             kstack[:, u, p, c * CK:(c + 1) * CK],
                                             queries(p, n), start=True, stop=True)
                    elif name[0] == "P":
                        c = int(name[2:])
                        wait_steps(pe, n, self.at("act", f"E{c}"), *([self.at("act", "V2")] if c == 0 else []),
                                   *([self.at("dve", "O", -1)] if c == 0 and prev else []))
                        for g, (h0, nh) in enumerate(GROUPS):
                            q = g % 4
                            at = 0 if g < 4 else 3 * LQ
                            last = pe.matmul(oacc_ps[q * GW:(q + 1) * GW, at:at + nh * LQ],
                                             val_sb[0:CK, u, c, g * GW:(g + 1) * GW],
                                             prob_sb[0:CK, c % 2, h0 * LQ:(h0 + nh) * LQ],
                                             start=(c == 0 and g < 4), stop=(c == NC - 1), skip_group_check=True)
                    elif name == "OT":
                        wait_steps(pe, n, self.at("dve", "O"), *free)
                        settle(pe)
                        for i in range(5):
                            rows = D if i < 3 else 64
                            at = 128 * i if i < 3 else 384 + 64 * (i - 3)
                            last = pe.transpose(ps[0:LQ, at:at + rows], o_sb[0:rows, i * LQ:(i + 1) * LQ],
                                                ident[0:rows, 0:rows])
                    elif name == "OTT":
                        wait_steps(pe, n, self.at("dve", "norm1"), *free)
                        settle(pe)
                        last = pe.transpose(ps[:, 0:LQ], on_sb[:, :], ident[0:LQ, 0:LQ])
                    self.done("pe", last, name)
                return emit

            def act_step(self, act):
                def emit(name, batch, prev, cur, nxt):
                    n, u, half = batch
                    ps = ring_ps[:, self.bank[name], :] if name in self.bank else None
                    if name[0] == "T":
                        j = int(name[1:])
                        act.wait_ge(*self.after("pe", name, n))
                        settle(act)
                        src, dst = ps[:, 0:KB], ctxT_sb[:, j * KB:(j + 1) * KB]
                        if self.modulated:
                            ins = act.activation(dst, src, ACT.Identity,
                                                 bias=mod_sb[:, MOD["L0.shift_kv"], bass.ds(n, 1)],
                                                 scale=mod_sb[:, MOD["L0.scale_kv"], bass.ds(n, 1)])
                        else:
                            ins = act.copy(dst, src)
                    elif name[0] in "kK":
                        j = int(name[-1])
                        cols, src = slice(j * KB, (j + 1) * KB), ring_ps[:, self.bank[f"K{j}"], 0:KB]
                        if name[0] == "k":
                            act.wait_ge(*self.after("pe", f"K{j}", n))
                            if j == 0 and nxt:
                                act.wait_ge(self.stacked[1 - u], REPLICA * (half + 1 if u else half))
                                wait_steps(act, n, self.at("pool", f"k2.{NJ - 1}", -1))
                            dst = part_sb[:, 0, cols]
                        else:
                            dst = key_sb[:, cols]
                        ins = act.activation(dst, src, ACT.Identity, bias=self.bkey)
                    elif name[0] == "V":
                        j = int(name[1:])
                        act.wait_ge(*self.after("pe", name, n))
                        src = ps[0:CK, :].rearrange("p (c k) -> p c k", c=CJ)
                        dst = val_sb[0:CK, u, j * CJ:(j + 1) * CJ, :].rearrange("p c (g k) -> p c g k", k=GW)
                        act.copy(dst[:, :, 0:4, 0:24], src[:, :, 0:96].rearrange("p c (g k) -> p c g k", k=24))
                        ins = act.copy(dst[:, :, 4:6, 0:16], src[:, :, 96:128].rearrange("p c (g k) -> p c g k", k=16))
                    elif name[0] == "E":
                        c = int(name[1:])
                        need = [self.at("pe", f"S{c}")]
                        if c < 2 and prev:
                            need.append(self.at("pe", f"PV{NC - 2 + c}", -1))
                        elif c >= 2:
                            need.append(self.at("pe", f"PV{c - 2}"))
                        wait_steps(act, n, *need)
                        dst = prob_sb[0:CK, c % 2, :].rearrange("p (h q) -> p h q", h=2)
                        ins = act.activation(dst, score_ps[0:CK, c % 2, :, 0:HALF], ACT.Exp)
                    else:
                        act.wait_ge(*self.after("pe", "MTb", n))
                        settle(act)
                        ins = act.copy(*self.shift(1, n))
                    self.done("act", ins, name)
                return emit

            def shift(self, half, n):
                rows = ring_ps[0:2, self.bank[("MTa", "MTb")[half]], :].rearrange("r (p k) -> r p k", p=4)[:, :, 0:QB]
                dst = qstack[SHIFT_ROW:SHIFT_ROW + 2, 0:PAIRS * B * QB].rearrange("r (p k) -> r p k", p=PAIRS)
                return dst[:, 4 * half:4 * half + 4, bass.ds(n * QB, QB)], rows

            def dve_step(self, dve):
                def view(base, off, dims):
                    return bass.AP(tensor=base.tensor, offset=base.offset + off, ap=[list(base.ap[0])] + dims)

                def emit(name, batch, prev, cur, nxt):
                    n, u, half = batch
                    ps_ot = ring_ps[0:LQ, self.bank["OT"], :]
                    if name[0] == "M":
                        j, p = (int(t) for t in name[1:].split("."))
                        dve.wait_ge(*self.after("pe", name, n))
                        ins = dve.tensor_reduce(max_sb[:, p, j:j + 1], ring_ps[:, self.bank[name], 0:KB], AX.X, ALU.max)
                    elif name == "maxall":
                        dve.wait_ge(*self.after("dve", self.mm[-1], n))
                        ins = dve.tensor_reduce(max1[:, :], max_sb[:, :, :], AX.X, ALU.max)
                    elif name == "maxb":
                        dve.wait_ge(*self.after("dve", "maxall", n))
                        ins = dve.tensor_scalar(maxb[:, :], max1[:, :], -1.0, None, ALU.mult)
                    elif name == "part0":
                        dve.wait_ge(*self.after("dve", "maxb", n))
                        ins = dve.tensor_copy(maxparts[:, :, 0], maxb[:, :])
                    elif name == "part1":
                        ins = dve.scalar_tensor_tensor(maxparts[:, :, 1], max1[:, :], -1.0, maxb[:, :],
                                                       ALU.mult, ALU.subtract)
                    elif name == "shift0":
                        dve.wait_ge(*self.after("pe", "MTa", n))
                        ins = dve.tensor_copy(*self.shift(0, n))
                    elif name == "O":
                        dve.wait_ge(*self.after("pe", f"PV{NC - 1}", n))
                        dve.tensor_copy(o_sb[:, 0:3 * LQ], oacc_ps[:, 0:3 * LQ])
                        ins = dve.tensor_copy(o_sb[0:64, 3 * LQ:5 * LQ], oacc_ps[0:64, 3 * LQ:5 * LQ])
                    elif name == "sum0":
                        dve.wait_ge(*self.after("pe", "OT", n))
                        ins = dve.reciprocal(view(osum_r[:, :], 0, [[1, 3], [3, 4]]),
                                             view(ps_ot, ONE, [[128, 3], [GW, 4]]))
                    elif name == "sum1":
                        ins = dve.reciprocal(view(osum_r[:, :], 12, [[1, 2], [2, 2]]),
                                             view(ps_ot, 384 + ONE, [[64, 2], [GW, 2]]))
                    elif name == "norm0":
                        dve.wait_ge(*self.after("dve", "sum1", n))
                        ins = dve.tensor_tensor(view(on_sb[:, :], 0, [[8, 3], [24, 4], [1, 8]]),
                                                view(ps_ot, 0, [[136, 3], [GW, 4], [1, 8]]),
                                                view(osum_r[:, :], 0, [[1, 3], [3, 4], [0, 8]]), ALU.mult)
                    elif name == "norm1":
                        ins = dve.tensor_tensor(view(on_sb[:, :], 96, [[8, 2], [16, 2], [1, 8]]),
                                                view(ps_ot, 384, [[72, 2], [GW, 2], [1, 8]]),
                                                view(osum_r[:, :], 12, [[1, 2], [2, 2], [0, 8]]), ALU.mult)
                    elif name == "OTT":
                        dve.wait_ge(*self.after("pe", "OTT", n))
                        ins = dve.tensor_scalar(by_batch(o_t)[:, n, :], ring_ps[:, self.bank["OTT"], 0:LQ], self.bval,
                                                None, ALU.add)
                    self.done("dve", ins, name)
                return emit

            def pool_step(self, pool):
                def emit(name, batch, prev, cur, nxt):
                    n, u, half = batch
                    if name == "norm":
                        if nxt:
                            pool.wait_ge(*self.after("pool", f"hat{NJ - 1}", n - 1))
                        at = 0 if self.modulated else 1
                        settle(pool)
                        ins = pool.tensor_copy(norm_now[:, :, :], norm_all[:, n, at:at + 2, :])
                    elif name[0:3] == "hat":
                        j = int(name[3:])
                        if j == 0:
                            pool.wait_ge(*self.after("pool", "norm", n))
                            pool.wait_ge(self.nat_loaded[u], 16 * (half + 1))
                            if nxt:
                                pool.wait_ge(*self.after("pe", f"T{NJ - 1}", n - 1))
                        settle(pool)
                        mean, scale = (1, 0) if self.modulated else (0, 1)
                        for c in range(j * CJ, (j + 1) * CJ):
                            ins = pool.tensor_scalar(hat_sb[:, c, :], nat_sb[0:CK, u, c, :], norm_now[:, mean, c:c + 1],
                                                    norm_now[:, scale, c:c + 1], ALU.add, ALU.mult)
                    else:
                        j = int(name[-1])
                        cols = slice(j * KB, (j + 1) * KB)
                        rest = key_sb[:, cols]
                        if name[0] == "r":
                            pool.wait_ge(*self.after("act", f"K{j}", n))
                            ins = pool.tensor_tensor(rest, rest, part_sb[:, 0, cols], ALU.subtract)
                        elif name[1] == "1":
                            pool.wait_ge(*self.after("pool", f"rest{j}", n))
                            settle(pool)
                            ins = pool.tensor_copy(part_sb[:, 1, cols], rest)
                        else:
                            pool.wait_ge(*self.after("pool", f"k1.{j}", n))
                            ins = pool.tensor_tensor(part_sb[:, 2, cols], rest, part_sb[:, 1, cols], ALU.subtract)
                    self.done("pool", ins, name)
                return emit

            def emitter(self, eng):
                return {"pe": self.pe_step, "act": self.act_step, "dve": self.dve_step, "pool": self.pool_step}[eng]

            def first_context(self, eng, engine, third=None):
                self.run(eng, engine, self.emitter(eng)(engine), None, None, None, (0, 0, 0), third)

            def clear_rows(self, pool, own_scores):
                pool.wait_ge(own_scores, B)
                pool.wait_ge(*self.after("pool", f"k2.{NJ - 1}", 0))
                pool.memset(qstack[SHIFT_ROW:SHIFT_ROW + 2, :].bitcast(F32), 0.0).then_inc(self.rows_clear, 1)
                pool.wait_ge(self.rows_clear, 1)

            def later(self, eng, engine):
                emit = self.emitter(eng)(engine)
                later_periods(lambda *batches: self.run(eng, engine, emit, *batches), engine)

            def load_nat(self, sp, n, u):
                sp.dma_start(nat_sb[0:CK, u, :, :], ctx_nat[n]).then_inc(self.nat_loaded[u], 16)

            def load_T(self, sp, n, u):
                sp.dma_start(self.context_T(u), ctx_T[n]).then_inc(self.loaded[u], 16)

            def sync_batch(self, sp, before, this):
                n, u, half = this
                last = isinstance(n, int) and n == B - 1
                if before and not last:
                    if self.hat:
                        sp.wait_ge(*self.after("pool", f"hat{NJ - 1}", before[0]))
                        self.load_nat(sp, n + 1, 1 - u)
                    else:
                        sp.wait_ge(*self.after("pe", f"V{NJ - 1}", before[0]))
                        self.load_T(sp, n + 1, 1 - u)
                if not isinstance(n, int) or n >= 2:
                    sp.wait_ge(*self.after("pe", f"S{NC - 1}", n - 2))
                for part, (eng, name) in enumerate((("act", "k0"), ("pool", "k1"), ("pool", "k2"))):
                    sp.wait_ge(*self.after(eng, f"{name}.{NJ - 1}", n))
                    stack_keys(sp, part_sb, part, u, slice(0, S), self.stacked[u])

            def sync_load(self, sp):
                if self.hat:
                    self.load_nat(sp, 0, 0)
                    self.load_nat(sp, 1, 1)
                else:
                    self.load_T(sp, 0, 0)
                    self.load_T(sp, 1, 1)

            def sync_later(self, sp):
                self.sync_batch(sp, (0, 0, 0), (1, 1, 0))
                with sp.Fori(0, (B - 4) // 2) as j:
                    self.sync_batch(sp, (2 * j + 1, 1, j), (2 * j + 2, 0, j + 1))
                    self.sync_batch(sp, (2 * j + 2, 0, j + 1), (2 * j + 3, 1, j + 1))
                self.sync_batch(sp, (B - 3, 1, B // 2 - 2), (B - 2, 0, B // 2 - 1))
                self.sync_batch(sp, (B - 2, 0, B // 2 - 1), (B - 1, 1, B // 2 - 1))

        class Own:
            def __init__(self, tag, wval, bval):
                self.wval, self.bval = wval, bval
                names = ("values_made", "values_in", "max_scores", "maxima", "max_parts", "shifts_turned", "shifts_in",
                         "scores", "probs", "attended", "sums", "normed", "turned", "finished", "rows_clear",
                         "shifts_placed", "queries_stacked", "keys_stacked")
                self.s = {n: sem(f"{tag}_{n}") for n in names}

            def tensor(self, pe, x_ready, meanwhile, meanwhile_read):
                s = self.s
                x_ready(pe)
                for b in range(B):
                    last = pe.matmul(score_ps[0:LQ, 0, b // 4, (b % 4) * D:(b % 4 + 1) * D], by_batch(xh_t)[:, b, :],
                                     self.wval, start=True, stop=True)
                last.then_inc(s["values_made"], 1)
                meanwhile(0)
                meanwhile(1)
                pe.wait_ge(s["values_in"], 2)
                pe.wait_ge(s["rows_clear"], 1)
                pe.wait_ge(s["queries_stacked"], REPLICA)
                pe.wait_ge(s["keys_stacked"], REPLICA)
                for k in range(B // 2):
                    pe.wait_ge(s["maxima"], k + 1)
                    for i in range(2):
                        n = 2 * k + i
                        for p in range(PAIRS):
                            last = pe.matmul(score_ps[:, k % 2, i, p * LQ:(p + 1) * LQ], queries(p, n, D),
                                             kstack[:, 1, p, n * LQ:(n + 1) * LQ], start=True, stop=True)
                    last.then_inc(s["max_scores"], 1)
                pe.wait_ge(s["max_parts"], 1)
                meanwhile_read(1)
                pe.transpose(ring_ps[:, 0, 0:D], own_maxparts[:, :, :, :].rearrange("r t p b -> r (t p b)"), ident[:, :])\
                    .then_inc(s["shifts_turned"], 1)

                def scores(n, r):
                    for p in range(PAIRS):
                        at = (p % 4) * 2 * LQ
                        last = pe.matmul(score_ps[:, r, p // 4, at:at + 2 * LQ], kstack[:, 1, p, n * LQ:n * LQ + D],
                                         queries(p, n), start=True, stop=True)
                    last.then_inc(s["scores"], 1)

                def pair(i, more):
                    pe.wait_ge(s["normed"], i + 1)
                    for r in range(2):
                        pe.wait_ge(s["probs"], 2 * i + r + 1)
                        for h in range(NH):
                            last = pe.matmul(oacc_ps[0:LQ, (r * NH + h) * OW:(r * NH + h + 1) * OW],
                                             prob_sb[0:LQ, r, h * LQ:(h + 1) * LQ], own_val[:, 2 * i + r, h, :],
                                             start=True, stop=True)
                        last.then_inc(s["attended"], 1)
                    if more:
                        for r in range(2):
                            scores(2 * i + 2 + r, r)
                    pe.wait_ge(s["normed"], i + 2)
                    pe.wait_ge(s["finished"], i + 1)
                    for r in range(2):
                        last = pe.transpose(ring_ps[:, 1, r * LQ:(r + 1) * LQ], own_out[:, r, :], ident[0:LQ, 0:LQ])
                    last.then_inc(s["turned"], 1)

                pe.wait_ge(s["shifts_in"], 1)
                meanwhile(2)
                pe.wait_ge(s["shifts_placed"], 16)
                for r in range(2):
                    scores(r, r)
                for i in range(B // 2):
                    pair(i, i < B // 2 - 1)

            def scalar(self, act, meanwhile):
                s = self.s
                act.wait_ge(s["values_made"], 1)
                for i in range(2):
                    act.copy(own_val[:, 4 * i:4 * i + 4, :, 0:HD],
                             score_ps[0:LQ, 0, i, :].rearrange("p (b h k) -> p b h k", b=4, k=HD))\
                        .then_inc(s["values_in"], 1)
                meanwhile(0)
                meanwhile(1)
                act.wait_ge(s["shifts_turned"], 1)
                act.copy(own_shift[:, :], ring_ps[:, 0, 0:QB])\
                    .then_inc(s["shifts_in"], 1)
                meanwhile(2)
                with act.Fori(0, B // 2) as i:
                    for r in range(2):
                        act.wait_ge(s["scores"], 2 * i + r + 1)
                        act.wait_ge(s["attended"], 2 * i + r + 1)
                        act.activation(prob_sb[0:LQ, r, :].rearrange("p (h q) -> p h q", h=2),
                                       score_ps[0:LQ, r, :, 0:HALF], ACT.Exp).then_inc(s["probs"], 1)

            def vector(self, dve):
                s = self.s
                for k in range(B // 2):
                    dve.wait_ge(s["max_scores"], k + 1)
                    dve.tensor_reduce(own_max[:, :, 2 * k:2 * k + 2].rearrange("r p b -> r b p"),
                                      score_ps[:, k % 2, :, 0:HALF].rearrange("r b (p k) -> r b p k", k=LQ),
                                      AX.X, ALU.max).then_inc(s["maxima"], 1)
                dve.wait_ge(s["maxima"], B // 2 + 2)
                dve.tensor_scalar(own_maxb[:, :, :], own_max[:, :, :], -1.0, None, ALU.mult).then_inc(s["maxima"], 1)
                dve.wait_ge(s["maxima"], B // 2 + 3)
                dve.tensor_copy(own_maxparts[:, 0, :, :], own_maxb[:, :, :])
                dve.scalar_tensor_tensor(own_maxparts[:, 1, :, :], own_max[:, :, :], -1.0, own_maxb[:, :, :], ALU.mult,
                                         ALU.subtract).then_inc(s["max_parts"], 1)
                with dve.Fori(0, B // 2) as i:
                    dve.wait_ge(s["attended"], 2 * i + 4)
                    ps = oacc_ps[0:LQ, 0:2 * NH * OW].rearrange("q (r h k) -> q r h k", r=2, k=OW)
                    dve.reciprocal(own_rec[:, :, :], ps[:, :, :, HD]).then_inc(s["sums"], 1)
                    dve.wait_ge(s["sums"], i + 1)
                    dve.tensor_tensor(own_out[:, :, :].rearrange("q r (h k) -> q r h k", k=HD), ps[:, :, :, 0:HD],
                                      own_rec[:, :, :].unsqueeze(3).broadcast_to([LQ, 2, NH, HD]),
                                      ALU.mult).then_inc(s["normed"], 1)
                    dve.wait_ge(s["turned"], i + 1)
                    dve.tensor_scalar(o_t[:, bass.ds(i * 2 * LQ, 2 * LQ)], ring_ps[:, 1, 0:2 * LQ], self.bval, None,
                                      ALU.add).then_inc(s["finished"], 1)

            def gpsimd(self, pool, rows_free, earlier):
                s = self.s
                for name, n in (("maxima", 2), ("attended", 2), ("normed", 1), ("finished", 1)):
                    pool.sem_inc(s[name], n)
                rows_free(pool)
                earlier(pool)
                pool.memset(qstack[SHIFT_ROW:SHIFT_ROW + 2, :].bitcast(F32), 0.0).then_inc(s["rows_clear"], 1)
                pool.wait_ge(s["rows_clear"], 1)

            def sync(self, sp, queries_ready, keys_ready, buffers_free):
                s = self.s
                buffers_free(sp)
                stack_queries(sp, queries_ready, s["queries_stacked"])
                for part in range(3):
                    keys_ready(sp, part)
                    stack_keys(sp, kpart_sb, part, 1, slice(0, NT), s["keys_stacked"])

            def sync_shifts(self, sp):
                s = self.s
                sp.wait_ge(s["shifts_in"], 1)
                sp.dma_start(qstack[SHIFT_ROW:SHIFT_ROW + 2, 0:PAIRS * B * QB].rearrange("r (k q) -> r k q", q=QB),
                             own_shift[:, :]).then_inc(s["shifts_placed"], 16)

        class Evidence:
            def __init__(self):
                self.pe = Periods(sem("ev_pe_done"), [("PT0", 0), ("PT1", 0), ("S", 1), ("U", 0)])
                self.act = Periods(sem("ev_act_done"), [("PT0", 0), ("PT1", 0), ("E", 1)])
                self.dve = Periods(sem("ev_dve_done"), [("rec", 0), ("max", 1), ("rep", 0), ("U", 0)])
                self.pool = Periods(sem("ev_pool_done"), [("q", 1)])
                self.loaded = [sem(f"ev_contextT_loaded{u}") for u in range(2)]
                self.nat_loaded = [sem(f"ev_context_loaded{u}") for u in range(2)]
                self.bank = {"PT0": 0, "PT1": 1, "U": 2}

            def context_T(self, u):
                return (part_flat if u else ctxT_sb[:, :])[:, 0:S]

            def probs(self, u):
                return (prob_flat if u else key_sb[:, :])[0:LQ, 0:S]

            def scores(self):
                return score_ps[0:LQ, :, :, :].rearrange("p a b c -> p (a b) c")[:, 0:NJ, 0:KB]

            def tensor(self, pe, before):
                P, A, V, G = self.pe, self.act, self.dve, self.pool
                before(pe)

                def body(cur, nxt):
                    P.start(pe, {0: cur, 1: nxt})
                    if cur:
                        n, u, half = cur
                        pe.wait_ge(V.sem, V.after("rec", n))
                        settle(pe)
                        for i in range(2):
                            for c in range(6):
                                k0 = (6 * i + c) * CK
                                last = pe.transpose(ring_ps[0:CK, self.bank[f"PT{i}"], c * LQ:(c + 1) * LQ],
                                                    self.probs(u)[:, k0:k0 + CK], ident[0:LQ, 0:LQ])
                            P.done(last, f"PT{i}")
                    if nxt:
                        n, u, half = nxt
                        pe.wait_ge(self.loaded[u], 16 * (half + 1))
                        pe.wait_ge(G.sem, G.after("q", n))
                        for j in range(NJ):
                            last = pe.matmul(self.scores()[:, j, :], xslice[:, u, :],
                                             self.context_T(u)[:, j * KB:(j + 1) * KB], start=True, stop=True)
                        P.done(last, "S")
                    if cur:
                        n, u, half = cur
                        pe.wait_ge(A.sem, A.after("PT1", n))
                        pe.wait_ge(self.nat_loaded[u], 16 * (half + 1))
                        for c in range(NC):
                            pe.matmul(ring_ps[:, self.bank["U"], 0:LQ], nat_sb[0:CK, u, c, :],
                                      hat_sb[:, c, 0:LQ], start=(c == 0), stop=(c == NC - 1))
                        P.done(pe.matmul(ring_ps[:, self.bank["U"], 64:64 + LQ], s_rec[:, 0:1].broadcast_to([LQ, D]),
                                         ident[0:LQ, 0:LQ], start=True, stop=True), "U")
                    P.end()

                periods(pe, body)

            def scalar(self, act):
                P, A, V = self.pe, self.act, self.dve

                def body(cur, nxt):
                    A.start(act, {0: cur, 1: nxt})
                    if cur:
                        n, u, half = cur
                        for i in range(2):
                            act.wait_ge(P.sem, P.after(f"PT{i}", n))
                            src = ring_ps[0:CK, self.bank[f"PT{i}"], 0:6 * LQ].rearrange("p (c q) -> p c q", q=LQ)
                            A.done(act.copy(hat_sb[:, 6 * i:6 * i + 6, 0:LQ], src), f"PT{i}")
                    if nxt:
                        n, u, half = nxt
                        act.wait_ge(V.sem, V.after("max", n))
                        A.done(act.activation(self.probs(u).rearrange("p (j k) -> p j k", j=NJ), self.scores(),
                                              ACT.Exp, bias=s_max[:, u, :], accum_out=s_sum[:, u, :]), "E")
                    A.end()

                periods(act, body)

            def vector(self, dve):
                P, A, V = self.pe, self.act, self.dve

                def body(cur, nxt):
                    V.start(dve, {0: cur, 1: nxt})
                    if cur:
                        n, u, half = cur
                        dve.wait_ge(A.sem, A.after("E", n))
                        V.done(dve.reciprocal(s_rec[:, :], s_sum[:, u, :]), "rec")
                    if nxt:
                        n, u, half = nxt
                        dve.wait_ge(P.sem, P.after("S", n))
                        V.done(dve.tensor_reduce(s_max[:, u, :], self.scores(), AX.XY, ALU.max, negate=True), "max")
                    if cur:
                        n, u, half = cur
                        dve.wait_ge(P.sem, P.after("U", n))
                        V.done(dve.tensor_copy(sum_rep[:, :], ring_ps[:, self.bank["U"], 64:64 + LQ]), "rep")
                        dve.wait_ge(V.sem, V.after("rep", n))
                        V.done(dve.tensor_tensor(by_batch(o_t)[:, n, :], ring_ps[:, self.bank["U"], 0:LQ], sum_rep[:, :],
                                                 ALU.mult), "U")
                    V.end()

                periods(dve, body)

            def gpsimd(self, pool, before):
                P, G = self.pe, self.pool
                before(pool)

                def body(cur, nxt):
                    G.start(pool, {0: cur, 1: nxt})
                    if nxt:
                        n, u, half = nxt
                        if cur:
                            pool.wait_ge(P.sem, P.after("S", cur[0]))
                            settle(pool)
                        G.done(pool.tensor_copy(xslice[:, u, :], by_batch(q_t)[:, n, :]), "q")
                    G.end()

                periods(pool, body)

            def sync(self, sp):
                P = self.pe
                for u in range(2):
                    sp.dma_start(self.context_T(u), ctx_T[u]).then_inc(self.loaded[u], 16)
                    sp.dma_start(nat_sb[0:CK, u, :, :], ctx_nat[u]).then_inc(self.nat_loaded[u], 16)

                def body(cur, nxt):
                    if not cur or isinstance(cur[0], int) and cur[0] >= B - 2:
                        return
                    n, u, half = cur
                    sp.wait_ge(P.sem, P.after("S", n))
                    sp.dma_start(self.context_T(u), ctx_T[n + 2]).then_inc(self.loaded[u], 16)
                    sp.wait_ge(P.sem, P.after("U", n))
                    sp.dma_start(nat_sb[0:CK, u, :, :], ctx_nat[n + 2]).then_inc(self.nat_loaded[u], 16)

                periods(sp, body)

        class Dense:

            def __init__(self, tag, products, curves, values):
                self.pe = Ticks(sem(f"{tag}_pe_done"), [p[0] for p in products])
                self.act = Ticks(sem(f"{tag}_act_done"), curves)
                self.dve = Ticks(sem(f"{tag}_dve_done"), values)
                self.pool = Ticks(sem(f"{tag}_pool_done"), [v.replace(".vs", ".rs") for v in values if v.endswith(".vs")])
                self.products = products

            def ps(self, name):
                return ring_ps[:, self.pe.names.index(name) % RING, 0:NT]

            def product(self, pe, name, pairs, out=None):
                i = self.pe.names.index(name)
                if i >= RING:
                    _, reader, step = self.products[i - RING]
                    plan = self.act if reader == "act" else self.dve
                    pe.wait_ge(plan.sem, plan.after(step))
                for k, (lhsT, rhs) in enumerate(pairs):
                    last = pe.matmul(self.ps(name) if out is None else out, lhsT, rhs, start=(k == 0),
                                     stop=(k == len(pairs) - 1))
                self.pe.done(last, name)

            @staticmethod
            def ln_products(t):
                return [(f"{t}.mean", "dve", f"{t}.xc"), (f"{t}.var", "dve", f"{t}.vs"), (f"{t}.rep", "dve", f"{t}.xh")]

            @staticmethod
            def ln_values(t):
                return [f"{t}.xc", f"{t}.sq", f"{t}.vs", f"{t}.xh"]

            def ln_pe(self, pe, t, x_ready):
                if x_ready:
                    pe.wait_ge(self.dve.sem, self.dve.after(x_ready))
                self.product(pe, f"{t}.mean", [(mean_mat[:, :], x_t)])
                pe.wait_ge(self.dve.sem, self.dve.after(f"{t}.sq"))
                i = self.pe.names.index(f"{t}.var")
                if i >= RING:
                    _, _, step = self.products[i - RING]
                    pe.wait_ge(self.dve.sem, self.dve.after(step))
                for c in range(4):
                    last = pe.matmul(self.ps(f"{t}.var")[0:TOK, c:c + 1], T(6)[:, c * TOK:(c + 1) * TOK],
                                     mean_mat[:, 0:1], start=True, stop=True)
                self.pe.done(last, f"{t}.var")
                pe.wait_ge(self.pool.sem, self.pool.after(f"{t}.rs"))
                i = self.pe.names.index(f"{t}.rep")
                if i >= RING:
                    _, _, step = self.products[i - RING]
                    pe.wait_ge(self.dve.sem, self.dve.after(step))
                for c in range(4):
                    last = pe.matmul(self.ps(f"{t}.rep")[:, c * TOK:(c + 1) * TOK],
                                     tok_rstd[:, c:c + 1].broadcast_to([TOK, D]), ident[0:TOK, 0:TOK],
                                     start=True, stop=True)
                self.pe.done(last, f"{t}.rep")

            def ln_pool(self, pool, t):
                pool.wait_ge(self.dve.sem, self.dve.after(f"{t}.vs"))
                self.pool.done(pool.tensor_tensor(tok_rstd[:, :], tok_var[:, :], minus_half[:, :], ALU.pow), f"{t}.rs")

            def step(self, dve, ins, name):
                self.dve.done(ins, name)
                dve.wait_ge(self.dve.sem, self.dve.after(name))

            def ln_dve(self, dve, t, eps, meanwhile=None):
                dve.wait_ge(self.pe.sem, self.pe.after(f"{t}.mean"))
                self.step(dve, dve.tensor_tensor(xc_t, x_t, self.ps(f"{t}.mean"), ALU.subtract), f"{t}.xc")
                self.step(dve, dve.tensor_tensor(T(6), xc_t, xc_t, ALU.mult), f"{t}.sq")
                if meanwhile:
                    meanwhile()
                dve.wait_ge(self.pe.sem, self.pe.after(f"{t}.var"))
                self.step(dve, dve.tensor_scalar(tok_var[:, :], self.ps(f"{t}.var")[0:TOK, 0:4], eps, None, ALU.add),
                          f"{t}.vs")
                dve.wait_ge(self.pe.sem, self.pe.after(f"{t}.rep"))
                self.step(dve, dve.tensor_tensor(xh_t, xc_t, self.ps(f"{t}.rep"), ALU.mult), f"{t}.xh")

            def split(self, dve, x, parts, t):
                self.step(dve, dve.tensor_copy(parts[0], x), f"{t}.0")
                self.step(dve, dve.tensor_tensor(T(6), x, parts[0], ALU.subtract), f"{t}.r")
                self.step(dve, dve.tensor_copy(parts[1], T(6)), f"{t}.1")
                self.step(dve, dve.tensor_tensor(parts[2], T(6), parts[1], ALU.subtract), f"{t}.2")

            def to_blocks(self, act):
                for part in range(3):
                    act.wait_ge(self.dve.sem, self.dve.after(f"q.{'012'[part]}"))
                    for e in range(2):
                        half = slice(64 * e, 64 * e + 64)
                        self.act.done(act.copy(qpart_sb[half, part, :, e, :], by_batch(qsplit_sb[half, part, :])),
                                      f"b{part}{e}")

            def modulate(self, dve, scale, shift, t):
                self.step(dve, dve.tensor_tensor(by_batch(xh_t), by_batch(xh_t), mod(scale), ALU.mult), f"{t}.scaled")
                self.step(dve, dve.tensor_tensor(by_batch(xh_t), by_batch(xh_t), mod(shift), ALU.add), f"{t}.shifted")

            def gated(self, dve, y, gate, t):
                self.step(dve, dve.tensor_tensor(by_batch(y), by_batch(y), mod(gate), ALU.mult), f"{t}.gated")
                self.step(dve, dve.tensor_tensor(x_t, x_t, y, ALU.add), f"{t}.x")

        L = Dense
        BLOCKS = [f"b{part}{e}" for part in range(3) for e in range(2)]
        d0 = Dense("d0", [("mods", "dve", "mods"), *L.ln_products("ln"), ("q", "dve", "q")],
                   ["tanh", "c.sd", "c.sd2", *BLOCKS],
                   ["half", "silu", "mods", "scales", *L.ln_values("ln"), "m.scaled", "m.shifted",
                    "c.negmean", "c.rs", "c.rs2", "q", *[f"q.{s}" for s in "0r12"]])
        att0 = Heads("att0", w("L0_Wkv", 0, 0, 128), w("L0_Wkv", 0, 128, 128), vec("L0_bkv", 0), vec("L0_bkv", 1),
                     hat=True, modulated=True)
        d1 = Dense("d1", [("proj", "dve", "x"), *L.ln_products("ln"), ("q", "dve", "q"), ("qk", "dve", "qk"),
                         ("anchors", "dve", "anchors")],
                   [], ["x", *L.ln_values("ln"), "nx", "q", "qk", "anchors"])
        evi = Evidence()
        H = [(e, r) for e in range(E_N) for r in range(2)]

        def own_products(t):
            return [*L.ln_products(t), (f"{t}.q", "dve", f"{t}.q"), (f"{t}.k", "dve", f"{t}.k")]

        def own_values(t):
            return [*L.ln_values(t), f"{t}.scaled", f"{t}.shifted", f"{t}.q", *[f"q.{s}" for s in "0r12"], f"{t}.k", *[f"k.{s}" for s in "0r12"]]

        d2 = Dense("d2", [("ev", "dve", "ev"), *[(f"l{e}", "dve", f"l{e}") for e in range(E_N)],
                          ("g1", "dve", "gu"), ("g2", "act", "gt2"),
                          *[(f"u{e}{r}", "dve", f"u{e}{r}") for e, r in H],
                          *[(f"o{e}", "dve", f"o{e}") for e in range(E_N)],
                          ("out", "dve", "outg"), *own_products("own")],
                   ["gt", *[f"p{e}" for e in range(E_N)], "gt2", *[f"t{e}{r}" for e, r in H], *BLOCKS],
                   ["ev", *[f"l{e}" for e in range(E_N)], "m01", "m", *[f"d{e}" for e in range(E_N)],
                    "gu", "gh", "s01", "s", "r", *[f"p{e}" for e in range(E_N)], "g",
                    *[f"u{e}{r}" for e, r in H], *[f"h{e}{r}" for e, r in H],
                    "o0", "r0", "o1", "r1", "a1", "o2", "r2", "a2", "outg", "x", *own_values("own")])
        att_own = {"L2": Own("own2", w("L2_W_qkv", 0, 256, 128), vec("L2_b_qkv", 2)),
                   "L3": Own("own3", w("L3_qkv_w", 0, 256, 128), vec("L3_qkv_b", 2))}
        att_ctx = {"L2": Heads("att2", w("L2_W_kvc", 0, 0, 128), w("L2_W_kvc", 0, 128, 128), vec("L2_b_kvc", 0),
                               vec("L2_b_kvc", 1), hat=True),
                   "L3": Heads("att3", w("L3_kv_w", 0, 0, 128), w("L3_kv_w", 0, 128, 128), vec("L3_kv_b", 0),
                               vec("L3_kv_b", 1), hat=False)}
        NAMES = {"L2": dict(qkv="L2_W_qkv", qkv_b="L2_b_qkv", proj="L2_W_proj", proj_b="L2_b_proj", q="L2_W_qc",
                            q_b="L2_b_qc", cproj="L2_W_cproj", cproj_b="L2_b_cproj", w1="L2_W_mlp1", b1="L2_b_mlp1",
                            w2="L2_W_mlp2", b2="L2_b_mlp2"),
                 "L3": dict(qkv="L3_qkv_w", qkv_b="L3_qkv_b", proj="L3_sa_proj_w", proj_b="L3_sa_proj_b", q="L3_q_w",
                            q_b="L3_q_b", cproj="L3_ca_proj_w", cproj_b="L3_ca_proj_b", w1="L3_fc1_w", b1="L3_fc1_b",
                            w2="L3_fc2_w", b2="L3_fc2_b")}
        d_mid = {l: Dense(f"dm{l}", [("proj", "dve", "y"), *L.ln_products("ln"), ("q", "dve", "q")], BLOCKS,
                          ["y", "y.gated", "y.x", *L.ln_values("ln"), "q", *[f"q.{s}" for s in "0r12"]]) for l in ("L2", "L3")}
        J4 = range(4)

        def end_part(l, follow):
            return Dense(f"de{l}", [("proj", "dve", "x"), *L.ln_products("ln"), *[(f"u{j}", "dve", f"u{j}") for j in J4],
                                    ("y", "dve", "y"), *(own_products("own") if follow else [])],
                         [*[f"sq{j}" for j in J4], *[f"t{j}" for j in J4], *(BLOCKS if follow else [])],
                         ["x", *L.ln_values("ln"), "m.scaled", "m.shifted",
                          *[f"{s}{j}" for s in ("u", "in", "h") for j in J4],
                          "y", "y.gated", "y.x", *(own_values("own") if follow else [])])

        d_end = {"L2": end_part("L2", True), "L3": end_part("L3", False)}

        def own_pe(d, pe, l, x_ready):
            d.ln_pe(pe, "own", x_ready)
            pe.wait_ge(d.dve.sem, d.dve.after("own.shifted"))
            d.product(pe, "own.q", [(w(NAMES[l]["qkv"], 0, 0, 128), xh_t)])
            d.product(pe, "own.k", [(w(NAMES[l]["qkv"], 0, 128, 128), xh_t)])

        def own_dve(d, dve, l):
            d.ln_dve(dve, "own", 1e-6)
            d.modulate(dve, f"{l}.scale_a", f"{l}.shift_a", "own")
            dve.wait_ge(d.pe.sem, d.pe.after("own.q"))
            d.step(dve, dve.tensor_scalar(q_t, d.ps("own.q"), vec(NAMES[l]["qkv_b"], 0), HD ** -0.5, ALU.add, ALU.mult),
                   "own.q")
            d.split(dve, q_t, [qsplit_sb[:, i, :] for i in range(3)], "q")
            dve.wait_ge(d.pe.sem, d.pe.after("own.k"))
            d.step(dve, dve.tensor_scalar(k_t, d.ps("own.k"), vec(NAMES[l]["qkv_b"], 1), None, ALU.add), "own.k")
            d.split(dve, k_t, [kpart_sb[:, i, :] for i in range(3)], "k")

        def anchored(k, c):
            name, block, _, _ = ANCHORED[k]
            if name == "L1_router_W":
                return w(name, c, block, 1).broadcast_to([D, D])
            if name == "L1_gate_w1":
                return w(name, c)
            return w(name, 3 * block[0] + c, block[1] * D, D)

        def anchor(k):
            return anchors[:, k, :].unsqueeze(2).broadcast_to([D, B, LQ])

        def last_output(att):
            if isinstance(att, Own):
                return att.s["finished"], B // 2 + 1
            if isinstance(att, Heads):
                return att.after("dve", "OTT", B - 1)
            return att.dve.sem, att.dve.after("U", B - 1)

        def ready(d, name):
            return lambda eng, part="": eng.wait_ge(d.dve.sem, d.dve.after(f"{name}{part}"))

        def queries_ready(d):
            return lambda eng, part: eng.wait_ge(d.act.sem, d.act.after(f"b{part}1"))

        a0, a2, a3 = att0, att_ctx["L2"], att_ctx["L3"]
        own2, own3 = att_own["L2"], att_own["L3"]
        buffers_ready = sem("buffers_ready")
        ones_placed = sem("ones_placed")
        stats_loaded = [sem(f"statistics_context_loaded{u}") for u in range(3)]
        stats_done = sem("statistics_done")

        def stats_buffer(u):
            return nat_sb[0:CK, u, :, :] if u < 2 else hat_sb[:, :, :]

        stats_joined = sem("statistics_joined")
        stats_kept = sem("statistics_kept")

        loaded_early = sem("condition_and_constants_loaded")
        loaded_w0 = sem("first_weights_loaded")
        loaded_w1 = sem("other_weights_loaded")
        loaded_w3 = sem("last_weights_loaded")
        loaded_x = sem("tokens_loaded")
        stored = sem("output_stored")

        block = ctx.enter_context(nc.Block())

        @block.sync
        def _(sp):
            w0 = W_AT["L1_Wq"][0]
            sp.dma_start(cond_sb[:, :], cond_T).then_inc(loaded_early, 16)
            sp.dma_start(vec_sb[:, :], vectors).then_inc(loaded_early, 16)
            sp.dma_start(ident[:, :], identity).then_inc(loaded_early, 16)
            with sp.Fori(0, (B - 2) // 3) as j:
                for u in range(3):
                    sp.wait_ge(stats_done, 3 * j + u + 1)
                    sp.dma_start(stats_buffer(u), ctx_nat[3 * j + 2 + u]).then_inc(stats_loaded[u], 16)
            sp.dma_start(w_sb[:, 0:w0], weights[:, 0:w0]).then_inc(loaded_w0, 16)
            sp.dma_start(x_t, x_T).then_inc(loaded_x, 16)
            for u in range(2):
                sp.wait_ge(stats_done, B - 5 + u + 4)
                a0.load_nat(sp, u, u)
            sp.wait_ge(buffers_ready, BUFFERS)
            for u in range(2):
                sp.dma_start(kstack[SHIFT_ROW:SHIFT_ROW + 2, u, :, :],
                             part_sb[0:2, 0, :].unsqueeze(1).broadcast_to([2, PAIRS, S])).then_inc(ones_placed, 16)
            w1 = w0
            sp.dma_start(w_sb[:, w1:W_L3], weights[:, w1:W_L3]).then_inc(loaded_w1, 16)
            stack_queries(sp, queries_ready(d0), a0.qstacked)
            a0.sync_batch(sp, None, (0, 0, 0))
            a0.sync_later(sp)
            sp.wait_ge(*a0.after("pe", f"S{NC - 1}", B - 1))
            evi.sync(sp)
            sp.wait_ge(*last_output(evi))
            a2.sync_load(sp)
            own2.sync(sp, queries_ready(d2), ready(d2, "k."), ready(d2, "own.xc"))
            sp.dma_start(w_sb[:, w1:w1 + L3_COLS], weights[:, W_L3:W_L3 + L3_COLS]).then_inc(loaded_w3, 16)
            own2.sync_shifts(sp)
            a2.sync_batch(sp, None, (0, 0, 0))
            stack_queries(sp, queries_ready(d_mid["L2"]), a2.qstacked)
            a2.sync_later(sp)
            sp.wait_ge(*a2.after("pe", f"S{NC - 1}", B - 1))
            a3.sync_load(sp)
            own3.sync(sp, queries_ready(d_end["L2"]), ready(d_end["L2"], "k."), lambda eng: None)
            own3.sync_shifts(sp)
            a3.sync_batch(sp, None, (0, 0, 0))
            stack_queries(sp, queries_ready(d_mid["L3"]), a3.qstacked)
            a3.sync_later(sp)
            d = d_end["L3"]
            sp.wait_ge(d.dve.sem, d.dve.after("y.x"))
            sp.dma_start(out, x_t).then_inc(stored, 16)
            sp.wait_ge(stored, 16)

        @block.gpsimd
        def _(pool):
            pool.memset(mean_mat[:, :], 1.0 / D).then_inc(consts_ready, 1)
            pool.memset(eps_sb[:, 0:1], 1e-5).then_inc(consts_ready, 1)
            pool.memset(eps_sb[:, 1:2], 1e-6).then_inc(consts_ready, 1)
            pool.wait_ge(consts_ready, 3)
            pool.memset(minus_half[:, :], -0.5).then_inc(consts_ready, 1)
            pool.wait_ge(consts_ready, 4)
            pool.memset(qstack[:, :].bitcast(F32), 0.0).then_inc(buffers_ready, 1)
            pool.wait_ge(buffers_ready, 1)
            pool.memset(kstack[96:128, :, :, :].bitcast(F32), 0.0).then_inc(buffers_ready, 1)
            pool.wait_ge(buffers_ready, 2)
            pool.memset(part_sb[0:2, 0, :], 1.0).then_inc(buffers_ready, 1)
            pool.wait_ge(buffers_ready, 3)
            pool.memset(own_val[:, :, :, :], 1.0).then_inc(buffers_ready, 1)
            pool.wait_ge(buffers_ready, 4)
            pool.memset(val_sb[:, :, :, :], 0.0).then_inc(buffers_ready, 1)
            pool.wait_ge(buffers_ready, 5)
            for u in range(2):
                pool.memset(val_sb[:, u, :, :].rearrange("p c (g k) -> p (c g) k", k=GW)[:, :, ONE:ONE + 1], 1.0)\
                    .then_inc(buffers_ready, 1)
            pool.wait_ge(buffers_ready, 7)
            pool.memset(qpart_sb[:, :, :, :, :], 0.0).then_inc(buffers_ready, 1)
            pool.wait_ge(buffers_ready, BUFFERS)
            pool.sem_inc(a0.rows_clear, 1)
            d0.ln_pool(pool, "ln")
            pool.wait_ge(loaded_early, 48)
            ready(d0, "c.rs2")(pool)
            a0.first_context("pool", pool)
            a0.later("pool", pool)
            d1.ln_pool(pool, "ln")
            evi.gpsimd(pool, ready(d1, "qk"))
            own2.gpsimd(pool, lambda eng: eng.wait_ge(*last_output(evi)),
                        lambda eng: eng.wait_ge(evi.pool.sem, evi.pool.after("q", B - 1)))
            d2.ln_pool(pool, "own")
            a2.first_context("pool", pool)
            a2.clear_rows(pool, own2.s["scores"])
            d_mid["L2"].ln_pool(pool, "ln")
            a2.later("pool", pool)
            own3.gpsimd(pool, lambda eng: eng.wait_ge(*a2.after("pe", f"S{NC - 1}", B - 1)),
                        lambda eng: eng.wait_ge(*a2.after("pool", f"k2.{NJ - 1}", B - 1)))
            for t in ("ln", "own"):
                d_end["L2"].ln_pool(pool, t)
            a3.first_context("pool", pool)
            a3.clear_rows(pool, own3.s["scores"])
            d_mid["L3"].ln_pool(pool, "ln")
            a3.later("pool", pool)
            d_end["L3"].ln_pool(pool, "ln")

        @block.tensor
        def _(pe):
            pe.wait_ge(consts_ready, CONSTS)
            pe.wait_ge(loaded_early, 48)
            d = d0
            pe.wait_ge(loaded_w0, 16)
            pe.wait_ge(d.dve.sem, d.dve.after("silu"))
            for i, (_, name, _, j) in enumerate(MODS):
                last = pe.matmul(d.ps("mods")[:, i * B:(i + 1) * B], w(name, 0, j * D, D), cond_silu[:, :],
                                 start=True, stop=True)
            d.pe.done(last, "mods")
            pe.wait_ge(loaded_x, 16)
            d.ln_pe(pe, "ln", None)
            pe.wait_ge(d.dve.sem, d.dve.after("m.shifted"))
            d.product(pe, "q", [(w("L0_Wq"), xh_t)])
            pe.wait_ge(d.dve.sem, d.dve.after("q"))
            a0.first_context("pe", pe)
            pe.wait_ge(ones_placed, 32)
            a0.later("pe", pe)
            d = d1
            pe.wait_ge(*last_output(att0))
            pe.wait_ge(loaded_w1, 16)
            d.product(pe, "proj", [(w("L0_Wp"), o_t)])
            d.ln_pe(pe, "ln", "x")
            pe.wait_ge(d.dve.sem, d.dve.after("nx"))
            d.product(pe, "q", [(w("L1_Wq"), xh_t)])
            pe.wait_ge(d.dve.sem, d.dve.after("q"))
            d.product(pe, "qk", [(w("L1_WkT"), k_t)])
            pe.wait_ge(d.dve.sem, d.dve.after("ln.xh"))
            for k in range(len(ANCHORED)):
                last = pe.matmul(d.ps("anchors")[:, k * B:(k + 1) * B], anchored(k, 2), cond_sb[:, :], start=True,
                                 stop=True)
            d.pe.done(last, "anchors")
            evi.tensor(pe, lambda eng: eng.wait_ge(d1.dve.sem, d1.dve.after("qk")))
            d = d2
            pe.wait_ge(*last_output(evi))
            d.product(pe, "ev", [(w("L1_Wv"), o_t)])
            pe.wait_ge(d.dve.sem, d.dve.after("ev"))
            combined = (xh_t, ev_t)
            for e in range(E_N):
                d.product(pe, f"l{e}", [(anchored(e, c), combined[c]) for c in range(2)])
            d.product(pe, "g1", [(anchored(E_N, c), combined[c]) for c in range(2)])
            pe.wait_ge(d.dve.sem, d.dve.after("gh"))
            d.product(pe, "g2", [(w("L1_gate_w2"), T(8))])
            for e, r in H:
                d.product(pe, f"u{e}{r}", [(anchored(E_N + 1 + 2 * e + r, c), combined[c]) for c in range(2)])
            for e in range(E_N):
                pe.wait_ge(d.dve.sem, d.dve.after(f"h{e}1"))
                d.product(pe, f"o{e}", [(w("L1_e_w2", 2 * e + r), hidden[2 * e + r]) for r in range(2)])
            pe.wait_ge(d.dve.sem, d.dve.after("a2"))
            d.product(pe, "out", [(w("L1_out_w"), T(14))])
            own_pe(d, pe, "L2", "x")
            pe.wait_ge(d.dve.sem, d.dve.after("own.k"))
            own2.tensor(pe, ready(d2, "own.k"), lambda i: a2.first_context("pe", pe, i),
                        lambda i: pe.wait_ge(*a2.after("act", ("T2", "K2", "V2")[i], 0)))
            for l in ("L2", "L3"):
                d, nm = d_mid[l], NAMES[l]
                pe.wait_ge(*last_output(att_own[l]))
                d.product(pe, "proj", [(w(nm["proj"]), o_t)])
                d.ln_pe(pe, "ln", "y.x")
                pe.wait_ge(d.dve.sem, d.dve.after("ln.xh"))
                d.product(pe, "q", [(w(nm["q"]), xh_t)])
                pe.wait_ge(d.dve.sem, d.dve.after("q"))
                att_ctx[l].later("pe", pe)
                d = d_end[l]
                pe.wait_ge(*last_output(att_ctx[l]))
                d.product(pe, "proj", [(w(nm["cproj"]), o_t)])
                d.ln_pe(pe, "ln", "x")
                pe.wait_ge(d.dve.sem, d.dve.after("m.shifted"))
                for j in J4:
                    d.product(pe, f"u{j}", [(w(nm["w1"], 0, j * D, D), xh_t)])
                pe.wait_ge(d.dve.sem, d.dve.after("h3"))
                d.product(pe, "y", [(w(nm["w2"], j), T(8 + j)) for j in J4])
                if l == "L2":
                    pe.wait_ge(loaded_w3, 16)
                    own_pe(d, pe, "L3", "y.x")
                    pe.wait_ge(d.dve.sem, d.dve.after("own.k"))
                    own3.tensor(pe, ready(d, "own.k"), lambda i: a3.first_context("pe", pe, i),
                                lambda i: i and pe.wait_ge(*a3.after("act", ("", "K2", "V2")[i], 0)))

        @block.scalar
        def _(act):
            d = d0
            act.wait_ge(consts_ready, CONSTS)
            act.wait_ge(loaded_early, 48)
            d.act.done(act.activation(cond_t[:, :], cond_sb[:, :], ACT.Tanh, scale=0.5), "tanh")
            act.wait_ge(stats_kept, B + 1)
            d.act.done(act.activation(norm_all[:, :, 0, :], ctx_mv[:, :, :, 1], ACT.Sqrt, bias=eps_sb[0:CK, 0:1]),
                       "c.sd")
            d.act.done(act.activation(norm_all[:, :, 2, :], ctx_mv[:, :, :, 1], ACT.Sqrt, bias=eps_sb[0:CK, 1:2]),
                       "c.sd2")
            act.wait_ge(buffers_ready, BUFFERS)
            d.to_blocks(act)
            act.wait_ge(ones_placed, 32)
            a0.first_context("act", act)
            a0.later("act", act)
            evi.scalar(act)
            d = d2
            act.wait_ge(d.dve.sem, d.dve.after("gu"))
            d.act.done(act.activation(T(12), T(8), ACT.Tanh, scale=0.5), "gt")
            for e in range(E_N):
                act.wait_ge(d.dve.sem, d.dve.after(f"d{e}"))
                d.act.done(act.activation(logit[e], logit[e], ACT.Exp), f"p{e}")
            act.wait_ge(d.pe.sem, d.pe.after("g2"))
            d.act.done(act.activation(T(12), d.ps("g2"), ACT.Tanh, scale=0.25, bias=vec("L1_gate_b2", 0, half=True)),
                       "gt2")
            for i, (e, r) in enumerate(H):
                act.wait_ge(d.dve.sem, d.dve.after(f"u{e}{r}"))
                d.act.done(act.activation(curve[i], hidden[i], ACT.Tanh, scale=0.5), f"t{e}{r}")
            d.to_blocks(act)
            own2.scalar(act, lambda i: a2.first_context("act", act, i))
            for l in ("L2", "L3"):
                d_mid[l].to_blocks(act)
                att_ctx[l].later("act", act)
                d = d_end[l]
                for j in J4:
                    act.wait_ge(d.dve.sem, d.dve.after(f"u{j}"))
                    d.act.done(act.activation(scratch(j), T(8 + j), ACT.Square, scale=GELU_CUBE ** 0.5), f"sq{j}")
                for j in J4:
                    act.wait_ge(d.dve.sem, d.dve.after(f"in{j}"))
                    d.act.done(act.activation(scratch(j), scratch(j), ACT.Tanh, scale=GELU_IN), f"t{j}")
                if l == "L2":
                    d.to_blocks(act)
                    own3.scalar(act, lambda i: a3.first_context("act", act, i))

        @block.vector
        def _(dve):
            d = d0
            dve.sem_inc(stats_done, 3)
            dve.sem_inc(stats_kept, 1)
            dve.wait_ge(consts_ready, CONSTS)
            dve.wait_ge(loaded_early, 48)
            d.step(dve, dve.tensor_scalar(vec_half[:, :], vec_sb[:, :], 0.5, None, ALU.mult), "half")
            dve.wait_ge(d.act.sem, d.act.after("tanh"))
            d.step(dve, dve.scalar_tensor_tensor(cond_silu[:, :], cond_t[:, :], 1.0, cond_sb[:, :], ALU.add, ALU.mult),
                   "silu")

            def statistics(u, n, k):
                dve.wait_ge(stats_kept, k + 1)
                for c in range(NC):
                    last = dve.bn_stats(bn_tmp[:, c, :], stats_buffer(u)[:, c, :])
                last.then_inc(stats_done, 1)
                dve.wait_ge(stats_done, k + 4)
                settle(dve)
                for c in range(NC):
                    last = dve.bn_aggr(mv_now[:, c, :], bn_tmp[:, c, :])
                last.then_inc(stats_joined, 1)
                dve.wait_ge(stats_joined, k + 1)
                dve.tensor_copy(ctx_mv[:, n, :, :], mv_now[:, :, :]).then_inc(stats_kept, 1)

            with dve.Fori(0, (B - 2) // 3) as j:
                for u in range(3):
                    dve.wait_ge(stats_loaded[u], 16 * (j + 1))
                    settle(dve)
                    statistics(u, 3 * j + 2 + u, 3 * j + u)

            def last_statistics(u):
                dve.wait_ge(a0.nat_loaded[u], 16)
                statistics(u, u, B - 2 + u)

            dve.wait_ge(d.pe.sem, d.pe.after("mods"))
            d.step(dve, dve.scalar_tensor_tensor(
                mod_sb[:, :, :], d.ps("mods")[:, 0:len(MODS) * B].rearrange("p (m b) -> p m b", b=B), 0.5,
                vec_sb[:, 0:len(MODS)].unsqueeze(2).broadcast_to([D, len(MODS), B]), ALU.mult, ALU.add), "mods")
            d.step(dve, dve.tensor_scalar(mod_sb[:, 0:SCALES, :], mod_sb[:, 0:SCALES, :], 1.0, None, ALU.add), "scales")
            dve.wait_ge(loaded_x, 16)
            d.ln_dve(dve, "ln", 1e-5, lambda: last_statistics(0))
            d.modulate(dve, "L0.scale_q", "L0.shift_q", "m")
            last_statistics(1)
            dve.wait_ge(stats_kept, B + 1)
            d.step(dve, dve.tensor_scalar(norm_all[:, :, 1, :], ctx_mv[:, :, :, 0], -1.0, None, ALU.mult), "c.negmean")
            dve.wait_ge(d.act.sem, d.act.after("c.sd2"))
            d.step(dve, dve.reciprocal(norm_all[:, :, 0, :], norm_all[:, :, 0, :]), "c.rs")
            d.step(dve, dve.reciprocal(norm_all[:, :, 2, :], norm_all[:, :, 2, :]), "c.rs2")
            dve.wait_ge(d.pe.sem, d.pe.after("q"))
            d.step(dve, dve.tensor_scalar(q_t, d.ps("q"), vec("L0_bq"), HD ** -0.5, ALU.add, ALU.mult), "q")
            d.split(dve, q_t, [qsplit_sb[:, i, :] for i in range(3)], "q")
            dve.wait_ge(buffers_ready, BUFFERS)
            a0.later("dve", dve)
            d = d1
            dve.wait_ge(d.pe.sem, d.pe.after("proj"))
            d.step(dve, dve.scalar_tensor_tensor(x_t, d.ps("proj"), vec("L0_bp"), x_t, ALU.add, ALU.add), "x")
            d.ln_dve(dve, "ln", 1e-5)
            d.step(dve, dve.tensor_scalar(xh_t, xh_t, vec("L1_ln_gamma"), vec("L1_ln_beta"), ALU.mult, ALU.add), "nx")
            dve.wait_ge(d.pe.sem, d.pe.after("q"))
            d.step(dve, dve.tensor_copy(k_t, d.ps("q")), "q")
            dve.wait_ge(d.pe.sem, d.pe.after("qk"))
            d.step(dve, dve.tensor_scalar(q_t, d.ps("qk"), D ** -0.5, None, ALU.mult), "qk")
            dve.wait_ge(d.pe.sem, d.pe.after("anchors"))
            for k, (_, _, bias, j) in enumerate(ANCHORED):
                last = dve.tensor_scalar(anchors[:, k, :], d.ps("anchors")[:, k * B:(k + 1) * B], vec(bias, j), None,
                                         ALU.add)
            d.step(dve, last, "anchors")
            evi.vector(dve)
            d = d2
            dve.wait_ge(d.pe.sem, d.pe.after("ev"))
            d.step(dve, dve.tensor_copy(ev_t, d.ps("ev")), "ev")
            for e in range(E_N):
                dve.wait_ge(d.pe.sem, d.pe.after(f"l{e}"))
                d.step(dve, dve.tensor_tensor(by_batch(logit[e]), by_batch(d.ps(f"l{e}")), anchor(e), ALU.add), f"l{e}")
            d.step(dve, dve.tensor_tensor(xc_t, logit[0], logit[1], ALU.max), "m01")
            d.step(dve, dve.tensor_tensor(xc_t, xc_t, logit[2], ALU.max), "m")
            for e in range(E_N):
                d.step(dve, dve.tensor_tensor(logit[e], logit[e], xc_t, ALU.subtract), f"d{e}")
            dve.wait_ge(d.pe.sem, d.pe.after("g1"))
            d.step(dve, dve.tensor_tensor(by_batch(T(8)), by_batch(d.ps("g1")), anchor(E_N), ALU.add), "gu")
            dve.wait_ge(d.act.sem, d.act.after("gt"))
            d.step(dve, dve.scalar_tensor_tensor(T(8), T(12), 1.0, T(8), ALU.add, ALU.mult), "gh")
            dve.wait_ge(d.act.sem, d.act.after("p2"))
            d.step(dve, dve.tensor_tensor(xc_t, logit[0], logit[1], ALU.add), "s01")
            d.step(dve, dve.tensor_tensor(xc_t, xc_t, logit[2], ALU.add), "s")
            d.step(dve, dve.reciprocal(xc_t, xc_t), "r")
            for e in range(E_N):
                d.step(dve, dve.tensor_tensor(logit[e], logit[e], xc_t, ALU.mult), f"p{e}")
            dve.wait_ge(d.act.sem, d.act.after("gt2"))
            d.step(dve, dve.tensor_scalar(T(12), T(12), 1.0, None, ALU.add), "g")
            for i, (e, r) in enumerate(H):
                dve.wait_ge(d.pe.sem, d.pe.after(f"u{e}{r}"))
                d.step(dve, dve.tensor_tensor(by_batch(hidden[i]), by_batch(d.ps(f"u{e}{r}")), anchor(E_N + 1 + i), ALU.add),
                       f"u{e}{r}")
            for i, (e, r) in enumerate(H):
                dve.wait_ge(d.act.sem, d.act.after(f"t{e}{r}"))
                d.step(dve, dve.scalar_tensor_tensor(hidden[i], curve[i], 1.0, hidden[i], ALU.add, ALU.mult), f"h{e}{r}")
            for e in range(E_N):
                dve.wait_ge(d.pe.sem, d.pe.after(f"o{e}"))
                d.step(dve, dve.tensor_scalar(T(8), d.ps(f"o{e}"), 0.5, vec("L1_e_b2", e), ALU.mult, ALU.add), f"o{e}")
                d.step(dve, dve.tensor_tensor(T(14) if e == 0 else T(8), T(8), logit[e], ALU.mult), f"r{e}")
                if e:
                    d.step(dve, dve.tensor_tensor(T(14), T(14), T(8), ALU.add), f"a{e}")
            dve.wait_ge(d.pe.sem, d.pe.after("out"))
            d.step(dve, dve.scalar_tensor_tensor(T(13), d.ps("out"), vec("L1_out_b"), T(12), ALU.add, ALU.mult), "outg")
            d.step(dve, dve.scalar_tensor_tensor(x_t, T(13), 0.5, x_t, ALU.mult, ALU.add), "x")
            own_dve(d, dve, "L2")
            own2.vector(dve)
            for l in ("L2", "L3"):
                d, nm = d_mid[l], NAMES[l]
                dve.wait_ge(d.pe.sem, d.pe.after("proj"))
                d.step(dve, dve.tensor_scalar(T(8), d.ps("proj"), vec(nm["proj_b"]), None, ALU.add), "y")
                d.gated(dve, T(8), f"{l}.gate_a", "y")
                d.ln_dve(dve, "ln", 1e-6)
                dve.wait_ge(d.pe.sem, d.pe.after("q"))
                d.step(dve, dve.tensor_scalar(q_t, d.ps("q"), vec(nm["q_b"]), HD ** -0.5, ALU.add, ALU.mult), "q")
                d.split(dve, q_t, [qsplit_sb[:, i, :] for i in range(3)], "q")
                att_ctx[l].later("dve", dve)
                d = d_end[l]
                dve.wait_ge(d.pe.sem, d.pe.after("proj"))
                d.step(dve, dve.scalar_tensor_tensor(x_t, d.ps("proj"), vec(nm["cproj_b"]), x_t, ALU.add, ALU.add), "x")
                d.ln_dve(dve, "ln", 1e-6)
                d.modulate(dve, f"{l}.scale_m", f"{l}.shift_m", "m")
                for j in J4:
                    dve.wait_ge(d.pe.sem, d.pe.after(f"u{j}"))
                    d.step(dve, dve.tensor_scalar(T(8 + j), d.ps(f"u{j}"), vec(nm["b1"], j), None, ALU.add), f"u{j}")
                for j in J4:
                    dve.wait_ge(d.act.sem, d.act.after(f"sq{j}"))
                    d.step(dve, dve.scalar_tensor_tensor(scratch(j), scratch(j), 1.0, T(8 + j), ALU.add, ALU.mult), f"in{j}")
                for j in J4:
                    dve.wait_ge(d.act.sem, d.act.after(f"t{j}"))
                    d.step(dve, dve.scalar_tensor_tensor(T(8 + j), scratch(j), 1.0, T(8 + j), ALU.add, ALU.mult), f"h{j}")
                dve.wait_ge(d.pe.sem, d.pe.after("y"))
                d.step(dve, dve.tensor_scalar(T(12), d.ps("y"), 0.5, vec(nm["b2"]), ALU.mult, ALU.add), "y")
                d.gated(dve, T(12), f"{l}.gate_m", "y")
                if l == "L2":
                    own_dve(d, dve, "L3")
                    own3.vector(dve)


def kernel(**inputs):
    import concourse.bacc as bacc
    from concourse.bass_utils import run_bass_kernel_spmd

    a = {}
    for name, value in inputs.items():
        a[name.replace("_xcond", "")] = np.asarray(value)
    nat = a["ctx_1024"].reshape(B, CK, NC, D)
    a["L1_WkT"] = a["L1_Wk"].T
    for name, n in HEADED.items():
        cols = [j * D + f for j in range(n) for f in FEATURE_AT] + list(range(n * D, a[name].shape[-1]))
        a[name] = a[name][..., cols]
    blocks = [a[name].reshape(n, D, cols).transpose(1, 0, 2).reshape(D, n * cols) for name, n, cols in WEIGHTS]
    columns = [a[bias][j * D:(j + 1) * D][:, None] for _, _, bias, j in MODS]
    columns += [a[name].reshape(n, D).T for name, n in VECTORS]
    columns.append(np.broadcast_to(a["L1_router_b"][None, :], (D, E_N)))
    identity = np.eye(D, dtype=np.float32)
    arrays = {
        "ctx_nat": nat,
        "ctx_T": nat.transpose(0, 3, 2, 1).reshape(B, D, S),
        "x_T": a["x"].reshape(NT, D).T,
        "cond_T": a["cond_1024"].T,
        "weights": np.concatenate(blocks, axis=1),
        "vectors": np.concatenate(columns, axis=1),
        "identity": identity,
    }
    arrays = {name: np.ascontiguousarray(value) for name, value in arrays.items()}
    nc = bacc.Bacc("TRN2", target_bir_lowering=False, num_devices=1)
    args = [nc.dram_tensor(name, value.shape, F32, kind="ExternalInput").ap() for name, value in arrays.items()]
    out = nc.dram_tensor("out_T", (D, NT), F32, kind="ExternalOutput").ap()
    pixart_program(nc, *args, out)
    r = run_bass_kernel_spmd(nc, [arrays], core_ids=[0])
    return np.ascontiguousarray(r.results[0]["out_T"].T).reshape(B, LQ, D)
```
